# Optimizing a Trainium2 kernel written in Bass

```python
import numpy as np
import jax
import jax.numpy as jnp

def _softmax(x, axis=-1):
    return jax.nn.softmax(x, axis=axis)

def _gelu(x):
    return jax.nn.gelu(x, approximate=True)

def _silu(x):
    return jax.nn.silu(x)

def _sigmoid(x):
    return jax.nn.sigmoid(x)

def _layernorm(x, axis=-1, eps=1e-05):
    m = jnp.mean(x, axis=axis, keepdims=True)
    v = jnp.var(x, axis=axis, keepdims=True)
    return (x - m) / jnp.sqrt(v + eps)

def _scatter_add(tgt, idx, src, axis=0):
    return tgt.at[idx].add(src)

def _segment_sum(src, seg, n):
    return jax.ops.segment_sum(src, seg, n)
kernel_name = 'mk_hybrid_d1_jaxref_r4_a3307e'

def setup_inputs(seed: int=0):
    np.random.seed(seed)
    _w = jnp.asarray

    def _L0_attn_a_setup():
        import jax, jax.numpy as jnp
        import numpy as np
        from jax import lax
        D = 256
        DI = 2 * D
        NS = 16
        DTR = D // 16
        KC = 4
        E = 8
        DFF = 2 * D
        TOPK = 2

        def _ln(x, g, b):
            mu = x.mean(-1, keepdims=True)
            var = ((x - mu) ** 2).mean(-1, keepdims=True)
            return (x - mu) * lax.rsqrt(var + 1e-05) * g + b

        def _silu(x):
            return x * jax.nn.sigmoid(x)

        def _mamba(x, in_proj_w, in_proj_b, conv_w, conv_b, x_proj_w, dt_proj_w, dt_proj_b, A_log, D_skip, out_proj_w):
            Bz, T, _ = x.shape
            xz = x @ in_proj_w.T + in_proj_b
            xi, z = (xz[..., :DI], xz[..., DI:])
            xp = jnp.pad(xi, ((0, 0), (KC - 1, 0), (0, 0)))
            xc = conv_b + sum((conv_w[:, k] * xp[:, k:k + T, :] for k in range(KC)))
            xc = _silu(xc)
            proj = xc @ x_proj_w.T
            dt_r = proj[..., :DTR]
            Bm = proj[..., DTR:DTR + NS]
            Cm = proj[..., DTR + NS:]
            dt = jax.nn.softplus(dt_r @ dt_proj_w.T + dt_proj_b)
            A = -jnp.exp(A_log)

            def step(h, inp):
                xt, dtt, Bt, Ct = inp
                dA = jnp.exp(dtt[:, :, None] * A)
                h = dA * h + (dtt * xt)[:, :, None] * Bt[:, None, :]
                y = jnp.einsum('bdn,bn->bd', h, Ct)
                return (h, y)
            h0 = jnp.zeros((Bz, DI, NS), x.dtype)
            xs = (xc.transpose(1, 0, 2), dt.transpose(1, 0, 2), Bm.transpose(1, 0, 2), Cm.transpose(1, 0, 2))
            _, ys = lax.scan(step, h0, xs)
            y = ys.transpose(1, 0, 2) + xc * D_skip
            y = y * _silu(z)
            return y @ out_proj_w.T

        def _moe(x, router_w, w1, b1, w2, b2):
            logits = x @ router_w.T
            probs = jax.nn.softmax(logits, axis=-1)
            topv, topi = lax.top_k(probs, TOPK)
            topv = topv / topv.sum(-1, keepdims=True)
            w = (jax.nn.one_hot(topi, E, dtype=x.dtype) * topv[..., None]).sum(-2)
            out = jnp.zeros_like(x)
            for e in range(E):
                h1 = _silu(x @ w1[e].T + b1[e])
                ye = h1 @ w2[e].T + b2[e]
                out = out + w[..., e:e + 1] * ye
            return (out, {'router_probs': probs})

        def _reference_tuple_inner(x, ln_mamba_g, ln_mamba_b, ln_moe_g, ln_moe_b, in_proj_w, in_proj_b, conv_w, conv_b, x_proj_w, dt_proj_w, dt_proj_b, A_log, D_skip, out_proj_w, router_w, w1, b1, w2, b2):
            h_norm = _ln(x, ln_mamba_g, ln_mamba_b)
            mamba_out = _mamba(h_norm, in_proj_w, in_proj_b, conv_w, conv_b, x_proj_w, dt_proj_w, dt_proj_b, A_log, D_skip, out_proj_w)
            h = x + mamba_out
            h_moe_in = _ln(h, ln_moe_g, ln_moe_b)
            moe_delta, aux = _moe(h_moe_in, router_w, w1, b1, w2, b2)
            h = h + moe_delta
            return (h, aux['router_probs'])
        key = jax.random.key(seed)
        ks = jax.random.split(key, 20)
        s = 0.02
        inp = {'x': jax.random.normal(ks[0], (2, 512, D), jnp.float32), 'ln_mamba_g': jnp.ones((D,), jnp.float32), 'ln_mamba_b': jnp.zeros((D,), jnp.float32), 'ln_moe_g': jnp.ones((D,), jnp.float32), 'ln_moe_b': jnp.zeros((D,), jnp.float32), 'in_proj_w': jax.random.normal(ks[1], (2 * DI, D), jnp.float32) * s, 'in_proj_b': jnp.zeros((2 * DI,), jnp.float32), 'conv_w': jax.random.normal(ks[2], (DI, KC), jnp.float32) * s, 'conv_b': jnp.zeros((DI,), jnp.float32), 'x_proj_w': jax.random.normal(ks[3], (DTR + 2 * NS, DI), jnp.float32) * s, 'dt_proj_w': jax.random.normal(ks[4], (DI, DTR), jnp.float32) * s, 'dt_proj_b': jnp.full((DI,), -4.6, jnp.float32), 'A_log': jnp.log(jnp.broadcast_to(jnp.arange(1, NS + 1, dtype=jnp.float32), (DI, NS))), 'D_skip': jnp.ones((DI,), jnp.float32), 'out_proj_w': jax.random.normal(ks[5], (D, DI), jnp.float32) * s, 'router_w': jax.random.normal(ks[6], (E, D), jnp.float32) * s, 'w1': jax.random.normal(ks[7], (E, DFF, D), jnp.float32) * s, 'b1': jnp.zeros((E, DFF), jnp.float32), 'w2': jax.random.normal(ks[8], (E, D, DFF), jnp.float32) * s, 'b2': jnp.zeros((E, D), jnp.float32)}
        return inp
    _L0_attn_a_in = _L0_attn_a_setup()

    def _L0_attn_b_setup():
        import jax, jax.numpy as jnp
        import numpy as np
        ALPHA = 1.2
        A = 1.0
        BANDWIDTH = 1.0
        D_INTRINSIC = 2
        SPHERE_RADIUS = 1.0
        NUM_HEADS = 16
        HIDDEN = 256
        HEAD_DIM = HIDDEN // NUM_HEADS
        EPS = 1e-07

        def _l2norm(t):
            n = jnp.sqrt(jnp.sum(t * t, axis=-1, keepdims=True))
            return t / jnp.maximum(n, 1e-12)
        key = jax.random.key(seed)
        k1, k2, k3, k4, k5 = jax.random.split(key, 5)
        B, S = (2, 512)
        scale = 0.02
        return {'x': jax.random.normal(k1, (B, S, HIDDEN), dtype=jnp.float32), 'w_qkv': jax.random.normal(k2, (3 * HIDDEN, HIDDEN), dtype=jnp.float32) * scale, 'b_qkv': jnp.zeros((3 * HIDDEN,), dtype=jnp.float32), 'w_out': jax.random.normal(k3, (HIDDEN, HIDDEN), dtype=jnp.float32) * scale, 'b_out': jnp.zeros((HIDDEN,), dtype=jnp.float32)}
    _L0_attn_b_in = _L0_attn_b_setup()

    def _L0_ffn_setup():
        import jax, jax.numpy as jnp
        import numpy as np
        DIM = 256
        HIDDEN = 768
        SCALE = 1.0 / 127.0

        def _dequant(w_int, dtype):
            return w_int.astype(dtype) * jnp.asarray(SCALE, dtype)
        key = jax.random.key(seed)
        k_x, k_g, k_u, k_d = jax.random.split(key, 4)
        x = jax.random.normal(k_x, (4, 512, DIM), dtype=jnp.float32)
        w_gate = jax.random.randint(k_g, (HIDDEN, DIM), -127, 128, dtype=jnp.int32)
        w_up = jax.random.randint(k_u, (HIDDEN, DIM), -127, 128, dtype=jnp.int32)
        w_down = jax.random.randint(k_d, (DIM, HIDDEN), -127, 128, dtype=jnp.int32)
        return {'x': x, 'w_gate': w_gate, 'w_up': w_up, 'w_down': w_down}
    _L0_ffn_in = _L0_ffn_setup()
    _d = {'L0_attn_a_x': _L0_attn_a_in['x'], 'L0_attn_a_ln_mamba_g': _L0_attn_a_in['ln_mamba_g'], 'L0_attn_a_ln_mamba_b': _L0_attn_a_in['ln_mamba_b'], 'L0_attn_a_ln_moe_g': _L0_attn_a_in['ln_moe_g'], 'L0_attn_a_ln_moe_b': _L0_attn_a_in['ln_moe_b'], 'L0_attn_a_in_proj_w': _L0_attn_a_in['in_proj_w'], 'L0_attn_a_in_proj_b': _L0_attn_a_in['in_proj_b'], 'L0_attn_a_conv_w': _L0_attn_a_in['conv_w'], 'L0_attn_a_conv_b': _L0_attn_a_in['conv_b'], 'L0_attn_a_x_proj_w': _L0_attn_a_in['x_proj_w'], 'L0_attn_a_dt_proj_w': _L0_attn_a_in['dt_proj_w'], 'L0_attn_a_dt_proj_b': _L0_attn_a_in['dt_proj_b'], 'L0_attn_a_A_log': _L0_attn_a_in['A_log'], 'L0_attn_a_D_skip': _L0_attn_a_in['D_skip'], 'L0_attn_a_out_proj_w': _L0_attn_a_in['out_proj_w'], 'L0_attn_a_router_w': _L0_attn_a_in['router_w'], 'L0_attn_a_w1': _L0_attn_a_in['w1'], 'L0_attn_a_b1': _L0_attn_a_in['b1'], 'L0_attn_a_w2': _L0_attn_a_in['w2'], 'L0_attn_a_b2': _L0_attn_a_in['b2'], 'L0_attn_b_w_qkv': _L0_attn_b_in['w_qkv'], 'L0_attn_b_b_qkv': _L0_attn_b_in['b_qkv'], 'L0_attn_b_w_out': _L0_attn_b_in['w_out'], 'L0_attn_b_b_out': _L0_attn_b_in['b_out'], 'L0_ffn_w_gate': _L0_ffn_in['w_gate'], 'L0_ffn_w_up': _L0_ffn_in['w_up'], 'L0_ffn_w_down': _L0_ffn_in['w_down']}
    _x0 = _d['L0_attn_a_x']
    _d['L0_attn_a_x'] = jax.random.normal(jax.random.fold_in(jax.random.key(seed), 1), (16, 512, 256), dtype=_x0.dtype)
    del _x0
    return _d

def reference(L0_attn_a_x, L0_attn_a_ln_mamba_g, L0_attn_a_ln_mamba_b, L0_attn_a_ln_moe_g, L0_attn_a_ln_moe_b, L0_attn_a_in_proj_w, L0_attn_a_in_proj_b, L0_attn_a_conv_w, L0_attn_a_conv_b, L0_attn_a_x_proj_w, L0_attn_a_dt_proj_w, L0_attn_a_dt_proj_b, L0_attn_a_A_log, L0_attn_a_D_skip, L0_attn_a_out_proj_w, L0_attn_a_router_w, L0_attn_a_w1, L0_attn_a_b1, L0_attn_a_w2, L0_attn_a_b2, L0_attn_b_w_qkv, L0_attn_b_b_qkv, L0_attn_b_w_out, L0_attn_b_b_out, L0_ffn_w_gate, L0_ffn_w_up, L0_ffn_w_down):

    def _L0_attn_a_ref(x, ln_mamba_g, ln_mamba_b, ln_moe_g, ln_moe_b, in_proj_w, in_proj_b, conv_w, conv_b, x_proj_w, dt_proj_w, dt_proj_b, A_log, D_skip, out_proj_w, router_w, w1, b1, w2, b2):
        import jax, jax.numpy as jnp
        import numpy as np
        from jax import lax
        D = 256
        DI = 2 * D
        NS = 16
        DTR = D // 16
        KC = 4
        E = 8
        DFF = 2 * D
        TOPK = 2

        def _ln(x, g, b):
            mu = x.mean(-1, keepdims=True)
            var = ((x - mu) ** 2).mean(-1, keepdims=True)
            return (x - mu) * lax.rsqrt(var + 1e-05) * g + b

        def _silu(x):
            return x * jax.nn.sigmoid(x)

        def _mamba(x, in_proj_w, in_proj_b, conv_w, conv_b, x_proj_w, dt_proj_w, dt_proj_b, A_log, D_skip, out_proj_w):
            Bz, T, _ = x.shape
            xz = x @ in_proj_w.T + in_proj_b
            xi, z = (xz[..., :DI], xz[..., DI:])
            xp = jnp.pad(xi, ((0, 0), (KC - 1, 0), (0, 0)))
            xc = conv_b + sum((conv_w[:, k] * xp[:, k:k + T, :] for k in range(KC)))
            xc = _silu(xc)
            proj = xc @ x_proj_w.T
            dt_r = proj[..., :DTR]
            Bm = proj[..., DTR:DTR + NS]
            Cm = proj[..., DTR + NS:]
            dt = jax.nn.softplus(dt_r @ dt_proj_w.T + dt_proj_b)
            A = -jnp.exp(A_log)

            def step(h, inp):
                xt, dtt, Bt, Ct = inp
                dA = jnp.exp(dtt[:, :, None] * A)
                h = dA * h + (dtt * xt)[:, :, None] * Bt[:, None, :]
                y = jnp.einsum('bdn,bn->bd', h, Ct)
                return (h, y)
            h0 = jnp.zeros((Bz, DI, NS), x.dtype)
            xs = (xc.transpose(1, 0, 2), dt.transpose(1, 0, 2), Bm.transpose(1, 0, 2), Cm.transpose(1, 0, 2))
            _, ys = lax.scan(step, h0, xs)
            y = ys.transpose(1, 0, 2) + xc * D_skip
            y = y * _silu(z)
            return y @ out_proj_w.T

        def _moe(x, router_w, w1, b1, w2, b2):
            logits = x @ router_w.T
            probs = jax.nn.softmax(logits, axis=-1)
            topv, topi = lax.top_k(probs, TOPK)
            topv = topv / topv.sum(-1, keepdims=True)
            w = (jax.nn.one_hot(topi, E, dtype=x.dtype) * topv[..., None]).sum(-2)
            out = jnp.zeros_like(x)
            for e in range(E):
                h1 = _silu(x @ w1[e].T + b1[e])
                ye = h1 @ w2[e].T + b2[e]
                out = out + w[..., e:e + 1] * ye
            return (out, {'router_probs': probs})

        def _reference_tuple_inner(x, ln_mamba_g, ln_mamba_b, ln_moe_g, ln_moe_b, in_proj_w, in_proj_b, conv_w, conv_b, x_proj_w, dt_proj_w, dt_proj_b, A_log, D_skip, out_proj_w, router_w, w1, b1, w2, b2):
            h_norm = _ln(x, ln_mamba_g, ln_mamba_b)
            mamba_out = _mamba(h_norm, in_proj_w, in_proj_b, conv_w, conv_b, x_proj_w, dt_proj_w, dt_proj_b, A_log, D_skip, out_proj_w)
            h = x + mamba_out
            h_moe_in = _ln(h, ln_moe_g, ln_moe_b)
            moe_delta, aux = _moe(h_moe_in, router_w, w1, b1, w2, b2)
            h = h + moe_delta
            return (h, aux['router_probs'])
        return _reference_tuple_inner(x, ln_mamba_g, ln_mamba_b, ln_moe_g, ln_moe_b, in_proj_w, in_proj_b, conv_w, conv_b, x_proj_w, dt_proj_w, dt_proj_b, A_log, D_skip, out_proj_w, router_w, w1, b1, w2, b2)[0]

    def _L0_attn_b_ref(x, w_qkv, b_qkv, w_out, b_out):
        import jax, jax.numpy as jnp
        import numpy as np
        ALPHA = 1.2
        A = 1.0
        BANDWIDTH = 1.0
        D_INTRINSIC = 2
        SPHERE_RADIUS = 1.0
        NUM_HEADS = 16
        HIDDEN = 256
        HEAD_DIM = HIDDEN // NUM_HEADS
        EPS = 1e-07

        def _l2norm(t):
            n = jnp.sqrt(jnp.sum(t * t, axis=-1, keepdims=True))
            return t / jnp.maximum(n, 1e-12)
        B, S, H = x.shape
        qkv = x @ w_qkv.T + b_qkv
        q, k, v = jnp.split(qkv, 3, axis=-1)
        to_heads = lambda t: t.reshape(B, S, NUM_HEADS, HEAD_DIM).transpose(0, 2, 1, 3)
        q = _l2norm(to_heads(q))
        k = _l2norm(to_heads(k))
        v = to_heads(v)
        cos = jnp.einsum('bhsd,bhtd->bhst', q, k)
        g_dist = jnp.arccos(jnp.clip(cos, -1.0 + EPS, 1.0 - EPS)) * SPHERE_RADIUS
        attn_score = (1.0 + g_dist / BANDWIDTH ** 0.5) ** (-D_INTRINSIC - ALPHA)
        n_r = jnp.sum(attn_score, axis=-1)
        n_c = jnp.sum(attn_score, axis=-2)
        k_tilde = (n_r ** (-A))[..., :, None] * attn_score * (n_c ** (-A))[..., None, :]
        probs = k_tilde / jnp.maximum(jnp.sum(k_tilde, axis=-1, keepdims=True), 1e-12)
        out = jnp.einsum('bhst,bhtd->bhsd', probs, v)
        out = out.transpose(0, 2, 1, 3).reshape(B, S, H)
        return out @ w_out.T + b_out

    def _L0_ffn_ref(x, w_gate, w_up, w_down):
        import jax, jax.numpy as jnp
        import numpy as np
        DIM = 256
        HIDDEN = 768
        SCALE = 1.0 / 127.0

        def _dequant(w_int, dtype):
            return w_int.astype(dtype) * jnp.asarray(SCALE, dtype)
        wg = _dequant(w_gate, x.dtype)
        wu = _dequant(w_up, x.dtype)
        wd = _dequant(w_down, x.dtype)
        gate = jnp.einsum('bsd,hd->bsh', x, wg)
        up = jnp.einsum('bsd,hd->bsh', x, wu)
        h = jax.nn.silu(gate) * up
        return jnp.einsum('bsh,dh->bsd', h, wd)
    x = L0_attn_a_x
    x = x + _L0_attn_a_ref(_layernorm(x, axis=-1), L0_attn_a_ln_mamba_g, L0_attn_a_ln_mamba_b, L0_attn_a_ln_moe_g, L0_attn_a_ln_moe_b, L0_attn_a_in_proj_w, L0_attn_a_in_proj_b, L0_attn_a_conv_w, L0_attn_a_conv_b, L0_attn_a_x_proj_w, L0_attn_a_dt_proj_w, L0_attn_a_dt_proj_b, L0_attn_a_A_log, L0_attn_a_D_skip, L0_attn_a_out_proj_w, L0_attn_a_router_w, L0_attn_a_w1, L0_attn_a_b1, L0_attn_a_w2, L0_attn_a_b2)
    x = x + _L0_ffn_ref(_layernorm(x, axis=-1), L0_ffn_w_gate, L0_ffn_w_up, L0_ffn_w_down)
    x = x + _L0_attn_b_ref(_layernorm(x, axis=-1), L0_attn_b_w_qkv, L0_attn_b_b_qkv, L0_attn_b_w_out, L0_attn_b_b_out)
    x = x + _L0_ffn_ref(_layernorm(x, axis=-1), L0_ffn_w_gate, L0_ffn_w_up, L0_ffn_w_down)
    return x

_drawn_inputs = setup_inputs


def setup_inputs(seed=0):
    import zlib

    import numpy as np

    out = dict(_drawn_inputs(seed))
    spreads = {'L0_attn_a_ln_mamba_g': (1.0, 0.6),
     'L0_attn_a_ln_mamba_b': (0.0, 0.8),
     'L0_attn_a_ln_moe_g': (1.0, 0.6),
     'L0_attn_a_ln_moe_b': (0.0, 2.0),
     'L0_attn_a_in_proj_b': (0.0, 0.8),
     'L0_attn_a_conv_b': (0.0, 0.8),
     'L0_attn_a_dt_proj_b': (-4.599999904632568, 0.6),
     'L0_attn_a_D_skip': (1.0, 0.6),
     'L0_attn_a_b1': (0.0, 2.0),
     'L0_attn_a_b2': (0.0, 2.0),
     'L0_attn_b_b_qkv': (0.0, 2.0),
     'L0_attn_b_b_out': (0.0, 2.0)}
    factors = {'L0_attn_a_in_proj_w': 8.0,
     'L0_attn_a_conv_w': 8.0,
     'L0_attn_a_x_proj_w': 8.0,
     'L0_attn_a_dt_proj_w': 8.0,
     'L0_attn_a_A_log': 8.0,
     'L0_attn_a_out_proj_w': 8.0,
     'L0_attn_b_w_qkv': 64.0,
     'L0_attn_b_w_out': 64.0,
     'L0_attn_a_router_w': 8.0,
     'L0_attn_a_w1': 8.0,
     'L0_attn_a_w2': 8.0}
    for name, (base, spread) in spreads.items():
        noise = np.random.default_rng([zlib.crc32(name.encode()), seed]).standard_normal(out[name].shape)
        drawn = base * np.exp(spread * noise) if base else spread * noise
        out[name] = jnp.asarray(drawn.astype(out[name].dtype))
    for name, factor in factors.items():
        out[name] = (out[name] * factor).astype(out[name].dtype)
    return out
```

```python
import math
from contextlib import ExitStack

import concourse.bass as bass
from concourse import mybir

F32 = mybir.dt.float32
BF16 = mybir.dt.bfloat16
I32 = mybir.dt.int32
ACT = mybir.ActivationFunctionType
ALU = mybir.AluOpType
AX = mybir.AxisListType

P = 128
D = 256
T = 512
J = T // P
KD = D // P
DI = 2 * D
C = DI // P
NS = 16
DTR = D // 16
KC = 4
E = 8
DFF = 2 * D
FE = DFF // P
HID = 768
FH = HID // P
H = 16
DH = D // H
HG = 4
NG = H // HG
VW = P // HG
LN_EPS = 1e-5
Q_SHIFT = 2.0 ** 30

VEC = {}
_at = 0
for _name, _n in (("ln_mamba_g", KD), ("ln_mamba_b", KD), ("ln_moe_g", KD), ("ln_moe_b", KD),
                  ("in_proj_b", 2 * C), ("conv_w", C * KC), ("conv_b", C), ("dt_proj_b", C),
                  ("A_log", C * NS), ("D_skip", C), ("b1", E * FE), ("head_mask", P // DH),
                  ("before", E * E)):
    VEC[_name] = (_at, _at + _n)
    _at += _n
VEC_N = _at


class Chain:

    def __init__(self, eng, sem):
        self.eng, self.sem, self.n = eng, sem, 0

    def inc(self, ins):
        ins.then_inc(self.sem, 1)
        self.n += 1

    def sync(self):
        self.eng.wait_ge(self.sem, self.n)

    def step(self, ins):
        self.inc(ins)
        self.sync()


def layer_stats(ch, dve, x, stats, mv, var_ready):
    for j in range(J):
        ch.inc(dve.bn_stats(stats[:, j, :], x[:, j, :]))
    ch.sync()
    for j in range(J):
        last = dve.bn_aggr(mv[:, j, :], stats[:, j, :])
    last.then_inc(var_ready, 1)


def layer_rstd(ch, act, mv, rstd, eps, rstd_ready):
    ch.step(act.activation(rstd, mv[:, :, 1], ACT.Ln, bias=eps))
    act.activation(rstd, rstd, ACT.Exp, scale=-0.5).then_inc(rstd_ready, 1)


def layer_apply(dve, out, x, mv, rstd):
    for j in range(J):
        last = dve.tensor_scalar(out[:, j, :], x[:, j, :], mv[:, j, 0:1], rstd[:, j:j + 1],
                                 ALU.subtract, ALU.mult)
    return last


def transpose_tokens(pe, out, x, ident):
    for k in range(KD):
        for j in range(J):
            last = pe.transpose(out[:, k, j * P:(j + 1) * P], x[:, j, k * P:(k + 1) * P], ident)
    return last


def run(order, **parts):
    for name, *args in order:
        if name in parts:
            parts[name](*args)


def beside(a, b):
    n = [(i / max(len(a), 1), 0, s) for i, s in enumerate(a)] + [(i / max(len(b), 1), 1, s) for i, s in enumerate(b)]
    return [s for _, _, s in sorted(n, key=lambda x: x[:2])]


def mamba_moe_pass(nc, io, x1_dram):
    NB = io["x"].shape[0]
    x_dram = io["x"].rearrange("b (j p) d -> b p j d", p=P)
    with ExitStack() as ctx:
        first_sem = []

        def sb(name, shape, dt=F32):
            return ctx.enter_context(nc.sbuf_tensor(name, [P] + shape, dt))

        def sem(name):
            s = ctx.enter_context(nc.semaphore(name))
            first_sem.append(s.num)
            return s

        vec = sb("m_vec", [VEC_N])
        ident = sb("m_ident", [P])
        pick = sb("m_pick", [2 * NS], BF16)
        w_in = sb("w_in", [KD, 2 * DI])
        w_bc = sb("w_bc", [C, 6 * NS])
        w_dtr = sb("w_dtr", [C, DTR])
        w_dt = sb("w_dt", [DI])
        w_op = sb("w_op", [C, D])
        w_rt = sb("w_rt", [KD, E])
        w_1 = sb("w_1", [E, KD, DFF])
        w_2 = sb("w_2", [E, FE, D])
        b_2 = sb("b_2", [D])
        neg_a = sb("neg_a", [C, NS])
        eps = sb("m_eps", [1])
        xa = sb("xa", [J, D])
        ua = sb("ua", [J, D])
        a_stats = sb("a_stats", [J, 6])
        a_mv = sb("a_mv", [J, 2])
        a_rstd = sb("a_rstd", [J])
        gate = sb("gate", [C, T])
        both = sb("delta_dx", [2, C, T])
        delta, dx = both[:, 0], both[:, 1]
        y = sb("y", [C, T])
        decay = sb("decay", [2, C, T])
        state = sb("state", [2, C, T])
        bc3 = sb("bc3", [T], BF16)
        bc_rest = sb("bc_rest", [T])
        dtr = sb("dtr", [T])
        xpad = both[:].rearrange("p a c t -> p (a c t)")[:, 0:C * (T + KC - 1)].rearrange("p (c t) -> p c t", c=C)
        va, ha = decay[:, 1, 0:2, :].rearrange("p c (j d) -> p (c j) d", d=D), decay[:, 1, 2:4, :]
        soft, soft1 = state[:, 0], decay[:, 1]
        xc = state[:, 1]
        h_in = sb("h_in", [J, D])
        xh_in = sb("xh_in", [J, D])
        acc = sb("acc", [J, D])
        b_stats = sb("b_stats", [J, 6])
        b_mv = sb("b_mv", [J, 2])
        b_rstd = sb("b_rstd", [J])
        mt = sb("mt", [KD, T])
        h1 = sb("h1", [2, FE, T])
        vb = h1[:, 0, 0:2, :].rearrange("p c (j d) -> p (c j) d", d=D)
        r_p = sb("r_p", [J, E])
        r_m = sb("r_m", [J])
        r_gt = sb("r_gt", [J, E, E])
        r_eq = sb("r_eq", [J, E, E])
        r_w = sb("r_w", [J, E])
        r_wt = sb("r_wt", [T])

        pa = ctx.enter_context(nc.psum_tensor("pa", [P, 2, T], F32))
        pb = ctx.enter_context(nc.psum_tensor("pb", [P, 6, T], F32))

        def v(name, i=0, n=None):
            a, b = VEC[name]
            return vec[:, a + i:a + i + (n or 1)]

        loaded = sem("m_loaded")
        setup = sem("m_setup")
        x_loaded = sem("x_loaded")
        a_dve = sem("a_dve"); a_act = sem("a_act")
        a_var = sem("a_var"); a_rs = sem("a_rs"); va_ready = sem("va_ready")
        va_turned = sem("va_turned"); ha_ready = sem("ha_ready")
        in_ready = sem("in_ready"); in_taken = sem("in_taken")
        conv_ready = sem("conv_ready"); xc_ready = sem("xc_ready")
        bc_mm = sem("bc_mm"); dtr_mm = sem("dtr_mm"); bc_ready = sem("bc_ready"); dtr_ready = sem("dtr_ready")
        dt_mm = sem("dt_mm"); dt_taken = sem("dt_taken")
        sp_neg = sem("sp_neg"); sp_exp = sem("sp_exp"); sp_one = sem("sp_one"); sp_log = sem("sp_log")
        sp_fix = sem("sp_fix"); sp_inv = sem("sp_inv")
        delta_ready = sem("delta_ready")
        b_row = sem("b_row"); c_row = sem("c_row"); decay_ready = sem("decay_ready")
        u_done = sem("u_done"); scan_done = sem("scan_done"); hc_done = sem("hc_done"); y_added = sem("y_added")
        y_start = sem("y_start")
        y_gated = sem("y_gated"); op_mm = sem("op_mm"); handed = sem("handed")
        b_dve = sem("b_dve"); b_act = sem("b_act")
        b_var = sem("b_var"); b_rs = sem("b_rs"); vb_ready = sem("vb_ready")
        vb_turned = sem("vb_turned"); mt_ready = sem("mt_ready")
        logit_mm = sem("logit_mm"); r_neg = sem("r_neg"); r_exp = sem("r_exp"); rw_ready = sem("rw_ready")
        rwt_mm = sem("rwt_mm"); rwt_ready = sem("rwt_ready"); seed_mm = sem("seed_mm"); acc_ready = sem("acc_ready")
        up_mm = sem("up_mm"); h1_ready = sem("h1_ready"); down_mm = sem("down_mm"); ye_taken = sem("ye_taken")
        moe_done = sem("moe_done"); x1_stored = sem("x1_stored")
        sems = range(min(first_sem), max(first_sem) + 1)
        assert len(sems) == len(first_sem)

        def clear_all():
            nc.sync.sem_clear(sems)
            nc.all_engine_barrier()

        with nc.Block() as block:
            loads = [(vec, "vectors"), (ident, "ident"), (w_in, "w_in"), (w_bc, "w_bc"), (w_dtr, "w_dtr"),
                     (w_op, "w_op"), (w_rt, "w_rt"), (w_1, "w_1"), (w_2, "w_2")]

            @block.sync
            def _(sp):
                for dst, name in loads:
                    sp.dma_start(dst[:], io[name]).then_inc(loaded, 16)
                sp.dma_start(w_dt[0:DTR, :], io["w_dt"]).then_inc(loaded, 16)
                sp.dma_start(b_2[0:E, :], io["b2"]).then_inc(loaded, 16)
                sp.dma_start(pick[0:6 * NS, :], io["pick"]).then_inc(loaded, 16)

            @block.scalar
            def _(act):
                act.wait_ge(loaded, 16 * (len(loads) + 3))
                act.activation(neg_a[:].rearrange("p c n -> p (c n)"), v("A_log", 0, C * NS), ACT.Exp).then_inc(setup, 1)

            @block.vector
            def _(dve):
                ch = Chain(dve, a_dve)
                ch.inc(dve.memset(eps[:], LN_EPS))
                ch.inc(dve.memset(decay[:], 0.0))
                dve.wait_ge(setup, 1)
                ch.step(dve.tensor_scalar(neg_a[:], neg_a[:], -1.0, None, ALU.mult))
        clear_all()

        def body(i, mamba, moe):
            mamba_steps = [("mamba_ln",), ("mamba_conv",), ("mamba_dt",)] + [("mamba_scan", n) for n in range(NS)] + [("mamba_out",)]
            moe_steps = [("moe_ln",), ("moe_route",)] + [("moe_expert", e) for e in range(E)]
            order = beside(mamba_steps if mamba else [], moe_steps if moe else [])
            with nc.Block() as block:
                @block.sync
                def _(sp):
                    if mamba:
                        sp.dma_start(xa[:], x_dram[bass.ds(i, 1)].rearrange("o p j d -> (o p) j d")).then_inc(x_loaded, 16)
                    if moe:
                        sp.wait_ge(moe_done, 1)
                        sp.dma_start(x1_dram[bass.ds(i - 1, 1)].rearrange("o p j d -> (o p) j d"), acc[:]).then_inc(x1_stored, 16)
                        sp.wait_ge(x1_stored, 16)

                @block.vector
                def _(dve):
                    cha, chb = Chain(dve, a_dve), Chain(dve, b_dve)

                    def mamba_ln():
                        cha.inc(dve.memset(xpad[:, :, 0:KC - 1], 0.0))
                        dve.wait_ge(x_loaded, 16)
                        layer_stats(cha, dve, xa, a_stats, a_mv, a_var)
                        dve.wait_ge(a_rs, 1)
                        cha.step(layer_apply(dve, ua, xa, a_mv, a_rstd))
                        layer_stats(cha, dve, ua, a_stats, a_mv, a_var)
                        dve.wait_ge(a_rs, 2)
                        layer_apply(dve, va, ua, a_mv, a_rstd).then_inc(va_ready, 1)
                        dve.wait_ge(va_turned, 1)
                        for k in range(KD):
                            last = dve.tensor_scalar(ha[:, k], pa[:, k], v("ln_mamba_g", k), v("ln_mamba_b", k),
                                                     ALU.mult, ALU.add)
                        last.then_inc(ha_ready, 1)

                    def mamba_conv():
                        for c in range(C):
                            dve.wait_ge(in_taken, c + 1)
                            cha.step(dve.tensor_scalar(y[:, c], xpad[:, c, 0:T], v("conv_w", c * KC), v("conv_b", c),
                                                       ALU.mult, ALU.add))
                            for t in range(1, KC):
                                last = dve.scalar_tensor_tensor(out=y[:, c], in0=xpad[:, c, t:t + T],
                                                                scalar=v("conv_w", c * KC + t), in1=y[:, c],
                                                                op0=ALU.mult, op1=ALU.add)
                                if t < KC - 1:
                                    cha.step(last)
                            last.then_inc(conv_ready, 1)

                    def mamba_dt():
                        n = 2 * NS
                        dve.wait_ge(bc_mm, 1)
                        cha.step(dve.tensor_copy(bc3[0:3 * n, :], pa[0:3 * n, 0]))
                        for part in range(1, 3):
                            cha.step(dve.tensor_tensor(bc_rest[n * part:n * part + n, :], pa[n * part:n * part + n, 0],
                                                       bc3[n * part:n * part + n, :], ALU.subtract))
                            last = dve.tensor_copy(bc3[n * part:n * part + n, :], bc_rest[n * part:n * part + n, :])
                            if part == 1:
                                cha.step(last)
                        cha.step(last)
                        last = dve.tensor_tensor(bc_rest[2 * n:3 * n, :], bc_rest[2 * n:3 * n, :], bc3[2 * n:3 * n, :],
                                                 ALU.subtract)
                        cha.step(last)
                        dve.tensor_copy(bc3[2 * n:3 * n, :], bc_rest[2 * n:3 * n, :]).then_inc(bc_ready, 1)
                        z = delta
                        for c in range(C):
                            dve.wait_ge(dt_mm, c + 1)
                            dve.tensor_scalar(z[:, c], pa[:, c % 2], v("dt_proj_b", c), None, ALU.add).then_inc(dt_taken, 1)
                        dve.wait_ge(dt_taken, C)
                        dve.scalar_tensor_tensor(out=soft, in0=z, scalar=-1.0, in1=z, op0=ALU.mult,
                                                 op1=ALU.min).then_inc(sp_neg, 1)
                        dve.wait_ge(sp_exp, 1)
                        dve.tensor_scalar(soft1, soft, 1.0, None, ALU.add).then_inc(sp_one, 1)
                        dve.wait_ge(sp_one, 1)
                        dve.scalar_tensor_tensor(out=soft, in0=soft1, scalar=-1.0, in1=soft, op0=ALU.add,
                                                 op1=ALU.subtract).then_inc(sp_fix, 1)
                        dve.wait_ge(sp_fix, 1)
                        dve.wait_ge(sp_inv, 1)
                        cha.step(dve.tensor_tensor(soft, soft, soft1, ALU.mult))
                        cha.step(dve.tensor_tensor(soft, dx, soft, ALU.subtract))
                        cha.step(dve.scalar_tensor_tensor(out=delta, in0=z, scalar=0.0, in1=soft, op0=ALU.max, op1=ALU.add))
                        cha.inc(dve.memset(decay[:, 1, :, 0:1], 0.0))
                        dve.tensor_tensor(dx, delta, xc, ALU.mult).then_inc(delta_ready, 1)
                        for c in range(C):
                            last = dve.tensor_scalar(y[:, c], xc[:, c], v("D_skip", c), None, ALU.mult)
                        last.then_inc(y_start, 1)

                    def mamba_scan(n):
                        s = state[:, n % 2]
                        dve.wait_ge(b_row, n + 1)
                        dve.wait_ge(y_start, 1)
                        if n >= 2:
                            dve.wait_ge(y_added, n - 1)
                        dve.tensor_tensor(s, dx, pa[:, 0:1, :].to_broadcast([P, C, T]), ALU.mult).then_inc(u_done, 1)
                        dve.wait_ge(u_done, n + 1)
                        dve.wait_ge(decay_ready, n + 1)
                        flat = s.rearrange("p c t -> p (c t)")
                        dve.tensor_tensor_scan(out=flat, data0=decay[:, n % 2].rearrange("p c t -> p (c t)"), data1=flat,
                                               initial=0.0, op0=ALU.mult, op1=ALU.add).then_inc(scan_done, 1)
                        dve.wait_ge(scan_done, n + 1)
                        dve.wait_ge(c_row, n + 1)
                        dve.tensor_tensor(s, s, pa[:, 1:2, :].to_broadcast([P, C, T]), ALU.mult).then_inc(hc_done, 1)

                    def mamba_out():
                        dve.wait_ge(y_added, NS)
                        dve.tensor_tensor(y[:], y[:], gate[:], ALU.mult).then_inc(y_gated, 1)
                        dve.wait_ge(op_mm, 1)
                        if moe:
                            dve.wait_ge(acc_ready, 1)
                        cha.step(dve.tensor_tensor(h_in[:].rearrange("p j d -> p (j d)"), ua[:].rearrange("p j d -> p (j d)"),
                                                   pa[:].rearrange("p a t -> p (a t)"), ALU.add))
                        dve.tensor_tensor(xh_in[:], h_in[:], xa[:], ALU.add).then_inc(handed, 1)

                    def moe_ln():
                        layer_stats(chb, dve, h_in, b_stats, b_mv, b_var)
                        dve.wait_ge(b_rs, 1)
                        layer_apply(dve, vb, h_in, b_mv, b_rstd).then_inc(vb_ready, 1)
                        dve.wait_ge(vb_turned, 1)
                        for k in range(KD):
                            last = dve.tensor_scalar(mt[:, k], pb[:, 4 + k], v("ln_moe_g", k), v("ln_moe_b", k),
                                                     ALU.mult, ALU.add)
                        last.then_inc(mt_ready, 1)

                    def moe_route():
                        logits = pb[:, 0, 0:J * E].rearrange("p (j e) -> p j e", e=E)
                        dve.wait_ge(logit_mm, 1)
                        chb.step(dve.tensor_reduce(r_m[:], logits, AX.X, ALU.max))
                        dve.tensor_tensor(r_p[:], logits, r_m[:].unsqueeze(2).to_broadcast([P, J, E]),
                                          ALU.subtract).then_inc(r_neg, 1)
                        dve.wait_ge(r_exp, 1)
                        chb.step(dve.tensor_reduce(r_m[:], r_p[:], AX.X, ALU.add))
                        chb.step(dve.reciprocal(r_m[:], r_m[:]))
                        chb.step(dve.tensor_tensor(r_p[:], r_p[:], r_m[:].unsqueeze(2).to_broadcast([P, J, E]), ALU.mult))
                        this = r_p[:].unsqueeze(3).to_broadcast([P, J, E, E])
                        other = r_p[:].unsqueeze(2).to_broadcast([P, J, E, E])
                        before = v("before", 0, E * E).rearrange("p (e o) -> p e o", o=E).unsqueeze(1).to_broadcast([P, J, E, E])
                        chb.inc(dve.tensor_tensor(r_gt[:], other, this, ALU.is_gt))
                        chb.step(dve.tensor_tensor(r_eq[:], other, this, ALU.is_equal))
                        chb.step(dve.tensor_tensor(r_eq[:], r_eq[:], before, ALU.mult))
                        chb.step(dve.tensor_tensor(r_gt[:], r_gt[:], r_eq[:], ALU.add))
                        chb.step(dve.tensor_reduce(r_w[:], r_gt[:], AX.X, ALU.add))
                        chb.step(dve.scalar_tensor_tensor(out=r_w[:], in0=r_w[:], scalar=1.5, in1=r_p[:], op0=ALU.is_lt, op1=ALU.mult))
                        chb.step(dve.tensor_reduce(r_m[:], r_w[:], AX.X, ALU.add))
                        chb.step(dve.reciprocal(r_m[:], r_m[:]))
                        dve.tensor_tensor(r_w[:], r_w[:], r_m[:].unsqueeze(2).to_broadcast([P, J, E]), ALU.mult).then_inc(rw_ready, 1)
                        dve.wait_ge(rwt_mm, 1)
                        dve.tensor_copy(r_wt[0:E, :], pb[0:E, 1, :]).then_inc(rwt_ready, 1)
                        dve.wait_ge(seed_mm, 1)
                        dve.tensor_tensor(acc[:].rearrange("p j d -> p (j d)"), xh_in[:].rearrange("p j d -> p (j d)"),
                                          pb[:, 2:4, :].rearrange("p a t -> p (a t)"), ALU.add).then_inc(acc_ready, 1)

                    def moe_expert(e):
                        dve.wait_ge(down_mm, e + 1)
                        if e == 0:
                            dve.wait_ge(acc_ready, 1)
                        else:
                            dve.wait_ge(ye_taken, e)
                        b = 2 + 2 * (e % 2)
                        ye = pb[:, b:b + 2, :].rearrange("p a (j d) -> p (a j) d", d=D)
                        for j in range(J):
                            last = dve.scalar_tensor_tensor(out=acc[:, j], in0=ye[:, j], scalar=r_w[:, j, e:e + 1],
                                                            in1=acc[:, j], op0=ALU.mult, op1=ALU.add)
                        last.then_inc(moe_done if e == E - 1 else ye_taken, 1)

                    run(order, mamba_ln=mamba_ln, mamba_conv=mamba_conv, mamba_dt=mamba_dt, mamba_scan=mamba_scan,
                        mamba_out=mamba_out, moe_ln=moe_ln, moe_route=moe_route, moe_expert=moe_expert)

                @block.scalar
                def _(act):
                    cha, chb = Chain(act, a_act), Chain(act, b_act)

                    def mamba_ln():
                        act.wait_ge(a_var, 1)
                        layer_rstd(cha, act, a_mv, a_rstd[:], eps[:, 0:1], a_rs)
                        act.wait_ge(a_var, 2)
                        layer_rstd(cha, act, a_mv, a_rstd[:], eps[:, 0:1], a_rs)

                    def mamba_conv():
                        for m in range(2 * C):
                            act.wait_ge(in_ready, m + 1)
                            dst = xpad[:, m, KC - 1:] if m < C else gate[:, m - C]
                            act.activation(dst, pa[:, m % 2], ACT.Identity if m < C else ACT.Silu,
                                           bias=v("in_proj_b", m)).then_inc(in_taken, 1)
                        for c in range(C):
                            act.wait_ge(conv_ready, c + 1)
                            act.activation(xc[:, c], y[:, c], ACT.Silu).then_inc(xc_ready, 1)

                    def mamba_dt():
                        act.wait_ge(dtr_mm, 1)
                        act.activation(dtr[0:DTR, :], pa[0:DTR, 1], ACT.Copy).then_inc(dtr_ready, 1)
                        act.wait_ge(sp_neg, 1)
                        act.activation(soft, soft, ACT.Exp).then_inc(sp_exp, 1)
                        act.wait_ge(sp_one, 1)
                        act.activation(dx, soft1, ACT.Ln).then_inc(sp_log, 1)
                        act.wait_ge(sp_log, 1)
                        act.wait_ge(sp_fix, 1)
                        act.activation(soft1, dx, ACT.Exp, scale=-1.0).then_inc(sp_inv, 1)

                    def mamba_scan(n):
                        act.wait_ge(delta_ready, 1)
                        if n >= 2:
                            act.wait_ge(scan_done, n - 1)
                        for c in range(C):
                            last = act.activation(decay[:, n % 2, c, 1:], delta[:, c, 1:], ACT.Exp, scale=neg_a[:, c, n:n + 1])
                        last.then_inc(decay_ready, 1)

                    def moe_ln():
                        act.wait_ge(b_var, 1)
                        layer_rstd(chb, act, b_mv, b_rstd[:], eps[:, 0:1], b_rs)

                    def moe_route():
                        act.wait_ge(r_neg, 1)
                        act.activation(r_p[:], r_p[:], ACT.Exp).then_inc(r_exp, 1)

                    def moe_expert(e):
                        if e >= 2:
                            act.wait_ge(down_mm, e - 1)
                        if e == 0:
                            act.wait_ge(vb_turned, 1)
                        for f in range(FE):
                            act.wait_ge(up_mm, e * FE + f + 1)
                            act.activation(h1[:, e % 2, f], pb[:, (e * FE + f) % 2], ACT.Silu,
                                           bias=v("b1", e * FE + f)).then_inc(h1_ready, 1)

                    run(order, mamba_ln=mamba_ln, mamba_conv=mamba_conv, mamba_dt=mamba_dt, mamba_scan=mamba_scan,
                        moe_ln=moe_ln, moe_route=moe_route, moe_expert=moe_expert)

                @block.gpsimd
                def _(pool):
                    def mamba_scan(n):
                        pool.wait_ge(hc_done, n + 1)
                        if n >= 1:
                            pool.wait_ge(y_added, n)
                        pool.tensor_tensor(y[:], y[:], state[:, n % 2], ALU.add).then_inc(y_added, 1)

                    run(order, mamba_scan=mamba_scan)

                @block.tensor
                def _(pe):
                    def mamba_ln():
                        pe.wait_ge(va_ready, 1)
                        transpose_tokens(pe, pa, va, ident[:]).then_inc(va_turned, 1)

                    def mamba_conv():
                        pe.wait_ge(ha_ready, 1)
                        for m in range(2 * C):
                            if m >= 2:
                                pe.wait_ge(in_taken, m - 1)
                            for k in range(KD):
                                last = pe.matmul(pa[:, m % 2], w_in[:, k, m * P:(m + 1) * P], ha[:, k],
                                                 start=k == 0, stop=k == KD - 1)
                            last.then_inc(in_ready, 1)

                    def mamba_dt():
                        pe.wait_ge(in_taken, 2 * C)
                        for c in range(C):
                            pe.wait_ge(xc_ready, c + 1)
                            last = pe.matmul(pa[0:6 * NS, 0], w_bc[:, c, :], xc[:, c], start=c == 0, stop=c == C - 1)
                        last.then_inc(bc_mm, 1)
                        for c in range(C):
                            last = pe.matmul(pa[0:DTR, 1], w_dtr[:, c, :], xc[:, c], start=c == 0, stop=c == C - 1)
                        last.then_inc(dtr_mm, 1)
                        pe.wait_ge(dtr_ready, 1)
                        pe.wait_ge(bc_ready, 1)
                        for c in range(C):
                            if c >= 2:
                                pe.wait_ge(dt_taken, c - 1)
                            pe.matmul(pa[:, c % 2], w_dt[0:DTR, c * P:(c + 1) * P], dtr[0:DTR, :],
                                      start=True, stop=True).then_inc(dt_mm, 1)
                        pe.wait_ge(dt_taken, C)

                    def mamba_scan(n):
                        if n >= 1:
                            pe.wait_ge(u_done, n)
                        pe.matmul(pa[:, 0], pick[0:6 * NS, n:n + 1].to_broadcast([6 * NS, P]), bc3[0:6 * NS, :],
                                  start=True, stop=True).then_inc(b_row, 1)
                        if n >= 1:
                            pe.wait_ge(hc_done, n)
                        pe.matmul(pa[:, 1], pick[0:6 * NS, NS + n:NS + n + 1].to_broadcast([6 * NS, P]), bc3[0:6 * NS, :],
                                  start=True, stop=True).then_inc(c_row, 1)

                    def mamba_out():
                        pe.wait_ge(y_gated, 1)
                        out = pa[:].rearrange("p a (j d) -> p (a j) d", d=D)
                        for j in range(J):
                            for c in range(C):
                                last = pe.matmul(out[:, j], y[:, c, j * P:(j + 1) * P], w_op[:, c, :],
                                                 start=c == 0, stop=c == C - 1)
                        last.then_inc(op_mm, 1)

                    def moe_ln():
                        pe.wait_ge(vb_ready, 1)
                        transpose_tokens(pe, pb[:, 4:6], vb, ident[:]).then_inc(vb_turned, 1)

                    def moe_route():
                        pe.wait_ge(mt_ready, 1)
                        for j in range(J):
                            for k in range(KD):
                                last = pe.matmul(pb[:, 0, j * E:(j + 1) * E], mt[:, k, j * P:(j + 1) * P], w_rt[:, k, :],
                                                 start=k == 0, stop=k == KD - 1)
                        last.then_inc(logit_mm, 1)
                        pe.wait_ge(rw_ready, 1)
                        for j in range(J):
                            last = pe.transpose(pb[0:E, 1, j * P:(j + 1) * P], r_w[:, j, :], ident[:])
                        last.then_inc(rwt_mm, 1)
                        pe.wait_ge(rwt_ready, 1)
                        out = pb[:, 2:4].rearrange("p a (j d) -> p (a j) d", d=D)
                        for j in range(J):
                            last = pe.matmul(out[:, j], r_wt[0:E, j * P:(j + 1) * P], b_2[0:E, :], start=True, stop=True)
                        last.then_inc(seed_mm, 1)

                    def up(e):
                        for f in range(FE):
                            n = e * FE + f
                            if n >= 2:
                                pe.wait_ge(h1_ready, n - 1)
                            for k in range(KD):
                                last = pe.matmul(pb[:, n % 2], w_1[:, e, k, f * P:(f + 1) * P], mt[:, k],
                                                 start=k == 0, stop=k == KD - 1)
                            last.then_inc(up_mm, 1)

                    def down(e):
                        pe.wait_ge(h1_ready, (e + 1) * FE)
                        if e == 0:
                            pe.wait_ge(acc_ready, 1)
                        if e >= 2:
                            pe.wait_ge(ye_taken, e - 1)
                        b = 2 + 2 * (e % 2)
                        out = pb[:, b:b + 2].rearrange("p a (j d) -> p (a j) d", d=D)
                        for j in range(J):
                            for f in range(FE):
                                last = pe.matmul(out[:, j], h1[:, e % 2, f, j * P:(j + 1) * P], w_2[:, e, f, :],
                                                 start=f == 0, stop=f == FE - 1)
                        last.then_inc(down_mm, 1)

                    def moe_expert(e):
                        up(e)
                        down(e)

                    run(order, mamba_ln=mamba_ln, mamba_conv=mamba_conv, mamba_dt=mamba_dt, mamba_scan=mamba_scan,
                        mamba_out=mamba_out, moe_ln=moe_ln, moe_route=moe_route, moe_expert=moe_expert)
            clear_all()

        body(0, True, False)
        if NB > 1:
            with nc.Fori(1, NB) as i:
                body(i, True, True)
        body(NB, False, True)


def attention_ffn_pass(nc, io, x1_dram):
    NB = io["x"].shape[0]
    out_dram = io["out"].rearrange("b (j p) d -> b p j d", p=P)
    with ExitStack() as ctx:
        sem_nums = []

        def sb(name, shape, dt=F32):
            return ctx.enter_context(nc.sbuf_tensor(name, [P] + shape, dt))

        def sem(name):
            s = ctx.enter_context(nc.semaphore(name))
            sem_nums.append(s.num)
            return s

        ident = sb("t_ident", [P])
        head_mask = sb("head_mask", [P // DH])
        w_gate = sb("w_gate", [KD, HID])
        w_up = sb("w_up", [KD, HID])
        w_down = sb("w_down", [FH, D])
        w_qkv = sb("w_qkv", [KD, 3 * D])
        w_out = sb("w_out", [KD, D])
        b_qkv = sb("b_qkv", [3 * D])
        b_out = sb("b_out", [D])
        eps = sb("t_eps", [1])
        norm_bias = sb("norm_bias", [1])
        acos_bias = sb("acos_bias", [1])
        xf = sb("xf", [J, D])
        f_stats = sb("f_stats", [J, 6]); f_mv = sb("f_mv", [J, 2]); f_rstd = sb("f_rstd", [J])
        nf = sb("nf", [KD, T])
        g_sb = sb("g_sb", [FH, T])
        vf = g_sb[:, 0:2].rearrange("p k (j d) -> p (k j) d", d=D)
        u_sb = sb("u_sb", [FH, T])
        yf = sb("yf", [J, D])
        x2_in = sb("x2_in", [J, D])
        x3 = sb("x3", [J, D])
        x2 = sb("x2", [J, D])
        t_stats = sb("t_stats", [J, 6]); t_mv = sb("t_mv", [J, 2]); t_rstd = sb("t_rstd", [J])
        vt = sb("vt", [J, D])
        nt = sb("nt", [KD, T])
        qk = sb("qk", [J, 2 * D])
        val = sb("val", [J, D])
        ss = sb("ss", [J, 2 * H])
        qkt = sb("qkt", [2 * KD, T])
        k_one = sb("k_one", [2, T])
        score = sb("score", [2, HG, J, T])
        cosine = sb("cosine", [2, 2, T])
        log_m = sb("log_m", [2, 2, T])
        n_c = sb("n_c", [J])
        v_n = sb("v_n", [HG, J, VW])
        o_t = sb("o_t", [T])
        d_n = sb("d_n", [J, HG]); d_m = sb("d_m", [J, HG])
        o_tok = vt
        ot = nt
        pc = ctx.enter_context(nc.psum_tensor("pc", [P, 6, T], F32))
        pf = ctx.enter_context(nc.psum_tensor("pf", [P, 2, T], F32))

        loaded = sem("t_loaded")
        x1_loaded = sem("x1_loaded"); y_stored = sem("y_stored")
        f_dve = sem("f_dve"); f_act = sem("f_act"); f_var = sem("f_var"); f_rs = sem("f_rs")
        vf_ready = sem("vf_ready"); vf_turned = sem("vf_turned"); nf_ready = sem("nf_ready")
        gate_mm = sem("gate_mm"); gate_taken = sem("gate_taken"); upf_mm = sem("upf_mm"); upf_taken = sem("upf_taken")
        silu_done = sem("silu_done"); hid_ready = sem("hid_ready"); dn_mm = sem("dn_mm"); ffn_done = sem("ffn_done")
        t_dve = sem("t_dve"); t_act = sem("t_act"); t_var = sem("t_var"); t_rs = sem("t_rs")
        x2_taken = sem("x2_taken"); vt_ready = sem("vt_ready"); vt_turned = sem("vt_turned"); nt_ready = sem("nt_ready")
        qkv_mm = sem("qkv_mm"); qkv_taken = sem("qkv_taken"); ss_ready = sem("ss_ready"); rn_ready = sem("rn_ready")
        qk_ready = sem("qk_ready"); qk_turned = sem("qk_turned"); qkt_ready = sem("qkt_ready")
        k_ready = sem("k_ready"); s_mm = sem("s_mm"); cos_ready = sem("cos_ready")
        logp_done = sem("logp_done"); logm_done = sem("logm_done"); tan_done = sem("tan_done")
        atan_done = sem("atan_done"); s_ready = sem("s_ready"); log1_done = sem("log1_done")
        v_ready = sem("v_ready"); pv_mm = sem("pv_mm"); ot_ready = sem("ot_ready"); ot_turned = sem("ot_turned")
        o_norm = sem("o_norm"); o_turned = sem("o_turned"); o_ready = sem("o_ready"); wo_mm = sem("wo_mm")
        x3_ready = sem("x3_ready")
        sems = range(min(sem_nums), max(sem_nums) + 1)
        assert len(sems) == len(sem_nums)

        def clear_all():
            nc.sync.sem_clear(sems)
            nc.all_engine_barrier()

        with nc.Block() as block:
            plain = [(ident, "ident"), (head_mask, "head_mask"), (w_qkv, "w_qkv"), (w_out, "w_out"),
                     (b_qkv, "b_qkv"), (b_out, "b_out")]
            coded = [(w_gate, "w_gate", score[:, 0, 0:1]), (w_up, "w_up", score[:, 0, 1:2]), (w_down, "w_down", score[:, 0, 2:3])]

            @block.sync
            def _(sp):
                for dst, name in plain:
                    src = io[name]
                    if name in ("b_qkv", "b_out"):
                        src = src.partition_broadcast(P)
                    sp.dma_start(dst[:], src).then_inc(loaded, 16)
                for dst, name, room in coded:
                    flat = room.rearrange("p a j t -> p (a j t)")[:, 0:FH * D].bitcast(I32)
                    sp.dma_start(flat, io[name].rearrange("p a b -> p (a b)")).then_inc(loaded, 16)

            @block.vector
            def _(dve):
                ch = Chain(dve, t_dve)
                ch.inc(dve.memset(eps[:], LN_EPS))
                ch.inc(dve.memset(norm_bias[:], 0.5 * math.log(Q_SHIFT)))
                ch.inc(dve.memset(acos_bias[:], 1.0 + math.pi / 2))
                ch.step(dve.memset(v_n[:], 0.0))
                ch.inc(dve.memset(v_n[:, :, :, DH + 1:DH + 2], 1.0))
                dve.wait_ge(loaded, 16 * (len(plain) + len(coded)))
                for dst, name, room in coded:
                    flat = room.rearrange("p a j t -> p (a j t)")[:, 0:FH * D].bitcast(I32)
                    ch.step(dve.tensor_scalar(dst[:].rearrange("p a b -> p (a b)"), flat, 1.0 / 127.0, None, ALU.mult))
        clear_all()

        def body(i, attend, last_ffn, first_ffn):
            ffns = (["last"] if last_ffn else []) + (["first"] if first_ffn else [])
            ffn_steps = []
            for n, which in enumerate(ffns):
                ffn_steps += [("ffn_ln", n, which), ("ffn_up", n), ("ffn_down", n, which)]
            t_steps = [("t_ln",), ("t_qkv",), ("t_turn",)]
            for g in range(NG + 1):
                if g >= 1:
                    t_steps += [("t_weigh", g - 1)]
                if g < NG:
                    t_steps += [("t_score", g)]
                if g >= 1:
                    t_steps += [("t_values", g - 1)]
                if g < NG:
                    t_steps += [("t_angle", g)]
            t_steps += [("t_out",)]
            order = beside(t_steps if attend else [], ffn_steps)

            with nc.Block() as block:
                @block.sync
                def _(sp):
                    for n, which in enumerate(ffns):
                        if which == "first":
                            if n == 1:
                                sp.wait_ge(ffn_done, 1)
                            sp.dma_start(xf[:], x1_dram[bass.ds(i + 1, 1)].rearrange("o p j d -> (o p) j d")).then_inc(x1_loaded, 16)
                        else:
                            sp.wait_ge(ffn_done, 1)
                            sp.dma_start(out_dram[bass.ds(i - 1, 1)].rearrange("o p j d -> (o p) j d"), yf[:]).then_inc(y_stored, 16)
                            sp.wait_ge(y_stored, 16)

                @block.vector
                def _(dve):
                    chf, cht = Chain(dve, f_dve), Chain(dve, t_dve)

                    def ffn_ln(n, which):
                        x = xf if which == "first" else x3
                        if which == "first":
                            dve.wait_ge(x1_loaded, 16)
                        layer_stats(chf, dve, x, f_stats, f_mv, f_var)
                        dve.wait_ge(f_rs, n + 1)
                        if n:
                            dve.wait_ge(dn_mm, n)
                        layer_apply(dve, vf, x, f_mv, f_rstd).then_inc(vf_ready, 1)
                        dve.wait_ge(vf_turned, n + 1)
                        dve.tensor_copy(nf[:], pf[:]).then_inc(nf_ready, 1)

                    def ffn_up(n):
                        for m in range(FH):
                            dve.wait_ge(gate_mm, n * FH + m + 1)
                            dve.tensor_copy(g_sb[:, m], pf[:, 0]).then_inc(gate_taken, 1)
                            dve.wait_ge(upf_mm, n * FH + m + 1)
                            dve.tensor_copy(u_sb[:, m], pf[:, 1]).then_inc(upf_taken, 1)

                    def ffn_down(n, which):
                        dve.wait_ge(dn_mm, n + 1)
                        if which == "first" and attend:
                            dve.wait_ge(x2_taken, 1)
                        x, dst = (xf, x2_in) if which == "first" else (x3, yf)
                        dve.tensor_tensor(dst[:].rearrange("p j d -> p (j d)"), x[:].rearrange("p j d -> p (j d)"),
                                          pf[:].rearrange("p a t -> p (a t)"), ALU.add).then_inc(ffn_done, 1)

                    def t_ln():
                        dve.tensor_copy(x2[:], x2_in[:]).then_inc(x2_taken, 1)
                        dve.wait_ge(x2_taken, 1)
                        layer_stats(cht, dve, x2, t_stats, t_mv, t_var)
                        dve.wait_ge(t_rs, 1)
                        layer_apply(dve, vt, x2, t_mv, t_rstd).then_inc(vt_ready, 1)
                        dve.wait_ge(vt_turned, 1)
                        dve.tensor_copy(nt[:], pc[:, 0:2]).then_inc(nt_ready, 1)

                    def t_qkv():
                        for j in range(J):
                            dve.wait_ge(qkv_mm, j + 1)
                            b = 2 * (j % 2)
                            dve.tensor_tensor(qk[:, j], pc[:, b], b_qkv[:, 0:2 * D], ALU.add).then_inc(qkv_taken, 1)
                            dve.tensor_tensor(val[:, j], pc[:, b + 1, 0:D], b_qkv[:, 2 * D:], ALU.add).then_inc(qkv_taken, 1)
                        dve.wait_ge(qkv_taken, 2 * J)
                        sq = score[:, 1, 0]
                        cht.step(dve.tensor_tensor(sq, qk[:], qk[:], ALU.mult))
                        cht.step(dve.tensor_reduce(ss[:], sq.rearrange("p j (h d) -> p j h d", d=DH), AX.X, ALU.add))
                        dve.tensor_scalar(ss[:], ss[:], 1e-24, None, ALU.max).then_inc(ss_ready, 1)
                        dve.wait_ge(rn_ready, 1)
                        q4 = qk[:].rearrange("p j (h d) -> p (j h) d", d=DH)
                        dve.tensor_tensor(q4, q4, ss[:].rearrange("p j h -> p (j h)").unsqueeze(2).to_broadcast([P, J * 2 * H, DH]),
                                          ALU.mult).then_inc(qk_ready, 1)

                    def t_turn():
                        dve.wait_ge(qk_turned, 1)
                        dve.tensor_copy(qkt[:], pc[:, 0:4]).then_inc(qkt_ready, 1)

                    def t_score(g):
                        for h in range(g * HG, (g + 1) * HG):
                            if h == 0:
                                dve.wait_ge(qkt_ready, 1)
                            if h >= 2:
                                dve.wait_ge(s_mm, 2 * (h - 1))
                            m = h % (P // DH)
                            dve.tensor_scalar(k_one[:, h % 2], qkt[:, KD + h // (P // DH)], head_mask[:, m:m + 1], None,
                                              ALU.mult).then_inc(k_ready, 1)
                            for s in range(2):
                                n = 2 * h + s
                                dve.wait_ge(s_mm, n + 1)
                                if n >= 2:
                                    dve.wait_ge(logm_done, n - 1)
                                dve.tensor_scalar(cosine[:, s], pc[:, 2 * s:2 * s + 2], -1.0 + 1e-7, 1.0 - 1e-7,
                                                  ALU.max, ALU.min).then_inc(cos_ready, 1)

                    def t_weigh(g):
                        for hh in range(HG):
                            h = g * HG + hh
                            dve.wait_ge(s_ready, h + 1)
                            cht.step(dve.tensor_reduce(n_c[:], score[:, g % 2, hh], AX.X, ALU.add))
                            cht.step(dve.reciprocal(n_c[:], n_c[:]))
                            if hh == 0 and g >= 1:
                                dve.wait_ge(pv_mm, g)
                            cht.inc(dve.tensor_tensor(v_n[:, hh, :, 0:DH], val[:, :, h * DH:(h + 1) * DH],
                                                      n_c[:].unsqueeze(2).to_broadcast([P, J, DH]), ALU.mult))
                            cht.inc(dve.tensor_copy(v_n[:, hh, :, DH:DH + 1], n_c[:].unsqueeze(2)))
                            dve.wait_ge(t_dve, cht.n)
                        dve.sem_inc(v_ready, 1)

                    def t_values(g):
                        dve.wait_ge(pv_mm, g + 1)
                        if g >= 1:
                            dve.wait_ge(ot_turned, g)
                        dve.tensor_copy(o_t[:], pc[:, 4]).then_inc(ot_ready, 1)
                        dve.wait_ge(ot_turned, g + 1)
                        o = pc[:, 5].rearrange("p (j h w) -> p j h w", h=HG, w=P // HG)
                        cht.step(dve.reciprocal(d_n[:], o[:, :, :, DH + 1]))
                        cht.step(dve.tensor_tensor(d_m[:], d_n[:], o[:, :, :, DH], ALU.mult))
                        cht.step(dve.tensor_scalar(d_m[:], d_m[:], 1e-12, None, ALU.max))
                        cht.step(dve.reciprocal(d_m[:], d_m[:]))
                        cht.step(dve.tensor_tensor(d_m[:], d_m[:], d_n[:], ALU.mult))
                        dst = o_tok[:, :, g * HG * DH:(g + 1) * HG * DH].rearrange("p j (h d) -> p j h d", d=DH)
                        dve.tensor_tensor(dst, o[:, :, :, 0:DH], d_m[:].unsqueeze(3).to_broadcast([P, J, HG, DH]),
                                          ALU.mult).then_inc(o_norm, 1)

                    def t_out():
                        dve.wait_ge(o_turned, 1)
                        cht.inc(dve.tensor_tensor(x2[:], x2[:], b_out[:].unsqueeze(1).to_broadcast([P, J, D]), ALU.add))
                        dve.tensor_copy(ot[:], pc[:, 0:2]).then_inc(o_ready, 1)
                        dve.wait_ge(wo_mm, 1)
                        cht.sync()
                        if last_ffn:
                            dve.wait_ge(ffn_done, 1)
                        dve.tensor_tensor(x3[:].rearrange("p j d -> p (j d)"), x2[:].rearrange("p j d -> p (j d)"),
                                          pc[:, 2:4].rearrange("p a t -> p (a t)"), ALU.add).then_inc(x3_ready, 1)

                    run(order, ffn_ln=ffn_ln, ffn_up=ffn_up, ffn_down=ffn_down, t_ln=t_ln, t_qkv=t_qkv, t_turn=t_turn,
                        t_score=t_score, t_weigh=t_weigh, t_values=t_values, t_out=t_out)

                @block.scalar
                def _(act):
                    chf, cht = Chain(act, f_act), Chain(act, t_act)

                    def ffn_ln(n, which):
                        act.wait_ge(f_var, n + 1)
                        layer_rstd(chf, act, f_mv, f_rstd[:], eps[:, 0:1], f_rs)

                    def ffn_up(n):
                        act.wait_ge(gate_taken, (n + 1) * FH)
                        act.activation(g_sb[:], g_sb[:], ACT.Silu).then_inc(silu_done, 1)

                    def t_ln():
                        act.wait_ge(t_var, 1)
                        layer_rstd(cht, act, t_mv, t_rstd[:], eps[:, 0:1], t_rs)

                    def t_qkv():
                        act.wait_ge(ss_ready, 1)
                        cht.step(act.activation(ss[:], ss[:], ACT.Ln, scale=Q_SHIFT))
                        act.activation(ss[:], ss[:], ACT.Exp, scale=-0.5, bias=norm_bias[:, 0:1]).then_inc(rn_ready, 1)

                    def t_score(g):
                        for h in range(g * HG, (g + 1) * HG):
                            for s in range(2):
                                n = 2 * h + s
                                act.wait_ge(cos_ready, n + 1)
                                if g >= 2:
                                    act.wait_ge(pv_mm, g - 1)
                                if n == 0:
                                    act.wait_ge(ss_ready, 1)
                                act.activation(score[:, g % 2, h % HG, 2 * s:2 * s + 2], cosine[:, s], ACT.Ln,
                                               bias=1.0).then_inc(logp_done, 1)
                                if n >= 2:
                                    act.wait_ge(tan_done, n - 1)
                                act.activation(log_m[:, s], cosine[:, s], ACT.Ln, scale=-1.0, bias=1.0).then_inc(logm_done, 1)

                    def t_angle(g):
                        for h in range(g * HG, (g + 1) * HG):
                            s = score[:, g % 2, h % HG]
                            act.wait_ge(tan_done, 2 * h + 2)
                            cht.inc(act.activation(s, s, ACT.Tanh, scale=0.25))
                        for h in range(g * HG, (g + 1) * HG):
                            s = score[:, g % 2, h % HG]
                            act.wait_ge(t_act, cht.n - HG + 1 + h % HG)
                            act.activation(s, s, ACT.Arctan).then_inc(atan_done, 1)

                    def t_weigh(g):
                        for h in range(g * HG, (g + 1) * HG):
                            s = score[:, g % 2, h % HG]
                            act.wait_ge(atan_done, h + 1)
                            act.activation(s, s, ACT.Ln, scale=-2.0, bias=acos_bias[:, 0:1]).then_inc(log1_done, 1)
                        for h in range(g * HG, (g + 1) * HG):
                            s = score[:, g % 2, h % HG]
                            act.wait_ge(log1_done, h + 1)
                            act.activation(s, s, ACT.Exp, scale=-3.2).then_inc(s_ready, 1)

                    run(order, ffn_ln=ffn_ln, ffn_up=ffn_up, t_ln=t_ln, t_qkv=t_qkv, t_score=t_score, t_angle=t_angle,
                        t_weigh=t_weigh)

                @block.gpsimd
                def _(pool):
                    def ffn_up(n):
                        pool.wait_ge(silu_done, n + 1)
                        pool.wait_ge(upf_taken, (n + 1) * FH)
                        pool.tensor_tensor(g_sb[:], g_sb[:], u_sb[:], ALU.mult).then_inc(hid_ready, 1)

                    def t_score(g):
                        for h in range(g * HG, (g + 1) * HG):
                            for s in range(2):
                                n = 2 * h + s
                                t = score[:, g % 2, h % HG, 2 * s:2 * s + 2]
                                pool.wait_ge(logp_done, n + 1)
                                pool.wait_ge(logm_done, n + 1)
                                pool.tensor_tensor(t, t, log_m[:, s], ALU.subtract).then_inc(tan_done, 1)

                    run(order, ffn_up=ffn_up, t_score=t_score)

                @block.tensor
                def _(pe):
                    def ffn_ln(n, which):
                        pe.wait_ge(vf_ready, n + 1)
                        if n:
                            pe.wait_ge(ffn_done, n)
                        transpose_tokens(pe, pf, vf, ident[:]).then_inc(vf_turned, 1)

                    def ffn_up(n):
                        pe.wait_ge(nf_ready, n + 1)
                        for m in range(FH):
                            if m:
                                pe.wait_ge(gate_taken, n * FH + m)
                            for k in range(KD):
                                last = pe.matmul(pf[:, 0], w_gate[:, k, m * P:(m + 1) * P], nf[:, k], start=k == 0, stop=k == KD - 1)
                            last.then_inc(gate_mm, 1)
                            if m:
                                pe.wait_ge(upf_taken, n * FH + m)
                            for k in range(KD):
                                last = pe.matmul(pf[:, 1], w_up[:, k, m * P:(m + 1) * P], nf[:, k], start=k == 0, stop=k == KD - 1)
                            last.then_inc(upf_mm, 1)

                    def ffn_down(n, which):
                        pe.wait_ge(hid_ready, n + 1)
                        out = pf[:].rearrange("p a (j d) -> p (a j) d", d=D)
                        for j in range(J):
                            for m in range(FH):
                                last = pe.matmul(out[:, j], g_sb[:, m, j * P:(j + 1) * P], w_down[:, m, :],
                                                 start=m == 0, stop=m == FH - 1)
                        last.then_inc(dn_mm, 1)

                    def t_ln():
                        pe.wait_ge(vt_ready, 1)
                        transpose_tokens(pe, pc, vt, ident[:]).then_inc(vt_turned, 1)

                    def t_qkv():
                        pe.wait_ge(nt_ready, 1)
                        for j in range(J):
                            b = 2 * (j % 2)
                            if j >= 2:
                                pe.wait_ge(qkv_taken, 2 * (j - 1))
                            for k in range(KD):
                                pe.matmul(pc[:, b], nt[:, k, j * P:(j + 1) * P], w_qkv[:, k, 0:2 * D], start=k == 0, stop=k == KD - 1)
                            for k in range(KD):
                                last = pe.matmul(pc[:, b + 1, 0:D], nt[:, k, j * P:(j + 1) * P], w_qkv[:, k, 2 * D:],
                                                 start=k == 0, stop=k == KD - 1)
                            last.then_inc(qkv_mm, 1)

                    def t_turn():
                        pe.wait_ge(qk_ready, 1)
                        for k in range(2 * KD):
                            for j in range(J):
                                last = pe.transpose(pc[:, k, j * P:(j + 1) * P], qk[:, j, k * P:(k + 1) * P], ident[:])
                        last.then_inc(qk_turned, 1)

                    def t_score(g):
                        for h in range(g * HG, (g + 1) * HG):
                            pe.wait_ge(k_ready, h + 1)
                            for s in range(2):
                                n = 2 * h + s
                                if n >= 2:
                                    pe.wait_ge(cos_ready, n - 1)
                                else:
                                    pe.wait_ge(qkt_ready, 1)
                                for c in range(2):
                                    t = 2 * s + c
                                    last = pe.matmul(pc[:, t], k_one[:, h % 2, t * P:(t + 1) * P], qkt[:, h // (P // DH)],
                                                     start=True, stop=True)
                                last.then_inc(s_mm, 1)

                    def t_values(g):
                        pe.wait_ge(v_ready, g + 1)
                        pe.wait_ge(s_ready, (g + 1) * HG)
                        if g >= 1:
                            pe.wait_ge(ot_ready, g)
                        for t in range(J):
                            for hh in range(HG):
                                a = hh * (P // HG)
                                last = pe.matmul(pc[a:a + VW, 4], v_n[:, hh, t, :], score[:, g % 2, hh, t], start=t == 0,
                                                 stop=t == J - 1)
                        last.then_inc(pv_mm, 1)
                        pe.wait_ge(ot_ready, g + 1)
                        if g >= 1:
                            pe.wait_ge(o_norm, g)
                        for j in range(J):
                            last = pe.transpose(pc[:, 5, j * P:(j + 1) * P], o_t[:, j * P:(j + 1) * P], ident[:])
                        last.then_inc(ot_turned, 1)

                    def t_out():
                        pe.wait_ge(o_norm, NG)
                        transpose_tokens(pe, pc, o_tok, ident[:]).then_inc(o_turned, 1)
                        pe.wait_ge(o_ready, 1)
                        out = pc[:, 2:4].rearrange("p a (j d) -> p (a j) d", d=D)
                        for j in range(J):
                            for k in range(KD):
                                last = pe.matmul(out[:, j], ot[:, k, j * P:(j + 1) * P], w_out[:, k, :], start=k == 0, stop=k == KD - 1)
                        last.then_inc(wo_mm, 1)

                    run(order, ffn_ln=ffn_ln, ffn_up=ffn_up, ffn_down=ffn_down, t_ln=t_ln, t_qkv=t_qkv, t_turn=t_turn,
                        t_score=t_score, t_values=t_values, t_out=t_out)
            clear_all()

        body(-1, False, False, True)
        body(0, True, False, NB > 1)
        if NB > 2:
            with nc.Fori(1, NB - 1) as i:
                body(i, True, True, True)
        if NB > 1:
            body(NB - 1, True, True, False)
        body(NB, False, True, False)


def program(nc, io):
    x1_dram = nc.dram_tensor("x1_rows", (io["x"].shape[0], P, J, D), F32, kind="Internal").ap()
    mamba_moe_pass(nc, io, x1_dram)
    attention_ffn_pass(nc, io, x1_dram)


def kernel(**inputs):
    import numpy as np
    import concourse.bacc as bacc
    from concourse import mybir as my
    from concourse.bass_utils import run_bass_kernel_spmd

    a = {k.replace("L0_attn_a_", "").replace("L0_ffn_", "").replace("L0_attn_b_", "t_"): np.asarray(x)
         for k, x in inputs.items()}
    rows = lambda w: np.ascontiguousarray(w.reshape(-1, P, w.shape[-1]).transpose(1, 0, 2))
    cols = lambda w: w.reshape(-1, P).T
    x_proj = a["x_proj_w"].T
    before = np.tril(np.ones((E, E), np.float32), -1).reshape(1, -1).repeat(P, 0)
    head_mask = np.kron(np.eye(P // DH, dtype=np.float32), np.ones((DH, 1), np.float32))
    vectors = {
        "ln_mamba_g": cols(a["ln_mamba_g"]), "ln_mamba_b": cols(a["ln_mamba_b"]), "ln_moe_g": cols(a["ln_moe_g"]),
        "ln_moe_b": cols(a["ln_moe_b"]), "in_proj_b": cols(a["in_proj_b"]),
        "conv_w": rows(a["conv_w"]).reshape(P, -1), "conv_b": cols(a["conv_b"]), "dt_proj_b": cols(a["dt_proj_b"]),
        "A_log": rows(a["A_log"]).reshape(P, -1), "D_skip": cols(a["D_skip"]),
        "b1": cols(a["b1"]), "head_mask": head_mask, "before": before,
    }
    arrays = {
        "x": a["x"],
        "vectors": np.concatenate([vectors[n] for n in VEC], axis=1),
        "ident": np.eye(P, dtype=np.float32),
        "pick": np.tile(np.eye(2 * NS, dtype=np.float32), (3, 1)).astype(my.dt.np(BF16)),
        "head_mask": head_mask,
        "w_in": rows(a["in_proj_w"].T),
        "w_bc": rows(np.tile(x_proj[:, DTR:], (1, 3))),
        "w_dtr": rows(x_proj[:, :DTR]),
        "w_dt": a["dt_proj_w"].T,
        "w_op": rows(a["out_proj_w"].T),
        "w_rt": rows(a["router_w"].T),
        "w_1": a["w1"].transpose(2, 0, 1).reshape(KD, P, E, DFF).transpose(1, 2, 0, 3),
        "w_2": a["w2"].transpose(2, 0, 1).reshape(FE, P, E, D).transpose(1, 2, 0, 3),
        "b2": a["b2"],
        "w_gate": rows(a["w_gate"].T), "w_up": rows(a["w_up"].T), "w_down": rows(a["w_down"].T),
        "w_qkv": rows(a["t_w_qkv"].T), "w_out": rows(a["t_w_out"].T), "b_qkv": a["t_b_qkv"], "b_out": a["t_b_out"],
    }
    arrays = {n: np.ascontiguousarray(x) for n, x in arrays.items()}
    nc = bacc.Bacc("TRN2", target_bir_lowering=False, num_devices=1)
    io = {n: nc.dram_tensor(f"in_{n}", x.shape, my.dt.from_np(x.dtype), kind="ExternalInput").ap() for n, x in arrays.items()}
    io["out"] = nc.dram_tensor("out_0", arrays["x"].shape, F32, kind="ExternalOutput").ap()
    program(nc, io)
    r = run_bass_kernel_spmd(nc, [{f"in_{n}": x for n, x in arrays.items()}], core_ids=[0])
    return r.results[0]["out_0"]
```

```python
import math
from contextlib import ExitStack

import concourse.bass as bass
from concourse import mybir

F32 = mybir.dt.float32
BF16 = mybir.dt.bfloat16
I32 = mybir.dt.int32
ACT = mybir.ActivationFunctionType
ALU = mybir.AluOpType
AX = mybir.AxisListType

P = 128
D = 256
T = 512
J = T // P
KD = D // P
DI = 2 * D
C = DI // P
NS = 16
DTR = D // 16
KC = 4
E = 8
DFF = 2 * D
FE = DFF // P
HID = 768
FH = HID // P
H = 16
DH = D // H
HG = 4
NG = H // HG
VW = P // HG
LN_EPS = 1e-5
Q_SHIFT = 2.0 ** 30

VEC = {}
_at = 0
for _name, _n in (("ln_mamba_g", KD), ("ln_mamba_b", KD), ("ln_moe_g", KD), ("ln_moe_b", KD),
                  ("in_proj_b", 2 * C), ("conv_w", C * KC), ("conv_b", C), ("dt_proj_b", C),
                  ("A_log", C * NS), ("D_skip", C), ("b1", E * FE), ("head_mask", P // DH),
                  ("before", E * E)):
    VEC[_name] = (_at, _at + _n)
    _at += _n
VEC_N = _at


class Chain:

    def __init__(self, eng, sem):
        self.eng, self.sem, self.n = eng, sem, 0

    def inc(self, ins):
        ins.then_inc(self.sem, 1)
        self.n += 1

    def sync(self):
        self.eng.wait_ge(self.sem, self.n)

    def step(self, ins):
        self.inc(ins)
        self.sync()


def layer_stats(ch, dve, x, stats, mv, var_ready):
    for j in range(J):
        ch.inc(dve.bn_stats(stats[:, j, :], x[:, j, :]))
    ch.sync()
    for j in range(J):
        last = dve.bn_aggr(mv[:, j, :], stats[:, j, :])
    last.then_inc(var_ready, 1)


def layer_rstd(ch, act, mv, rstd, eps, rstd_ready):
    ch.step(act.activation(rstd, mv[:, :, 1], ACT.Ln, bias=eps))
    act.activation(rstd, rstd, ACT.Exp, scale=-0.5).then_inc(rstd_ready, 1)


def layer_apply(dve, out, x, mv, rstd):
    for j in range(J):
        last = dve.tensor_scalar(out[:, j, :], x[:, j, :], mv[:, j, 0:1], rstd[:, j:j + 1],
                                 ALU.subtract, ALU.mult)
    return last


def transpose_tokens(pe, out, x, ident):
    for k in range(KD):
        for j in range(J):
            last = pe.transpose(out[:, k, j * P:(j + 1) * P], x[:, j, k * P:(k + 1) * P], ident)
    return last


def run(order, **parts):
    for name, *args in order:
        if name in parts:
            parts[name](*args)


def beside(a, b):
    n = [(i / max(len(a), 1), 0, s) for i, s in enumerate(a)] + [(i / max(len(b), 1), 1, s) for i, s in enumerate(b)]
    return [s for _, _, s in sorted(n, key=lambda x: x[:2])]


def mamba_moe_pass(nc, io, x1_dram):
    NB = io["x"].shape[0]
    x_dram = io["x"].rearrange("b (j p) d -> b p j d", p=P)
    with ExitStack() as ctx:
        first_sem = []

        def sb(name, shape, dt=F32):
            return ctx.enter_context(nc.sbuf_tensor(name, [P] + shape, dt))

        def sem(name):
            s = ctx.enter_context(nc.semaphore(name))
            first_sem.append(s.num)
            return s

        vec = sb("m_vec", [VEC_N])
        ident = sb("m_ident", [P])
        pick = sb("m_pick", [2 * NS], BF16)
        w_in = sb("w_in", [KD, 2 * DI])
        w_bc = sb("w_bc", [C, 6 * NS])
        w_dtr = sb("w_dtr", [C, DTR])
        w_dt = sb("w_dt", [DI])
        w_op = sb("w_op", [C, D])
        w_rt = sb("w_rt", [KD, E])
        w_1 = sb("w_1", [E, KD, DFF])
        w_2 = sb("w_2", [E, FE, D])
        b_2 = sb("b_2", [D])
        neg_a = sb("neg_a", [C, NS])
        eps = sb("m_eps", [1])
        xa = sb("xa", [J, D])
        ua = sb("ua", [J, D])
        a_stats = sb("a_stats", [J, 6])
        a_mv = sb("a_mv", [J, 2])
        a_rstd = sb("a_rstd", [J])
        gate = sb("gate", [C, T])
        both = sb("delta_dx", [2, C, T])
        delta, dx = both[:, 0], both[:, 1]
        y = sb("y", [C, T])
        decay = sb("decay", [2, C, T])
        state = sb("state", [2, C, T])
        bc3 = sb("bc3", [T], BF16)
        bc_rest = sb("bc_rest", [T])
        dtr = sb("dtr", [T])
        xpad = both[:].rearrange("p a c t -> p (a c t)")[:, 0:C * (T + KC - 1)].rearrange("p (c t) -> p c t", c=C)
        va, ha = decay[:, 1, 0:2, :].rearrange("p c (j d) -> p (c j) d", d=D), decay[:, 1, 2:4, :]
        soft, soft1 = state[:, 0], decay[:, 1]
        xc = state[:, 1]
        h_in = sb("h_in", [J, D])
        xh_in = sb("xh_in", [J, D])
        acc = sb("acc", [J, D])
        b_stats = sb("b_stats", [J, 6])
        b_mv = sb("b_mv", [J, 2])
        b_rstd = sb("b_rstd", [J])
        mt = sb("mt", [KD, T])
        h1 = sb("h1", [2, FE, T])
        vb = h1[:, 0, 0:2, :].rearrange("p c (j d) -> p (c j) d", d=D)
        r_p = sb("r_p", [J, E])
        r_m = sb("r_m", [J])
        r_gt = sb("r_gt", [J, E, E])
        r_eq = sb("r_eq", [J, E, E])
        r_w = sb("r_w", [J, E])
        r_wt = sb("r_wt", [T])

        pa = ctx.enter_context(nc.psum_tensor("pa", [P, 2, T], F32))
        pb = ctx.enter_context(nc.psum_tensor("pb", [P, 6, T], F32))

        def v(name, i=0, n=None):
            a, b = VEC[name]
            return vec[:, a + i:a + i + (n or 1)]

        loaded = sem("m_loaded")
        setup = sem("m_setup")
        x_loaded = sem("x_loaded")
        a_dve = sem("a_dve"); a_act = sem("a_act")
        a_var = sem("a_var"); a_rs = sem("a_rs"); va_ready = sem("va_ready")
        va_turned = sem("va_turned"); ha_ready = sem("ha_ready")
        in_ready = sem("in_ready"); in_taken = sem("in_taken")
        conv_ready = sem("conv_ready"); xc_ready = sem("xc_ready")
        bc_mm = sem("bc_mm"); dtr_mm = sem("dtr_mm"); bc_ready = sem("bc_ready"); dtr_ready = sem("dtr_ready")
        dt_mm = sem("dt_mm"); dt_taken = sem("dt_taken")
        sp_neg = sem("sp_neg"); sp_exp = sem("sp_exp"); sp_one = sem("sp_one"); sp_log = sem("sp_log")
        sp_fix = sem("sp_fix"); sp_inv = sem("sp_inv")
        delta_ready = sem("delta_ready")
        b_row = sem("b_row"); c_row = sem("c_row"); decay_ready = sem("decay_ready")
        u_done = sem("u_done"); scan_done = sem("scan_done"); hc_done = sem("hc_done"); y_added = sem("y_added")
        y_start = sem("y_start")
        y_gated = sem("y_gated"); op_mm = sem("op_mm"); handed = sem("handed")
        b_dve = sem("b_dve"); b_act = sem("b_act")
        b_var = sem("b_var"); b_rs = sem("b_rs"); vb_ready = sem("vb_ready")
        vb_turned = sem("vb_turned"); mt_ready = sem("mt_ready")
        logit_mm = sem("logit_mm"); r_neg = sem("r_neg"); r_exp = sem("r_exp"); rw_ready = sem("rw_ready")
        rwt_mm = sem("rwt_mm"); rwt_ready = sem("rwt_ready"); seed_mm = sem("seed_mm"); acc_ready = sem("acc_ready")
        up_mm = sem("up_mm"); h1_ready = sem("h1_ready"); down_mm = sem("down_mm"); ye_taken = sem("ye_taken")
        moe_done = sem("moe_done"); x1_stored = sem("x1_stored")
        sems = range(min(first_sem), max(first_sem) + 1)
        assert len(sems) == len(first_sem)

        def clear_all():
            nc.sync.sem_clear(sems)
            nc.all_engine_barrier()

        with nc.Block() as block:
            loads = [(vec, "vectors"), (ident, "ident"), (w_in, "w_in"), (w_bc, "w_bc"), (w_dtr, "w_dtr"),
                     (w_op, "w_op"), (w_rt, "w_rt"), (w_1, "w_1"), (w_2, "w_2")]

            @block.sync
            def _(sp):
                for dst, name in loads:
                    sp.dma_start(dst[:], io[name]).then_inc(loaded, 16)
                sp.dma_start(w_dt[0:DTR, :], io["w_dt"]).then_inc(loaded, 16)
                sp.dma_start(b_2[0:E, :], io["b2"]).then_inc(loaded, 16)
                sp.dma_start(pick[0:6 * NS, :], io["pick"]).then_inc(loaded, 16)

            @block.scalar
            def _(act):
                act.wait_ge(loaded, 16 * (len(loads) + 3))
                act.activation(neg_a[:].rearrange("p c n -> p (c n)"), v("A_log", 0, C * NS), ACT.Exp).then_inc(setup, 1)

            @block.vector
            def _(dve):
                ch = Chain(dve, a_dve)
                ch.inc(dve.memset(eps[:], LN_EPS))
                ch.inc(dve.memset(decay[:], 0.0))
                dve.wait_ge(setup, 1)
                ch.step(dve.tensor_scalar(neg_a[:], neg_a[:], -1.0, None, ALU.mult))
        clear_all()

        def body(i, mamba, moe):
            mamba_steps = [("mamba_ln",), ("mamba_conv",), ("mamba_dt",)] + [("mamba_scan", n) for n in range(NS)] + [("mamba_out",)]
            moe_steps = [("moe_ln",), ("moe_route",)] + [("moe_expert", e) for e in range(E)]
            order = beside(mamba_steps if mamba else [], moe_steps if moe else [])
            with nc.Block() as block:
                @block.sync
                def _(sp):
                    if mamba:
                        sp.dma_start(xa[:], x_dram[bass.ds(i, 1)].rearrange("o p j d -> (o p) j d")).then_inc(x_loaded, 16)
                    if moe:
                        sp.wait_ge(moe_done, 1)
                        sp.dma_start(x1_dram[bass.ds(i - 1, 1)].rearrange("o p j d -> (o p) j d"), acc[:]).then_inc(x1_stored, 16)
                        sp.wait_ge(x1_stored, 16)

                @block.vector
                def _(dve):
                    cha, chb = Chain(dve, a_dve), Chain(dve, b_dve)

                    def mamba_ln():
                        cha.inc(dve.memset(xpad[:, :, 0:KC - 1], 0.0))
                        dve.wait_ge(x_loaded, 16)
                        layer_stats(cha, dve, xa, a_stats, a_mv, a_var)
                        dve.wait_ge(a_rs, 1)
                        cha.step(layer_apply(dve, ua, xa, a_mv, a_rstd))
                        layer_stats(cha, dve, ua, a_stats, a_mv, a_var)
                        dve.wait_ge(a_rs, 2)
                        layer_apply(dve, va, ua, a_mv, a_rstd).then_inc(va_ready, 1)
                        dve.wait_ge(va_turned, 1)
                        for k in range(KD):
                            last = dve.tensor_scalar(ha[:, k], pa[:, k], v("ln_mamba_g", k), v("ln_mamba_b", k),
                                                     ALU.mult, ALU.add)
                        last.then_inc(ha_ready, 1)

                    def mamba_conv():
                        for c in range(C):
                            dve.wait_ge(in_taken, c + 1)
                            cha.step(dve.tensor_scalar(y[:, c], xpad[:, c, 0:T], v("conv_w", c * KC), v("conv_b", c),
                                                       ALU.mult, ALU.add))
                            for t in range(1, KC):
                                last = dve.scalar_tensor_tensor(out=y[:, c], in0=xpad[:, c, t:t + T],
                                                                scalar=v("conv_w", c * KC + t), in1=y[:, c],
                                                                op0=ALU.mult, op1=ALU.add)
                                if t < KC - 1:
                                    cha.step(last)
                            last.then_inc(conv_ready, 1)

                    def mamba_dt():
                        n = 2 * NS
                        dve.wait_ge(bc_mm, 1)
                        cha.step(dve.tensor_copy(bc3[0:3 * n, :], pa[0:3 * n, 0]))
                        for part in range(1, 3):
                            cha.step(dve.tensor_tensor(bc_rest[n * part:n * part + n, :], pa[n * part:n * part + n, 0],
                                                       bc3[n * part:n * part + n, :], ALU.subtract))
                            last = dve.tensor_copy(bc3[n * part:n * part + n, :], bc_rest[n * part:n * part + n, :])
                            if part == 1:
                                cha.step(last)
                        cha.step(last)
                        last = dve.tensor_tensor(bc_rest[2 * n:3 * n, :], bc_rest[2 * n:3 * n, :], bc3[2 * n:3 * n, :],
                                                 ALU.subtract)
                        cha.step(last)
                        dve.tensor_copy(bc3[2 * n:3 * n, :], bc_rest[2 * n:3 * n, :]).then_inc(bc_ready, 1)
                        z = delta
                        for c in range(C):
                            dve.wait_ge(dt_mm, c + 1)
                            dve.tensor_scalar(z[:, c], pa[:, c % 2], v("dt_proj_b", c), None, ALU.add).then_inc(dt_taken, 1)
                        dve.wait_ge(dt_taken, C)
                        dve.scalar_tensor_tensor(out=soft, in0=z, scalar=-1.0, in1=z, op0=ALU.mult,
                                                 op1=ALU.min).then_inc(sp_neg, 1)
                        dve.wait_ge(sp_exp, 1)
                        dve.tensor_scalar(soft1, soft, 1.0, None, ALU.add).then_inc(sp_one, 1)
                        dve.wait_ge(sp_one, 1)
                        dve.scalar_tensor_tensor(out=soft, in0=soft1, scalar=-1.0, in1=soft, op0=ALU.add,
                                                 op1=ALU.subtract).then_inc(sp_fix, 1)
                        dve.wait_ge(sp_fix, 1)
                        dve.wait_ge(sp_inv, 1)
                        cha.step(dve.tensor_tensor(soft, soft, soft1, ALU.mult))
                        cha.step(dve.tensor_tensor(soft, dx, soft, ALU.subtract))
                        cha.step(dve.scalar_tensor_tensor(out=delta, in0=z, scalar=0.0, in1=soft, op0=ALU.max, op1=ALU.add))
                        cha.inc(dve.memset(decay[:, 1, :, 0:1], 0.0))
                        dve.tensor_tensor(dx, delta, xc, ALU.mult).then_inc(delta_ready, 1)
                        for c in range(C):
                            last = dve.tensor_scalar(y[:, c], xc[:, c], v("D_skip", c), None, ALU.mult)
                        last.then_inc(y_start, 1)

                    def mamba_scan(n):
                        s = state[:, n % 2]
                        dve.wait_ge(b_row, n + 1)
                        dve.wait_ge(y_start, 1)
                        if n >= 2:
                            dve.wait_ge(y_added, n - 1)
                        dve.tensor_tensor(s, dx, pa[:, 0:1, :].to_broadcast([P, C, T]), ALU.mult).then_inc(u_done, 1)
                        dve.wait_ge(u_done, n + 1)
                        dve.wait_ge(decay_ready, n + 1)
                        flat = s.rearrange("p c t -> p (c t)")
                        dve.tensor_tensor_scan(out=flat, data0=decay[:, n % 2].rearrange("p c t -> p (c t)"), data1=flat,
                                               initial=0.0, op0=ALU.mult, op1=ALU.add).then_inc(scan_done, 1)
                        dve.wait_ge(scan_done, n + 1)
                        dve.wait_ge(c_row, n + 1)
                        dve.tensor_tensor(s, s, pa[:, 1:2, :].to_broadcast([P, C, T]), ALU.mult).then_inc(hc_done, 1)

                    def mamba_out():
                        dve.wait_ge(y_added, NS)
                        dve.tensor_tensor(y[:], y[:], gate[:], ALU.mult).then_inc(y_gated, 1)
                        dve.wait_ge(op_mm, 1)
                        if moe:
                            dve.wait_ge(acc_ready, 1)
                        cha.step(dve.tensor_tensor(h_in[:].rearrange("p j d -> p (j d)"), ua[:].rearrange("p j d -> p (j d)"),
                                                   pa[:].rearrange("p a t -> p (a t)"), ALU.add))
                        dve.tensor_tensor(xh_in[:], h_in[:], xa[:], ALU.add).then_inc(handed, 1)

                    def moe_ln():
                        layer_stats(chb, dve, h_in, b_stats, b_mv, b_var)
                        dve.wait_ge(b_rs, 1)
                        layer_apply(dve, vb, h_in, b_mv, b_rstd).then_inc(vb_ready, 1)
                        dve.wait_ge(vb_turned, 1)
                        for k in range(KD):
                            last = dve.tensor_scalar(mt[:, k], pb[:, 4 + k], v("ln_moe_g", k), v("ln_moe_b", k),
                                                     ALU.mult, ALU.add)
                        last.then_inc(mt_ready, 1)

                    def moe_route():
                        logits = pb[:, 0, 0:J * E].rearrange("p (j e) -> p j e", e=E)
                        dve.wait_ge(logit_mm, 1)
                        chb.step(dve.tensor_reduce(r_m[:], logits, AX.X, ALU.max))
                        dve.tensor_tensor(r_p[:], logits, r_m[:].unsqueeze(2).to_broadcast([P, J, E]),
                                          ALU.subtract).then_inc(r_neg, 1)
                        dve.wait_ge(r_exp, 1)
                        chb.step(dve.tensor_reduce(r_m[:], r_p[:], AX.X, ALU.add))
                        chb.step(dve.reciprocal(r_m[:], r_m[:]))
                        chb.step(dve.tensor_tensor(r_p[:], r_p[:], r_m[:].unsqueeze(2).to_broadcast([P, J, E]), ALU.mult))
                        this = r_p[:].unsqueeze(3).to_broadcast([P, J, E, E])
                        other = r_p[:].unsqueeze(2).to_broadcast([P, J, E, E])
                        before = v("before", 0, E * E).rearrange("p (e o) -> p e o", o=E).unsqueeze(1).to_broadcast([P, J, E, E])
                        chb.inc(dve.tensor_tensor(r_gt[:], other, this, ALU.is_gt))
                        chb.step(dve.tensor_tensor(r_eq[:], other, this, ALU.is_equal))
                        chb.step(dve.tensor_tensor(r_eq[:], r_eq[:], before, ALU.mult))
                        chb.step(dve.tensor_tensor(r_gt[:], r_gt[:], r_eq[:], ALU.add))
                        chb.step(dve.tensor_reduce(r_w[:], r_gt[:], AX.X, ALU.add))
                        chb.step(dve.scalar_tensor_tensor(out=r_w[:], in0=r_w[:], scalar=1.5, in1=r_p[:], op0=ALU.is_lt, op1=ALU.mult))
                        chb.step(dve.tensor_reduce(r_m[:], r_w[:], AX.X, ALU.add))
                        chb.step(dve.reciprocal(r_m[:], r_m[:]))
                        dve.tensor_tensor(r_w[:], r_w[:], r_m[:].unsqueeze(2).to_broadcast([P, J, E]), ALU.mult).then_inc(rw_ready, 1)
                        dve.wait_ge(rwt_mm, 1)
                        dve.tensor_copy(r_wt[0:E, :], pb[0:E, 1, :]).then_inc(rwt_ready, 1)
                        dve.wait_ge(seed_mm, 1)
                        dve.tensor_tensor(acc[:].rearrange("p j d -> p (j d)"), xh_in[:].rearrange("p j d -> p (j d)"),
                                          pb[:, 2:4, :].rearrange("p a t -> p (a t)"), ALU.add).then_inc(acc_ready, 1)

                    def moe_expert(e):
                        dve.wait_ge(down_mm, e + 1)
                        if e == 0:
                            dve.wait_ge(acc_ready, 1)
                        else:
                            dve.wait_ge(ye_taken, e)
                        b = 2 + 2 * (e % 2)
                        ye = pb[:, b:b + 2, :].rearrange("p a (j d) -> p (a j) d", d=D)
                        for j in range(J):
                            last = dve.scalar_tensor_tensor(out=acc[:, j], in0=ye[:, j], scalar=r_w[:, j, e:e + 1],
                                                            in1=acc[:, j], op0=ALU.mult, op1=ALU.add)
                        last.then_inc(moe_done if e == E - 1 else ye_taken, 1)

                    run(order, mamba_ln=mamba_ln, mamba_conv=mamba_conv, mamba_dt=mamba_dt, mamba_scan=mamba_scan,
                        mamba_out=mamba_out, moe_ln=moe_ln, moe_route=moe_route, moe_expert=moe_expert)

                @block.scalar
                def _(act):
                    cha, chb = Chain(act, a_act), Chain(act, b_act)

                    def mamba_ln():
                        act.wait_ge(a_var, 1)
                        layer_rstd(cha, act, a_mv, a_rstd[:], eps[:, 0:1], a_rs)
                        act.wait_ge(a_var, 2)
                        layer_rstd(cha, act, a_mv, a_rstd[:], eps[:, 0:1], a_rs)

                    def mamba_conv():
                        for m in range(2 * C):
                            act.wait_ge(in_ready, m + 1)
                            dst = xpad[:, m, KC - 1:] if m < C else gate[:, m - C]
                            act.activation(dst, pa[:, m % 2], ACT.Identity if m < C else ACT.Silu,
                                           bias=v("in_proj_b", m)).then_inc(in_taken, 1)
                        for c in range(C):
                            act.wait_ge(conv_ready, c + 1)
                            act.activation(xc[:, c], y[:, c], ACT.Silu).then_inc(xc_ready, 1)

                    def mamba_dt():
                        act.wait_ge(dtr_mm, 1)
                        act.activation(dtr[0:DTR, :], pa[0:DTR, 1], ACT.Copy).then_inc(dtr_ready, 1)
                        act.wait_ge(sp_neg, 1)
                        act.activation(soft, soft, ACT.Exp).then_inc(sp_exp, 1)
                        act.wait_ge(sp_one, 1)
                        act.activation(dx, soft1, ACT.Ln).then_inc(sp_log, 1)
                        act.wait_ge(sp_log, 1)
                        act.wait_ge(sp_fix, 1)
                        act.activation(soft1, dx, ACT.Exp, scale=-1.0).then_inc(sp_inv, 1)

                    def mamba_scan(n):
                        act.wait_ge(delta_ready, 1)
                        if n >= 2:
                            act.wait_ge(scan_done, n - 1)
                        for c in range(C):
                            last = act.activation(decay[:, n % 2, c, 1:], delta[:, c, 1:], ACT.Exp, scale=neg_a[:, c, n:n + 1])
                        last.then_inc(decay_ready, 1)

                    def moe_ln():
                        act.wait_ge(b_var, 1)
                        layer_rstd(chb, act, b_mv, b_rstd[:], eps[:, 0:1], b_rs)

                    def moe_route():
                        act.wait_ge(r_neg, 1)
                        act.activation(r_p[:], r_p[:], ACT.Exp).then_inc(r_exp, 1)

                    def moe_expert(e):
                        if e >= 2:
                            act.wait_ge(down_mm, e - 1)
                        if e == 0:
                            act.wait_ge(vb_turned, 1)
                        for f in range(FE):
                            act.wait_ge(up_mm, e * FE + f + 1)
                            act.activation(h1[:, e % 2, f], pb[:, (e * FE + f) % 2], ACT.Silu,
                                           bias=v("b1", e * FE + f)).then_inc(h1_ready, 1)

                    run(order, mamba_ln=mamba_ln, mamba_conv=mamba_conv, mamba_dt=mamba_dt, mamba_scan=mamba_scan,
                        moe_ln=moe_ln, moe_route=moe_route, moe_expert=moe_expert)

                @block.gpsimd
                def _(pool):
                    def mamba_scan(n):
                        pool.wait_ge(hc_done, n + 1)
                        if n >= 1:
                            pool.wait_ge(y_added, n)
                        pool.tensor_tensor(y[:], y[:], state[:, n % 2], ALU.add).then_inc(y_added, 1)

                    run(order, mamba_scan=mamba_scan)

                @block.tensor
                def _(pe):
                    def mamba_ln():
                        pe.wait_ge(va_ready, 1)
                        transpose_tokens(pe, pa, va, ident[:]).then_inc(va_turned, 1)

                    def mamba_conv():
                        pe.wait_ge(ha_ready, 1)
                        for m in range(2 * C):
                            if m >= 2:
                                pe.wait_ge(in_taken, m - 1)
                            for k in range(KD):
                                last = pe.matmul(pa[:, m % 2], w_in[:, k, m * P:(m + 1) * P], ha[:, k],
                                                 start=k == 0, stop=k == KD - 1)
                            last.then_inc(in_ready, 1)

                    def mamba_dt():
                        pe.wait_ge(in_taken, 2 * C)
                        for c in range(C):
                            pe.wait_ge(xc_ready, c + 1)
                            last = pe.matmul(pa[0:6 * NS, 0], w_bc[:, c, :], xc[:, c], start=c == 0, stop=c == C - 1)
                        last.then_inc(bc_mm, 1)
                        for c in range(C):
                            last = pe.matmul(pa[0:DTR, 1], w_dtr[:, c, :], xc[:, c], start=c == 0, stop=c == C - 1)
                        last.then_inc(dtr_mm, 1)
                        pe.wait_ge(dtr_ready, 1)
                        pe.wait_ge(bc_ready, 1)
                        for c in range(C):
                            if c >= 2:
                                pe.wait_ge(dt_taken, c - 1)
                            pe.matmul(pa[:, c % 2], w_dt[0:DTR, c * P:(c + 1) * P], dtr[0:DTR, :],
                                      start=True, stop=True).then_inc(dt_mm, 1)
                        pe.wait_ge(dt_taken, C)

                    def mamba_scan(n):
                        if n >= 1:
                            pe.wait_ge(u_done, n)
                        pe.matmul(pa[:, 0], pick[0:6 * NS, n:n + 1].to_broadcast([6 * NS, P]), bc3[0:6 * NS, :],
                                  start=True, stop=True).then_inc(b_row, 1)
                        if n >= 1:
                            pe.wait_ge(hc_done, n)
                        pe.matmul(pa[:, 1], pick[0:6 * NS, NS + n:NS + n + 1].to_broadcast([6 * NS, P]), bc3[0:6 * NS, :],
                                  start=True, stop=True).then_inc(c_row, 1)

                    def mamba_out():
                        pe.wait_ge(y_gated, 1)
                        out = pa[:].rearrange("p a (j d) -> p (a j) d", d=D)
                        for j in range(J):
                            for c in range(C):
                                last = pe.matmul(out[:, j], y[:, c, j * P:(j + 1) * P], w_op[:, c, :],
                                                 start=c == 0, stop=c == C - 1)
                        last.then_inc(op_mm, 1)

                    def moe_ln():
                        pe.wait_ge(vb_ready, 1)
                        transpose_tokens(pe, pb[:, 4:6], vb, ident[:]).then_inc(vb_turned, 1)

                    def moe_route():
                        pe.wait_ge(mt_ready, 1)
                        for j in range(J):
                            for k in range(KD):
                                last = pe.matmul(pb[:, 0, j * E:(j + 1) * E], mt[:, k, j * P:(j + 1) * P], w_rt[:, k, :],
                                                 start=k == 0, stop=k == KD - 1)
                        last.then_inc(logit_mm, 1)
                        pe.wait_ge(rw_ready, 1)
                        for j in range(J):
                            last = pe.transpose(pb[0:E, 1, j * P:(j + 1) * P], r_w[:, j, :], ident[:])
                        last.then_inc(rwt_mm, 1)
                        pe.wait_ge(rwt_ready, 1)
                        out = pb[:, 2:4].rearrange("p a (j d) -> p (a j) d", d=D)
                        for j in range(J):
                            last = pe.matmul(out[:, j], r_wt[0:E, j * P:(j + 1) * P], b_2[0:E, :], start=True, stop=True)
                        last.then_inc(seed_mm, 1)

                    def up(e):
                        for f in range(FE):
                            n = e * FE + f
                            if n >= 2:
                                pe.wait_ge(h1_ready, n - 1)
                            for k in range(KD):
                                last = pe.matmul(pb[:, n % 2], w_1[:, e, k, f * P:(f + 1) * P], mt[:, k],
                                                 start=k == 0, stop=k == KD - 1)
                            last.then_inc(up_mm, 1)

                    def down(e):
                        pe.wait_ge(h1_ready, (e + 1) * FE)
                        if e == 0:
                            pe.wait_ge(acc_ready, 1)
                        if e >= 2:
                            pe.wait_ge(ye_taken, e - 1)
                        b = 2 + 2 * (e % 2)
                        out = pb[:, b:b + 2].rearrange("p a (j d) -> p (a j) d", d=D)
                        for j in range(J):
                            for f in range(FE):
                                last = pe.matmul(out[:, j], h1[:, e % 2, f, j * P:(j + 1) * P], w_2[:, e, f, :],
                                                 start=f == 0, stop=f == FE - 1)
                        last.then_inc(down_mm, 1)

                    def moe_expert(e):
                        up(e)
                        down(e)

                    run(order, mamba_ln=mamba_ln, mamba_conv=mamba_conv, mamba_dt=mamba_dt, mamba_scan=mamba_scan,
                        mamba_out=mamba_out, moe_ln=moe_ln, moe_route=moe_route, moe_expert=moe_expert)
            clear_all()

        body(0, True, False)
        if NB > 1:
            with nc.Fori(1, NB) as i:
                body(i, True, True)
        body(NB, False, True)


def attention_ffn_pass(nc, io, x1_dram):
    NB = io["x"].shape[0]
    out_dram = io["out"].rearrange("b (j p) d -> b p j d", p=P)
    with ExitStack() as ctx:
        sem_nums = []

        def sb(name, shape, dt=F32):
            return ctx.enter_context(nc.sbuf_tensor(name, [P] + shape, dt))

        def sem(name):
            s = ctx.enter_context(nc.semaphore(name))
            sem_nums.append(s.num)
            return s

        ident = sb("t_ident", [P])
        head_mask = sb("head_mask", [P // DH])
        w_gate = sb("w_gate", [KD, HID])
        w_up = sb("w_up", [KD, HID])
        w_down = sb("w_down", [FH, D])
        w_qkv = sb("w_qkv", [KD, 3 * D])
        w_out = sb("w_out", [KD, D])
        b_qkv = sb("b_qkv", [3 * D])
        b_out = sb("b_out", [D])
        eps = sb("t_eps", [1])
        norm_bias = sb("norm_bias", [1])
        acos_bias = sb("acos_bias", [1])
        xf = sb("xf", [J, D])
        f_stats = sb("f_stats", [2, J, 6]); f_mv = sb("f_mv", [2, J, 2]); f_rstd = sb("f_rstd", [2, J])
        nf = sb("nf", [KD, T])
        g_sb = sb("g_sb", [FH, T])
        vf = g_sb[:, 0:2].rearrange("p k (j d) -> p (k j) d", d=D)
        yf = sb("yf", [J, D])
        x2_next = sb("x2_next", [J, D])
        x3 = sb("x3", [J, D])
        x2 = sb("x2", [J, D])
        t_stats = sb("t_stats", [J, 6]); t_mv = sb("t_mv", [J, 2]); t_rstd = sb("t_rstd", [J])
        vt = sb("vt", [J, D])
        nt = sb("nt", [KD, T])
        qk = sb("qk", [J, 2 * D])
        val_next = sb("val_next", [J, D])
        val = sb("val", [J, D])
        ss = sb("ss", [J, 2 * H])
        qkt_next = sb("qkt_next", [2 * KD, T])
        qkt = sb("qkt", [2 * KD, T])
        k_one = sb("k_one", [2, T])
        score = sb("score", [2, HG, J, T])
        log_m = sb("log_m", [2, J, T])
        n_c2 = sb("n_c", [2, 2, J])
        v_n = sb("v_n", [HG, J, VW])
        o_t = sb("o_t", [T])
        d_n = sb("d_n", [J, HG]); d_m = sb("d_m", [J, HG])
        o_tok = sb("o_tok", [J, D])
        ot = nt
        pc = ctx.enter_context(nc.psum_tensor("pc", [P, 6, T], F32))
        pf = ctx.enter_context(nc.psum_tensor("pf", [P, 2, T], F32))

        loaded = sem("t_loaded")
        x1_loaded = sem("x1_loaded"); y_stored = sem("y_stored")
        f_dve = sem("f_dve"); f_act = sem("f_act"); f_var = sem("f_var"); f_rs = sem("f_rs")
        vf_ready = sem("vf_ready"); vf_turned = sem("vf_turned"); nf_ready = sem("nf_ready")
        gate_mm = sem("gate_mm"); gate_taken = sem("gate_taken"); up_mm = sem("upf_mm"); hid_ready = sem("hid_ready")
        silu_done = sem("silu_done"); dn_mm = sem("dn_mm"); ffn_done = sem("ffn_done")
        t_var = sem("t_var"); t_rs = sem("t_rs")
        vt_ready = sem("vt_ready"); vt_turned = sem("vt_turned"); nt_ready = sem("nt_ready")
        qkv_mm = sem("qkv_mm"); qkv_taken = sem("qkv_taken"); ss_ready = sem("ss_ready"); rn_ready = sem("rn_ready")
        qk_ready = sem("qk_ready"); qk_turned = sem("qk_turned"); qkt_taken = sem("qkt_taken")
        o_turned = sem("o_turned"); o_ready = sem("o_ready"); wo_mm = sem("wo_mm"); x3_ready = sem("x3_ready")
        x2_moved = sem("x2_moved")
        t_dve = sem("t_dve"); t_act = sem("t_act")
        qkt_ready = sem("qkt_ready"); k_ready = sem("k_ready"); s_mm = sem("s_mm"); cos_ready = sem("cos_ready")
        logm_done = sem("logm_done"); logp_done = sem("logp_done")
        diff_pool = sem("diff_pool"); diff_dve = sem("diff_dve")
        tanh_done = sem("tanh_done"); atan_done = sem("atan_done"); log1_done = sem("log1_done"); s_ready = sem("s_ready")
        v_ready = sem("v_ready"); val_ready = sem("val_ready")
        pv_mm = sem("pv_mm"); ot_ready = sem("ot_ready"); ot_turned = sem("ot_turned"); o_norm = sem("o_norm")
        sems = range(min(sem_nums), max(sem_nums) + 1)
        assert len(sems) == len(sem_nums)

        def clear_all():
            nc.sync.sem_clear(sems)
            nc.all_engine_barrier()

        with nc.Block() as block:
            plain = [(ident, "ident"), (head_mask, "head_mask"), (w_qkv, "w_qkv"), (w_out, "w_out"),
                     (b_qkv, "b_qkv"), (b_out, "b_out")]
            coded = [(w_gate, "w_gate", score[:, 0, 0:1]), (w_up, "w_up", score[:, 0, 1:2]), (w_down, "w_down", score[:, 0, 2:3])]

            @block.sync
            def _(sp):
                for dst, name in plain:
                    src = io[name]
                    if name in ("b_qkv", "b_out"):
                        src = src.partition_broadcast(P)
                    sp.dma_start(dst[:], src).then_inc(loaded, 16)
                for dst, name, room in coded:
                    flat = room.rearrange("p a j t -> p (a j t)")[:, 0:FH * D].bitcast(I32)
                    sp.dma_start(flat, io[name].rearrange("p a b -> p (a b)")).then_inc(loaded, 16)

            @block.vector
            def _(dve):
                ch = Chain(dve, t_dve)
                ch.inc(dve.memset(eps[:], LN_EPS))
                ch.inc(dve.memset(norm_bias[:], 0.5 * math.log(Q_SHIFT)))
                ch.inc(dve.memset(acos_bias[:], 1.0 + math.pi / 2))
                ch.step(dve.memset(v_n[:], 0.0))
                ch.inc(dve.memset(v_n[:, :, :, DH + 1:DH + 2], 1.0))
                dve.wait_ge(loaded, 16 * (len(plain) + len(coded)))
                for dst, name, room in coded:
                    flat = room.rearrange("p a j t -> p (a j t)")[:, 0:FH * D].bitcast(I32)
                    ch.step(dve.tensor_scalar(dst[:].rearrange("p a b -> p (a b)"), flat, 1.0 / 127.0, None, ALU.mult))
        clear_all()

        def body(i, attend, before_, after):
            last_turn = attend or before_
            ffns = (["first"] if after else []) + (["last"] if before_ else [])
            n_first, n_last = 0, len(ffns) - 1
            extra = 1 if before_ else 0
            steps = []
            heads = [(g, hh) for g in range(NG) for hh in range(HG)] if attend else []
            made = [0]

            def make(n):
                out = [("t_make", g * HG + hh) for g, hh in heads[made[0]:made[0] + n]]
                made[0] += n
                return out

            def logs(g, mix=(), skip=0):
                mix, out = list(mix), []
                if attend:
                    for hh in range(HG):
                        out += [("t_log", g * HG + hh)]
                        if hh == 1:
                            out += column_sums(g - 1, 1)
                        if hh < skip:
                            continue
                        k = -(-len(mix) // (HG - hh))
                        out += mix[:k]
                        mix = mix[k:]
                elif g == 0:
                    out += column_sums(-1, 1)
                return out + mix

            def column_sums(g, half):
                return [("t_sum", g, half)] if (attend if g >= 0 else before_) else []

            def angle(g):
                return [("t_angle", g)] if attend else []

            def weigh(g):
                return [("t_weigh", g)] + column_sums(g, 0) if (attend if g >= 0 else before_) else []

            def log1(g):
                return [("t_log1", g)] if (attend if g >= 0 else before_) else []

            def values(g):
                return [("t_values", g)] if (attend if g >= 0 else before_) else []

            last, first = before_, after
            gates = lambda n: [("ffn_gate", n, m) for m in range(FH)]
            ups = lambda n: [("ffn_up", n, m) for m in range(FH)]
            downs = lambda n, which: [("ffn_down", n, which, j) for j in range(J)]
            only = lambda asked, *names: list(names) if asked else []
            steps += only(attend, ("t_take",)) + make(2)
            steps += only(first, ("ffn_stats", n_first, "first")) + make(2)
            steps += log1(-1) + weigh(-1)
            steps += logs(0, only(first, ("ffn_ln", n_first, "first"), *gates(n_first)), skip=2)
            steps += only(attend, ("t_take_val",)) + values(-1) + only(last, ("t_out",))
            steps += angle(0) + make(HG) + only(first, ("ffn_silu", n_first), *ups(n_first))
            steps += log1(0) + weigh(0)
            steps += logs(1, only(first, *downs(n_first, "first")), skip=1)
            steps += only(first, ("t_stats",)) + only(last, ("ffn_stats", n_last, "last")) + only(first, ("t_ln",))
            steps += values(0)
            steps += angle(1) + only(first, *[("t_qkv", j) for j in range(J)], ("t_square",)) + make(HG)
            steps += log1(1) + weigh(1) + only(first, ("t_norm",))
            steps += logs(2, only(first, ("t_turn", 0), ("t_turn", 1)) + only(last, ("ffn_ln", n_last, "last"), *gates(n_last)), skip=1)
            steps += values(1)
            steps += angle(2) + make(HG) + only(last, ("ffn_silu", n_last), *ups(n_last))
            steps += log1(2) + weigh(2)
            steps += logs(3, only(last, *downs(n_last, "last")), skip=1) + values(2)
            steps += angle(3)
            order = steps

            def which_of(n):
                return ffns[n]

            def buf(g):
                return g % 2

            with nc.Block() as block:
                @block.sync
                def _(sp):
                    if after:
                        sp.dma_start(xf[:], x1_dram[bass.ds(i + 1, 1)].rearrange("o p j d -> (o p) j d")).then_inc(x1_loaded, 16)
                    if before_:
                        sp.wait_ge(ffn_done, len(ffns))
                        sp.dma_start(out_dram[bass.ds(i - 1, 1)].rearrange("o p j d -> (o p) j d"), yf[:]).then_inc(y_stored, 16)
                        sp.wait_ge(y_stored, 16)

                @block.vector
                def _(dve):
                    chf, cht = Chain(dve, f_dve), Chain(dve, t_dve)

                    def ffn_stats(n, which):
                        if which == "first":
                            dve.wait_ge(x1_loaded, 16)
                        else:
                            dve.wait_ge(x3_ready, 1)
                        layer_stats(chf, dve, xf if which == "first" else x3, f_stats[:, n], f_mv[:, n], f_var)

                    def ffn_ln(n, which):
                        x = xf if which == "first" else x3
                        dve.wait_ge(f_rs, n + 1)
                        if n:
                            dve.wait_ge(dn_mm, n * J)
                        layer_apply(dve, vf, x, f_mv[:, n], f_rstd[:, n]).then_inc(vf_ready, 1)
                        dve.wait_ge(vf_turned, n + 1)
                        dve.tensor_copy(nf[:], pf[:]).then_inc(nf_ready, 1)

                    def ffn_gate(n, m):
                        dve.wait_ge(gate_mm, n * FH + m + 1)
                        dve.tensor_copy(g_sb[:, m], pf[:, m % 2]).then_inc(gate_taken, 1)

                    def ffn_up(n, m):
                        dve.wait_ge(up_mm, n * FH + m + 1)
                        dve.wait_ge(silu_done, n + 1)
                        dve.tensor_tensor(g_sb[:, m], g_sb[:, m], pf[:, m % 2], ALU.mult).then_inc(hid_ready, 1)

                    def ffn_down(n, which, j):
                        if j % 2 == 0:
                            return
                        dve.wait_ge(dn_mm, n * J + j + 1)
                        x, dst = (xf, x2_next) if which == "first" else (x3, yf)
                        if which == "first" and attend:
                            dve.wait_ge(x2_moved, 1)
                        last = dve.tensor_tensor(dst[:, j - 1:j + 1].rearrange("p j d -> p (j d)"),
                                                 x[:, j - 1:j + 1].rearrange("p j d -> p (j d)"), pf[:, j // 2], ALU.add)
                        if j == J - 1:
                            last.then_inc(ffn_done, 1)

                    def t_take():
                        dve.tensor_copy(qkt[:], qkt_next[:]).then_inc(qkt_ready, 1)

                    def t_take_val():
                        if before_:
                            dve.wait_ge(v_ready, 2)
                        dve.tensor_copy(val[:], val_next[:]).then_inc(val_ready, 1)
                        if not before_:
                            dve.tensor_copy(x2[:], x2_next[:]).then_inc(x2_moved, 1)

                    def t_stats_():
                        dve.wait_ge(ffn_done, 1)
                        layer_stats(chf, dve, x2_next, t_stats, t_mv, t_var)

                    def t_ln():
                        dve.wait_ge(t_rs, 1)
                        layer_apply(dve, vt, x2_next, t_mv, t_rstd).then_inc(vt_ready, 1)
                        dve.wait_ge(vt_turned, 1)
                        dve.tensor_copy(nt[:], pf[:]).then_inc(nt_ready, 1)

                    def t_qkv(j):
                        dve.wait_ge(qkv_mm, j + 1)
                        dve.tensor_tensor(qk[:, j], pf[:, 0], b_qkv[:, 0:2 * D], ALU.add).then_inc(qkv_taken, 1)
                        if j == 0 and attend:
                            dve.wait_ge(val_ready, 1)
                        dve.tensor_tensor(val_next[:, j], pf[:, 1, 0:D], b_qkv[:, 2 * D:], ALU.add).then_inc(qkv_taken, 1)

                    def t_square():
                        dve.wait_ge(qkv_taken, 2 * J)
                        if attend:
                            dve.wait_ge(qkt_ready, 1)
                        sq = qkt_next[:].rearrange("p k t -> p (k t)")
                        chf.step(dve.tensor_tensor(sq, qk[:].rearrange("p j f -> p (j f)"), qk[:].rearrange("p j f -> p (j f)"), ALU.mult))
                        chf.step(dve.tensor_reduce(ss[:], sq.rearrange("p (j h d) -> p j h d", j=J, d=DH), AX.X, ALU.add))
                        dve.tensor_scalar(ss[:], ss[:], 1e-24, None, ALU.max).then_inc(ss_ready, 1)

                    def t_norm():
                        dve.wait_ge(rn_ready, 1)
                        q4 = qk[:].rearrange("p j (h d) -> p (j h) d", d=DH)
                        dve.tensor_tensor(q4, q4, ss[:].rearrange("p j h -> p (j h)").unsqueeze(2).to_broadcast([P, J * 2 * H, DH]),
                                          ALU.mult).then_inc(qk_ready, 1)

                    def t_turn(k):
                        dve.wait_ge(qk_turned, k + 1)
                        dve.tensor_copy(qkt_next[:, 2 * k:2 * k + 2], pf[:]).then_inc(qkt_taken, 1)

                    def mask_keys(h):
                        if h >= 2:
                            dve.wait_ge(s_mm, 2 * (h - 1))
                        m = h % (P // DH)
                        dve.tensor_scalar(k_one[:, h % 2], qkt[:, KD + h // (P // DH)], head_mask[:, m:m + 1], None,
                                          ALU.mult).then_inc(k_ready, 1)

                    def t_make(h):
                        g = h // HG
                        if h == 0:
                            dve.wait_ge(qkt_ready, 1)
                            mask_keys(0)
                        if h + 1 < H:
                            mask_keys(h + 1)
                        if h % HG == 0 and g + extra >= 2:
                            dve.wait_ge(pv_mm, g + extra - 1)
                        for s in range(2):
                            dve.wait_ge(s_mm, 2 * h + s + 1)
                            dve.tensor_scalar(score[:, buf(g), h % HG, 2 * s:2 * s + 2], pc[:, 2 * s:2 * s + 2], -1.0 + 1e-7,
                                              1.0 - 1e-7, ALU.max, ALU.min).then_inc(cos_ready, 1)

                    def t_log(h):
                        if h % 2:
                            s = score[:, buf(h // HG), h % HG]
                            dve.wait_ge(logp_done, h + 1)
                            dve.tensor_tensor(s, s, log_m[:, h % 2], ALU.subtract).then_inc(diff_dve, 1)

                    def t_sum(g, half):
                        k = g + extra
                        h = (g % NG) * HG + 2 * half
                        n_c = n_c2[:, half]
                        if k >= 1:
                            dve.wait_ge(v_ready, 2 * k)
                        dve.wait_ge(s_ready, 2 * k + half + 1)
                        s = score[:, buf(g), 2 * half:2 * half + 2]
                        cht.step(dve.tensor_reduce(n_c, s, AX.X, ALU.add))
                        cht.step(dve.reciprocal(n_c, n_c))
                        if half == 0 and k >= 1:
                            dve.wait_ge(pv_mm, k)
                        if g == 0:
                            dve.wait_ge(val_ready, 1)
                        cht.inc(dve.tensor_tensor(v_n[:, 2 * half:2 * half + 2, :, 0:DH],
                                                  val[:, :, h * DH:(h + 2) * DH].rearrange("p j (h d) -> p h j d", d=DH),
                                                  n_c.unsqueeze(3).to_broadcast([P, 2, J, DH]), ALU.mult))
                        dve.tensor_copy(v_n[:, 2 * half:2 * half + 2, :, DH:DH + 1], n_c.unsqueeze(3)).then_inc(v_ready, 1)

                    def t_values(g):
                        k = g + extra
                        dve.wait_ge(pv_mm, k + 1)
                        if k >= 1:
                            dve.wait_ge(ot_turned, k)
                        dve.tensor_copy(o_t[:], pc[:, 4]).then_inc(ot_ready, 1)
                        dve.wait_ge(ot_turned, k + 1)
                        o = pc[:, 5].rearrange("p (j h w) -> p j h w", h=HG, w=P // HG)
                        cht.step(dve.reciprocal(d_n[:], o[:, :, :, DH + 1]))
                        cht.step(dve.tensor_tensor(d_m[:], d_n[:], o[:, :, :, DH], ALU.mult))
                        cht.step(dve.tensor_scalar(d_m[:], d_m[:], 1e-12, None, ALU.max))
                        cht.step(dve.reciprocal(d_m[:], d_m[:]))
                        cht.step(dve.tensor_tensor(d_m[:], d_m[:], d_n[:], ALU.mult))
                        if g == 0 and before_:
                            dve.wait_ge(o_turned, 1)
                        a = (g % NG) * HG * DH
                        dst = o_tok[:, :, a:a + HG * DH].rearrange("p j (h d) -> p j h d", d=DH)
                        dve.tensor_tensor(dst, o[:, :, :, 0:DH], d_m[:].unsqueeze(3).to_broadcast([P, J, HG, DH]),
                                          ALU.mult).then_inc(o_norm, 1)

                    def t_out():
                        dve.wait_ge(o_turned, 1)
                        chf.inc(dve.tensor_tensor(x2[:], x2[:], b_out[:].unsqueeze(1).to_broadcast([P, J, D]), ALU.add))
                        dve.tensor_copy(nt[:], pf[:]).then_inc(o_ready, 1)
                        dve.wait_ge(wo_mm, 1)
                        chf.sync()
                        dve.tensor_tensor(x3[:].rearrange("p j d -> p (j d)"), x2[:].rearrange("p j d -> p (j d)"),
                                          pf[:].rearrange("p a t -> p (a t)"), ALU.add).then_inc(x3_ready, 1)
                        if attend:
                            dve.wait_ge(x3_ready, 1)
                            dve.tensor_copy(x2[:], x2_next[:]).then_inc(x2_moved, 1)

                    run(order, ffn_stats=ffn_stats, t_stats=t_stats_, t_square=t_square, ffn_ln=ffn_ln, ffn_gate=ffn_gate, ffn_up=ffn_up,
                        ffn_down=ffn_down, t_take=t_take,
                        t_take_val=t_take_val, t_ln=t_ln,
                        t_qkv=t_qkv, t_norm=t_norm, t_turn=t_turn, t_make=t_make, t_log=t_log, t_sum=t_sum,
                        t_values=t_values, t_out=t_out)

                @block.scalar
                def _(act):
                    chf, cht = Chain(act, f_act), Chain(act, t_act)

                    def ffn_ln(n, which):
                        act.wait_ge(f_var, n + 1)
                        layer_rstd(chf, act, f_mv[:, n], f_rstd[:, n], eps[:, 0:1], f_rs)

                    def ffn_silu(n):
                        act.wait_ge(gate_taken, (n + 1) * FH)
                        act.activation(g_sb[:], g_sb[:], ACT.Silu).then_inc(silu_done, 1)

                    def t_ln():
                        act.wait_ge(t_var, 1)
                        layer_rstd(chf, act, t_mv, t_rstd[:], eps[:, 0:1], t_rs)

                    def t_norm():
                        act.wait_ge(ss_ready, 1)
                        chf.step(act.activation(ss[:], ss[:], ACT.Ln, scale=Q_SHIFT))
                        act.activation(ss[:], ss[:], ACT.Exp, scale=-0.5, bias=norm_bias[:, 0:1]).then_inc(rn_ready, 1)

                    def t_log(h):
                        s = score[:, buf(h // HG), h % HG]
                        act.wait_ge(cos_ready, 2 * (h + 1))
                        if h >= 2:
                            act.wait_ge(diff_dve if h % 2 else diff_pool, h // 2)
                        act.activation(log_m[:, h % 2], s, ACT.Ln, scale=-1.0, bias=1.0).then_inc(logm_done, 1)
                        act.wait_ge(logm_done, h + 1)
                        act.activation(s, s, ACT.Ln, bias=1.0).then_inc(logp_done, 1)

                    def t_angle(g):
                        pairs = [score[:, buf(g), 0:2], score[:, buf(g), 2:4]]
                        for half, s in enumerate(pairs):
                            act.wait_ge(diff_pool, 2 * g + half + 1)
                            act.wait_ge(diff_dve, 2 * g + half + 1)
                            act.activation(s, s, ACT.Tanh, scale=0.25).then_inc(tanh_done, 1)
                        for half, s in enumerate(pairs):
                            act.wait_ge(tanh_done, 2 * g + half + 1)
                            act.activation(s, s, ACT.Arctan).then_inc(atan_done, 1)

                    def t_log1(g):
                        pairs = [score[:, buf(g), 0:2], score[:, buf(g), 2:4]]
                        for half, s in enumerate(pairs):
                            if g >= 0:
                                act.wait_ge(atan_done, 2 * g + half + 1)
                            act.activation(s, s, ACT.Ln, scale=-2.0, bias=acos_bias[:, 0:1]).then_inc(log1_done, 1)

                    def t_weigh(g):
                        k = g + extra
                        pairs = [score[:, buf(g), 0:2], score[:, buf(g), 2:4]]
                        for half, s in enumerate(pairs):
                            act.wait_ge(log1_done, 2 * k + half + 1)
                            act.activation(s, s, ACT.Exp, scale=-3.2).then_inc(s_ready, 1)

                    run(order, ffn_ln=ffn_ln, ffn_silu=ffn_silu, t_ln=t_ln, t_norm=t_norm, t_log=t_log, t_angle=t_angle,
                        t_log1=t_log1, t_weigh=t_weigh)

                @block.gpsimd
                def _(pool):
                    def t_log(h):
                        if h % 2 == 0:
                            s = score[:, buf(h // HG), h % HG]
                            pool.wait_ge(logp_done, h + 1)
                            pool.tensor_tensor(s, s, log_m[:, h % 2], ALU.subtract).then_inc(diff_pool, 1)

                    run(order, t_log=t_log)

                @block.tensor
                def _(pe):
                    def ffn_ln(n, which):
                        pe.wait_ge(vf_ready, n + 1)
                        if n:
                            pe.wait_ge(qkt_taken, 2)
                        transpose_tokens(pe, pf, vf, ident[:]).then_inc(vf_turned, 1)

                    def ffn_gate(n, m):
                        if m == 0:
                            pe.wait_ge(nf_ready, n + 1)
                        if m >= 2:
                            pe.wait_ge(gate_taken, n * FH + m - 1)
                        for k in range(KD):
                            last = pe.matmul(pf[:, m % 2], w_gate[:, k, m * P:(m + 1) * P], nf[:, k], start=k == 0, stop=k == KD - 1)
                        last.then_inc(gate_mm, 1)

                    def ffn_up(n, m):
                        if m == 0 and before_ and which_of(n) == "first":
                            pe.wait_ge(x3_ready, 1)
                        if m < 2:
                            pe.wait_ge(gate_taken, n * FH + FH - 1 + m)
                        else:
                            pe.wait_ge(hid_ready, n * FH + m - 1)
                        for k in range(KD):
                            last = pe.matmul(pf[:, m % 2], w_up[:, k, m * P:(m + 1) * P], nf[:, k], start=k == 0, stop=k == KD - 1)
                        last.then_inc(up_mm, 1)

                    def ffn_down(n, which, j):
                        pe.wait_ge(hid_ready, (n + 1) * FH)
                        for m in range(FH):
                            last = pe.matmul(pf[:, j // 2, (j % 2) * D:(j % 2 + 1) * D], g_sb[:, m, j * P:(j + 1) * P],
                                             w_down[:, m, :], start=m == 0, stop=m == FH - 1)
                        last.then_inc(dn_mm, 1)

                    def t_ln():
                        pe.wait_ge(vt_ready, 1)
                        pe.wait_ge(ffn_done, 1)
                        transpose_tokens(pe, pf, vt, ident[:]).then_inc(vt_turned, 1)

                    def t_qkv(j):
                        if j == 0:
                            pe.wait_ge(nt_ready, 1)
                        else:
                            pe.wait_ge(qkv_taken, 2 * j)
                        for k in range(KD):
                            pe.matmul(pf[:, 0], nt[:, k, j * P:(j + 1) * P], w_qkv[:, k, 0:2 * D], start=k == 0, stop=k == KD - 1)
                        for k in range(KD):
                            last = pe.matmul(pf[:, 1, 0:D], nt[:, k, j * P:(j + 1) * P], w_qkv[:, k, 2 * D:],
                                             start=k == 0, stop=k == KD - 1)
                        last.then_inc(qkv_mm, 1)

                    def t_turn(k):
                        pe.wait_ge(qk_ready, 1)
                        if k:
                            pe.wait_ge(qkt_taken, k)
                        for c in range(2):
                            a = (2 * k + c) * P
                            for j in range(J):
                                last = pe.transpose(pf[:, c, j * P:(j + 1) * P], qk[:, j, a:a + P], ident[:])
                        last.then_inc(qk_turned, 1)

                    def t_make(h):
                        pe.wait_ge(k_ready, h + 1)
                        for s in range(2):
                            if h:
                                pe.wait_ge(cos_ready, 2 * (h - 1) + s + 1)
                            for c in range(2):
                                t = 2 * s + c
                                last = pe.matmul(pc[:, t], k_one[:, h % 2, t * P:(t + 1) * P], qkt[:, h // (P // DH)],
                                                 start=True, stop=True)
                            last.then_inc(s_mm, 1)

                    def t_values(g):
                        k = g + extra
                        pe.wait_ge(v_ready, 2 * (k + 1))
                        if k >= 1:
                            pe.wait_ge(ot_ready, k)
                        for t in range(J):
                            for hh in range(HG):
                                a = hh * VW
                                last = pe.matmul(pc[a:a + VW, 4], v_n[:, hh, t, :], score[:, buf(g), hh, t], start=t == 0,
                                                 stop=t == J - 1)
                        last.then_inc(pv_mm, 1)
                        pe.wait_ge(ot_ready, k + 1)
                        if k >= 1:
                            pe.wait_ge(o_norm, k)
                        for j in range(J):
                            last = pe.transpose(pc[:, 5, j * P:(j + 1) * P], o_t[:, j * P:(j + 1) * P], ident[:])
                        last.then_inc(ot_turned, 1)

                    def t_out():
                        pe.wait_ge(o_norm, 1)
                        if after:
                            pe.wait_ge(gate_taken, FH)
                        transpose_tokens(pe, pf, o_tok, ident[:]).then_inc(o_turned, 1)
                        pe.wait_ge(o_ready, 1)
                        for j in range(J):
                            for k in range(KD):
                                last = pe.matmul(pf[:, j // 2, (j % 2) * D:(j % 2 + 1) * D], nt[:, k, j * P:(j + 1) * P],
                                                 w_out[:, k, :], start=k == 0, stop=k == KD - 1)
                        last.then_inc(wo_mm, 1)

                    run(order, ffn_ln=ffn_ln, ffn_gate=ffn_gate, ffn_up=ffn_up, ffn_down=ffn_down, t_ln=t_ln, t_qkv=t_qkv,
                        t_turn=t_turn, t_make=t_make, t_values=t_values, t_out=t_out)
            clear_all()

        body(-1, False, False, True)
        body(0, True, False, NB > 1)
        if NB > 2:
            with nc.Fori(1, NB - 1) as i:
                body(i, True, True, True)
        if NB > 1:
            body(NB - 1, True, True, False)
        body(NB, False, True, False)


def program(nc, io):
    x1_dram = nc.dram_tensor("x1_rows", (io["x"].shape[0], P, J, D), F32, kind="Internal").ap()
    mamba_moe_pass(nc, io, x1_dram)
    attention_ffn_pass(nc, io, x1_dram)


def kernel(**inputs):
    import numpy as np
    import concourse.bacc as bacc
    from concourse import mybir as my
    from concourse.bass_utils import run_bass_kernel_spmd

    a = {k.replace("L0_attn_a_", "").replace("L0_ffn_", "").replace("L0_attn_b_", "t_"): np.asarray(x)
         for k, x in inputs.items()}
    rows = lambda w: np.ascontiguousarray(w.reshape(-1, P, w.shape[-1]).transpose(1, 0, 2))
    cols = lambda w: w.reshape(-1, P).T
    x_proj = a["x_proj_w"].T
    before = np.tril(np.ones((E, E), np.float32), -1).reshape(1, -1).repeat(P, 0)
    head_mask = np.kron(np.eye(P // DH, dtype=np.float32), np.ones((DH, 1), np.float32))
    vectors = {
        "ln_mamba_g": cols(a["ln_mamba_g"]), "ln_mamba_b": cols(a["ln_mamba_b"]), "ln_moe_g": cols(a["ln_moe_g"]),
        "ln_moe_b": cols(a["ln_moe_b"]), "in_proj_b": cols(a["in_proj_b"]),
        "conv_w": rows(a["conv_w"]).reshape(P, -1), "conv_b": cols(a["conv_b"]), "dt_proj_b": cols(a["dt_proj_b"]),
        "A_log": rows(a["A_log"]).reshape(P, -1), "D_skip": cols(a["D_skip"]),
        "b1": cols(a["b1"]), "head_mask": head_mask, "before": before,
    }
    arrays = {
        "x": a["x"],
        "vectors": np.concatenate([vectors[n] for n in VEC], axis=1),
        "ident": np.eye(P, dtype=np.float32),
        "pick": np.tile(np.eye(2 * NS, dtype=np.float32), (3, 1)).astype(my.dt.np(BF16)),
        "head_mask": head_mask,
        "w_in": rows(a["in_proj_w"].T),
        "w_bc": rows(np.tile(x_proj[:, DTR:], (1, 3))),
        "w_dtr": rows(x_proj[:, :DTR]),
        "w_dt": a["dt_proj_w"].T,
        "w_op": rows(a["out_proj_w"].T),
        "w_rt": rows(a["router_w"].T),
        "w_1": a["w1"].transpose(2, 0, 1).reshape(KD, P, E, DFF).transpose(1, 2, 0, 3),
        "w_2": a["w2"].transpose(2, 0, 1).reshape(FE, P, E, D).transpose(1, 2, 0, 3),
        "b2": a["b2"],
        "w_gate": rows(a["w_gate"].T), "w_up": rows(a["w_up"].T), "w_down": rows(a["w_down"].T),
        "w_qkv": rows(a["t_w_qkv"].T), "w_out": rows(a["t_w_out"].T), "b_qkv": a["t_b_qkv"], "b_out": a["t_b_out"],
    }
    arrays = {n: np.ascontiguousarray(x) for n, x in arrays.items()}
    nc = bacc.Bacc("TRN2", target_bir_lowering=False, num_devices=1)
    io = {n: nc.dram_tensor(f"in_{n}", x.shape, my.dt.from_np(x.dtype), kind="ExternalInput").ap() for n, x in arrays.items()}
    io["out"] = nc.dram_tensor("out_0", arrays["x"].shape, F32, kind="ExternalOutput").ap()
    program(nc, io)
    r = run_bass_kernel_spmd(nc, [{f"in_{n}": x for n, x in arrays.items()}], core_ids=[0])
    return r.results[0]["out_0"]
```

```python
import math
from contextlib import ExitStack

import concourse.bass as bass
from concourse import mybir

F32 = mybir.dt.float32
BF16 = mybir.dt.bfloat16
I32 = mybir.dt.int32
ACT = mybir.ActivationFunctionType
ALU = mybir.AluOpType
AX = mybir.AxisListType

P = 128
D = 256
T = 512
J = T // P
KD = D // P
DI = 2 * D
C = DI // P
NS = 16
DTR = D // 16
KC = 4
E = 8
DFF = 2 * D
FE = DFF // P
HID = 768
FH = HID // P
H = 16
DH = D // H
HG = 4
NG = H // HG
VW = P // HG
LN_EPS = 1e-5
Q_SHIFT = 2.0 ** 30

VEC = {}
_at = 0
for _name, _n in (("ln_mamba_g", KD), ("ln_mamba_b", KD), ("ln_moe_g", KD), ("ln_moe_b", KD),
                  ("in_proj_b", 2 * C), ("conv_w", C * KC), ("conv_b", C), ("dt_proj_b", C),
                  ("A_log", C * NS), ("D_skip", C), ("b1", E * FE), ("head_mask", P // DH),
                  ("before", E * E)):
    VEC[_name] = (_at, _at + _n)
    _at += _n
VEC_N = _at


class Chain:

    def __init__(self, eng, sem):
        self.eng, self.sem, self.n = eng, sem, 0

    def inc(self, ins):
        ins.then_inc(self.sem, 1)
        self.n += 1

    def sync(self):
        self.eng.wait_ge(self.sem, self.n)

    def step(self, ins):
        self.inc(ins)
        self.sync()


def layer_stats(ch, dve, x, stats, mv, var_ready):
    for j in range(J):
        ch.inc(dve.bn_stats(stats[:, j, :], x[:, j, :]))
    ch.sync()
    for j in range(J):
        last = dve.bn_aggr(mv[:, j, :], stats[:, j, :])
    last.then_inc(var_ready, 1)


def layer_rstd(ch, act, mv, rstd, eps, rstd_ready):
    ch.step(act.activation(rstd, mv[:, :, 1], ACT.Ln, bias=eps))
    act.activation(rstd, rstd, ACT.Exp, scale=-0.5).then_inc(rstd_ready, 1)


def layer_apply(dve, out, x, mv, rstd):
    for j in range(J):
        last = dve.tensor_scalar(out[:, j, :], x[:, j, :], mv[:, j, 0:1], rstd[:, j:j + 1],
                                 ALU.subtract, ALU.mult)
    return last


def transpose_tokens(pe, out, x, ident):
    for k in range(KD):
        for j in range(J):
            last = pe.transpose(out[:, k, j * P:(j + 1) * P], x[:, j, k * P:(k + 1) * P], ident)
    return last


def run(order, **parts):
    for name, *args in order:
        if name in parts:
            parts[name](*args)


def beside(a, b):
    n = [(i / max(len(a), 1), 0, s) for i, s in enumerate(a)] + [(i / max(len(b), 1), 1, s) for i, s in enumerate(b)]
    return [s for _, _, s in sorted(n, key=lambda x: x[:2])]


def mamba_moe_pass(nc, io, x1_dram):
    NB = io["x"].shape[0]
    x_dram = io["x"].rearrange("b (j p) d -> b p j d", p=P)
    with ExitStack() as ctx:
        first_sem = []

        def sb(name, shape, dt=F32):
            return ctx.enter_context(nc.sbuf_tensor(name, [P] + shape, dt))

        def sem(name):
            s = ctx.enter_context(nc.semaphore(name))
            first_sem.append(s.num)
            return s

        vec = sb("m_vec", [VEC_N])
        ident = sb("m_ident", [P])
        pick = sb("m_pick", [2 * NS], BF16)
        w_in = sb("w_in", [KD, 2 * DI])
        w_x = sb("w_x", [C, 6 * NS + DTR])
        w_dt = sb("w_dt", [DI])
        w_op = sb("w_op", [C, D])
        w_rt = sb("w_rt", [KD, E])
        w_1 = sb("w_1", [E, KD, DFF])
        w_2 = sb("w_2", [E, FE, D])
        b_2 = sb("b_2", [D])
        neg_a = sb("neg_a", [C, NS])
        eps = sb("m_eps", [1])
        xa = sb("xa", [J, D])
        ua = sb("ua", [J, D])
        a_stats = sb("a_stats", [J, 6])
        a_mv = sb("a_mv", [J, 2])
        a_rstd = sb("a_rstd", [J])
        gate = sb("gate", [C, T])
        both = sb("delta_dx", [2, C, T])
        delta, dx = both[:, 0], both[:, 1]
        y = sb("y", [C, T])
        decay = sb("decay", [2, C, T])
        state = sb("state", [2, C, T])
        bc3 = sb("bc3", [T], BF16)
        bc_rest = sb("bc_rest", [T])
        dtr = sb("dtr", [T])
        xpad = both[:].rearrange("p a c t -> p (a c t)")[:, 0:C * (T + KC - 1)].rearrange("p (c t) -> p c t", c=C)
        va, ha = decay[:, 1, 0:2, :].rearrange("p c (j d) -> p (c j) d", d=D), decay[:, 0, 2:4, :]
        soft, soft1 = state[:, 0], decay[:, 1]
        xc = state[:, 1]
        h_in = sb("h_in", [J, D])
        xh_in = sb("xh_in", [J, D])
        acc = sb("acc", [J, D])
        b_stats = sb("b_stats", [J, 6])
        b_mv = sb("b_mv", [J, 2])
        b_rstd = sb("b_rstd", [J])
        mt = sb("mt", [KD, T])
        h1 = sb("h1", [2, FE, T])
        vb = h1[:, 0, 0:2, :].rearrange("p c (j d) -> p (c j) d", d=D)
        r_p = sb("r_p", [J, E])
        r_m = sb("r_m", [J])
        r_gt = sb("r_gt", [J, E, E])
        r_eq = sb("r_eq", [J, E, E])
        r_w = sb("r_w", [J, E])
        r_wt = sb("r_wt", [T])

        pa = ctx.enter_context(nc.psum_tensor("pa", [P, 2, T], F32))
        pb = ctx.enter_context(nc.psum_tensor("pb", [P, 6, T], F32))

        def v(name, i=0, n=None):
            a, b = VEC[name]
            return vec[:, a + i:a + i + (n or 1)]

        def half(hf):
            return slice(hf * C // 2, (hf + 1) * C // 2)

        loaded = sem("m_loaded")
        setup = sem("m_setup")
        x_loaded = sem("x_loaded")
        a_dve = sem("a_dve"); a_act = sem("a_act")
        a_var = sem("a_var"); a_rs = sem("a_rs"); va_ready = sem("va_ready")
        va_turned = sem("va_turned"); ha_ready = sem("ha_ready")
        in_ready = sem("in_ready"); in_taken = sem("in_taken")
        gate_ready = sem("gate_ready"); gate_taken = sem("gate_taken")
        conv_ready = sem("conv_ready"); xc_ready = sem("xc_ready"); skip_ready = sem("skip_ready")
        bc_mm = sem("bc_mm"); bc_ready = sem("bc_ready"); dtr_ready = sem("dtr_ready")
        dt_mm = sem("dt_mm"); dt_taken = sem("dt_taken")
        sp_e = sem("sp_e"); sp_one = sem("sp_one"); sp_ln = sem("sp_ln"); sp_fix = sem("sp_fix"); sp_rec = sem("sp_rec")
        delta_ready = sem("delta_ready"); dx_ready = sem("dx_ready"); decay_zero = sem("decay_zero")
        b_row_ready = sem("b_row_ready"); c_row_ready = sem("c_row_ready"); decay_ready = sem("decay_ready")
        u_done = sem("u_done"); scan_done = sem("scan_done"); weighed = sem("weighed"); y_added = sem("y_added")
        y_gated = sem("y_gated"); op_mm = sem("op_mm"); handed = sem("handed")
        b_dve = sem("b_dve"); b_act = sem("b_act")
        b_var = sem("b_var"); b_rs = sem("b_rs"); vb_ready = sem("vb_ready")
        vb_turned = sem("vb_turned"); mt_ready = sem("mt_ready")
        logit_mm = sem("logit_mm"); r_neg = sem("r_neg"); r_exp = sem("r_exp"); rw_ready = sem("rw_ready")
        rwt_mm = sem("rwt_mm"); rwt_ready = sem("rwt_ready"); seed_mm = sem("seed_mm"); acc_ready = sem("acc_ready")
        up_mm = sem("up_mm"); h1_ready = sem("h1_ready"); down_mm = sem("down_mm"); mixed = sem("mixed")
        x1_stored = sem("x1_stored")
        sems = range(min(first_sem), max(first_sem) + 1)
        assert len(sems) == len(first_sem)

        def clear_all():
            nc.sync.sem_clear(sems)
            nc.all_engine_barrier()

        with nc.Block() as block:
            loads = [(vec, "vectors"), (ident, "ident"), (w_in, "w_in"), (w_x, "w_x"),
                     (w_op, "w_op"), (w_rt, "w_rt"), (w_1, "w_1"), (w_2, "w_2")]

            @block.sync
            def _(sp):
                for dst, name in loads:
                    sp.dma_start(dst[:], io[name]).then_inc(loaded, 16)
                sp.dma_start(w_dt[0:DTR, :], io["w_dt"]).then_inc(loaded, 16)
                sp.dma_start(b_2[0:E, :], io["b2"]).then_inc(loaded, 16)
                sp.dma_start(pick[0:6 * NS, :], io["pick"]).then_inc(loaded, 16)

            @block.scalar
            def _(act):
                act.wait_ge(loaded, 16 * (len(loads) + 3))
                act.activation(neg_a[:].rearrange("p c n -> p (c n)"), v("A_log", 0, C * NS), ACT.Exp).then_inc(setup, 1)

            @block.vector
            def _(dve):
                ch = Chain(dve, a_dve)
                ch.inc(dve.memset(eps[:], LN_EPS))
                ch.inc(dve.memset(decay[:], 0.0))
                dve.wait_ge(setup, 1)
                ch.step(dve.tensor_scalar(neg_a[:], neg_a[:], -1.0, None, ALU.mult))
        clear_all()

        def steps(mamba, moe):
            s = [("h_stats",), ("x_stats",), ("rstd",), ("u_stats",), ("h_norm",), ("u_norm",), ("logit_mm",), ("ln_turn",),
                 ("in_x", 0), ("logits",), ("in_x", 1), ("conv", 0), ("in_x", 2), ("conv", 1), ("in_x", 3), ("conv", 2),
                 ("gate_mm", 0), ("conv_silu", 0), ("gate_silu", 0), ("gate_mm", 1), ("conv", 3), ("conv_silu", 1),
                 ("gate_silu", 1), ("conv_silu", 2), ("conv_silu", 3), ("rank",), ("x_proj",), ("skip",), ("dt_proj",),
                 ("route_turn",), ("gate_mm", 2), ("gate_mm", 3),
                 ("sp_exp", 0), ("sp_exp", 1), ("sp_log", 0), ("sp_log", 1), ("seed",), ("up", 0, 0), ("up", 0, 1),
                 ("up", 0, 2), ("up", 0, 3), ("sp_inv", 0), ("sp_inv", 1), ("gate_silu", 2), ("gate_silu", 3), ("b_row", 0), ("c_row", 0),
                 ("silu", 0), ("decay", 0)]
            s += [("down", 0, j) for j in range(J)] + [("u", 0), ("up", 1, 0), ("b_row", 1)]
            s += [("up", 1, f) for f in range(1, FE)] + [("decay", 1), ("silu", 1)]
            for n in range(NS):
                e, odd = n // 2, n % 2
                if not odd and n:
                    s.append(("decay", n + 1))
                if n:
                    s += [("u", n), ("c_row", n), ("up", e + 2, 2 * odd), ("b_row", n + 1), ("up", e + 2, 2 * odd + 1)]
                else:
                    s += [("up", 2, 0), ("up", 2, 1)]
                s += [("mix", 0, 0), ("mix", 0, 1)] if n == 0 else []
                s.append(("scan", n))
                s += [("mix", (n - 1) // 2 + 1, (n - 1) % 2)] if n else []
                if not odd:
                    s.append(("decay", n + 2))
                s += [("weigh", n), ("down", e + 1, 2 * odd), ("down", e + 1, 2 * odd + 1)]
                if odd:
                    s.append(("silu", e + 2))
            s.append(("out",))
            of_moe = ("h_stats", "h_norm", "logit_mm", "logits", "rank", "route_turn", "seed", "up", "silu", "down", "mix")
            within = lambda x: len(x) == 1 or x[1] < (E if x[0] in of_moe else NS)
            asked = lambda x: moe if x[0] in of_moe else mamba or x[0] == "rstd"
            return [x for x in s if asked(x) and within(x)]

        def body(i, mamba, moe):
            order = steps(mamba, moe)
            N = 2 * NS

            def gate_bank(c):
                return pb[:, c] if c < 2 else pa[:, 3 - c]
            with nc.Block() as block:
                @block.sync
                def _(sp):
                    if mamba:
                        sp.dma_start(xa[:], x_dram[bass.ds(i, 1)].rearrange("o p j d -> (o p) j d")).then_inc(x_loaded, 16)
                    if moe:
                        sp.wait_ge(mixed, 2 * E)
                        sp.dma_start(x1_dram[bass.ds(i - 1, 1)].rearrange("o p j d -> (o p) j d"), acc[:]).then_inc(x1_stored, 16)
                        sp.wait_ge(x1_stored, 16)

                @block.vector
                def _(dve):
                    cha, chb = Chain(dve, a_dve), Chain(dve, b_dve)

                    def h_stats():
                        layer_stats(chb, dve, h_in, b_stats, b_mv, b_var)

                    def x_stats():
                        cha.inc(dve.memset(xpad[:, :, 0:KC - 1], 0.0))
                        dve.wait_ge(x_loaded, 16)
                        layer_stats(cha, dve, xa, a_stats, a_mv, a_var)

                    def h_norm():
                        dve.wait_ge(b_rs, 1)
                        layer_apply(dve, vb, h_in, b_mv, b_rstd).then_inc(vb_ready, 1)

                    def u_stats():
                        dve.wait_ge(a_rs, 1)
                        cha.step(layer_apply(dve, ua, xa, a_mv, a_rstd))
                        layer_stats(cha, dve, ua, a_stats, a_mv, a_var)

                    def u_norm():
                        dve.wait_ge(a_rs, 2)
                        layer_apply(dve, va, ua, a_mv, a_rstd).then_inc(va_ready, 1)

                    def ln_turn():
                        dve.wait_ge(va_turned, 1)
                        for k in range(KD):
                            last = dve.tensor_scalar(ha[:, k], pa[:, k], v("ln_mamba_g", k), v("ln_mamba_b", k),
                                                     ALU.mult, ALU.add)
                        last.then_inc(ha_ready, 1)

                    def conv(c):
                        dve.wait_ge(in_taken, c + 1)
                        cha.step(dve.tensor_scalar(y[:, c], xpad[:, c, 0:T], v("conv_w", c * KC), v("conv_b", c),
                                                   ALU.mult, ALU.add))
                        for t in range(1, KC):
                            last = dve.scalar_tensor_tensor(out=y[:, c], in0=xpad[:, c, t:t + T],
                                                            scalar=v("conv_w", c * KC + t), in1=y[:, c],
                                                            op0=ALU.mult, op1=ALU.add)
                            if t < KC - 1:
                                cha.step(last)
                        last.then_inc(conv_ready, 1)

                    def x_proj():
                        dve.wait_ge(bc_mm, 1)
                        dve.wait_ge(dtr_ready, 1)
                        cha.step(dve.tensor_copy(bc3[0:3 * N, :], pa[0:3 * N, 0]))
                        for part in range(1, 3):
                            cha.step(dve.tensor_tensor(bc_rest[N * part:N * part + N, :], pa[N * part:N * part + N, 0],
                                                       bc3[N * part:N * part + N, :], ALU.subtract))
                            last = dve.tensor_copy(bc3[N * part:N * part + N, :], bc_rest[N * part:N * part + N, :])
                            if part == 1:
                                cha.step(last)
                        cha.step(last)
                        cha.step(dve.tensor_tensor(bc_rest[2 * N:3 * N, :], bc_rest[2 * N:3 * N, :], bc3[2 * N:3 * N, :],
                                                   ALU.subtract))
                        dve.tensor_copy(bc3[2 * N:3 * N, :], bc_rest[2 * N:3 * N, :]).then_inc(bc_ready, 1)

                    def sp_exp(hf):
                        dve.wait_ge(sp_e, hf + 1)
                        dve.tensor_scalar(soft1[:, half(hf)], soft[:, half(hf)], 1.0, None, ALU.add).then_inc(sp_one, 1)

                    def sp_log(hf):
                        dve.wait_ge(sp_one, hf + 1)
                        dve.scalar_tensor_tensor(out=soft[:, half(hf)], in0=soft1[:, half(hf)], scalar=-1.0,
                                                 in1=soft[:, half(hf)], op0=ALU.add, op1=ALU.subtract).then_inc(sp_fix, 1)

                    def sp_inv(hf):
                        a = half(hf)
                        if hf == 0:
                            dve.wait_ge(sp_fix, 2)
                        dve.wait_ge(sp_rec, hf + 1)
                        cha.step(dve.tensor_tensor(soft[:, a], soft[:, a], soft1[:, a], ALU.mult))
                        cha.step(dve.tensor_tensor(soft[:, a], dx[:, a], soft[:, a], ALU.subtract))
                        if hf == 0:
                            dve.wait_ge(gate_ready, C)
                            cha.inc(dve.memset(decay[:, 0, :, 0:1], 0.0))
                        dve.scalar_tensor_tensor(out=delta[:, a], in0=delta[:, a], scalar=0.0, in1=soft[:, a],
                                                 op0=ALU.max, op1=ALU.add).then_inc(delta_ready, 1)
                        dve.wait_ge(delta_ready, hf + 1)
                        dve.tensor_tensor(dx[:, a], delta[:, a], xc[:, a], ALU.mult).then_inc(dx_ready, 1)
                        if hf == 1:
                            dve.memset(decay[:, 1, :, 0:1], 0.0).then_inc(decay_zero, 1)

                    def u(n):
                        if n == 0:
                            dve.wait_ge(dx_ready, 2)
                        if n == 1:
                            dve.wait_ge(skip_ready, 1)
                        dve.wait_ge(b_row_ready, n + 1)
                        if n >= 2:
                            dve.wait_ge(y_added, n - 1)
                        dve.tensor_tensor(state[:, n % 2], dx, pa[:, 0:1, :].to_broadcast([P, C, T]), ALU.mult).then_inc(u_done, 1)

                    def scan(n):
                        dve.wait_ge(u_done, n + 1)
                        dve.wait_ge(decay_ready, n + 1)
                        flat = state[:, n % 2].rearrange("p c t -> p (c t)")
                        dve.tensor_tensor_scan(out=flat, data0=decay[:, n % 2].rearrange("p c t -> p (c t)"), data1=flat,
                                               initial=0.0, op0=ALU.mult, op1=ALU.add).then_inc(scan_done, 1)

                    def weigh(n):
                        s = state[:, n % 2]
                        dve.wait_ge(scan_done, n + 1)
                        dve.wait_ge(c_row_ready, n + 1)
                        dve.tensor_tensor(s, s, pa[:, 1:2, :].to_broadcast([P, C, T]), ALU.mult).then_inc(weighed, 1)

                    def out():
                        dve.wait_ge(weighed, NS)
                        dve.wait_ge(y_added, NS - 1)
                        for hf in range(2):
                            a = slice(hf * T // 2, (hf + 1) * T // 2)
                            cha.step(dve.tensor_tensor(y[:, :, a], y[:, :, a], state[:, (NS - 1) % 2, :, a], ALU.add))
                            dve.tensor_tensor(y[:, :, a], y[:, :, a], gate[:, :, a], ALU.mult).then_inc(y_gated, 1)
                        if moe:
                            dve.wait_ge(acc_ready, 1)
                        for hf in range(2):
                            j = slice(hf * J // 2, (hf + 1) * J // 2)
                            dve.wait_ge(op_mm, hf + 1)
                            cha.step(dve.tensor_tensor(h_in[:, j].rearrange("p j d -> p (j d)"), ua[:, j].rearrange("p j d -> p (j d)"),
                                                       pa[:, hf], ALU.add))
                            dve.tensor_tensor(xh_in[:, j], h_in[:, j], xa[:, j], ALU.add).then_inc(handed, 1)

                    def logits():
                        lg = pb[:, 5, 0:J * E].rearrange("p (j e) -> p j e", e=E)
                        dve.wait_ge(logit_mm, 1)
                        chb.step(dve.tensor_reduce(r_m[:], lg, AX.X, ALU.max))
                        dve.tensor_tensor(r_p[:], lg, r_m[:].unsqueeze(2).to_broadcast([P, J, E]),
                                          ALU.subtract).then_inc(r_neg, 1)

                    def rank():
                        dve.wait_ge(r_exp, 1)
                        chb.step(dve.tensor_reduce(r_m[:], r_p[:], AX.X, ALU.add))
                        chb.step(dve.reciprocal(r_m[:], r_m[:]))
                        chb.step(dve.tensor_tensor(r_p[:], r_p[:], r_m[:].unsqueeze(2).to_broadcast([P, J, E]), ALU.mult))
                        this = r_p[:].unsqueeze(3).to_broadcast([P, J, E, E])
                        other = r_p[:].unsqueeze(2).to_broadcast([P, J, E, E])
                        before = v("before", 0, E * E).rearrange("p (e o) -> p e o", o=E).unsqueeze(1).to_broadcast([P, J, E, E])
                        chb.inc(dve.tensor_tensor(r_gt[:], other, this, ALU.is_gt))
                        chb.step(dve.tensor_tensor(r_eq[:], other, this, ALU.is_equal))
                        chb.step(dve.tensor_tensor(r_eq[:], r_eq[:], before, ALU.mult))
                        chb.step(dve.tensor_tensor(r_gt[:], r_gt[:], r_eq[:], ALU.add))
                        chb.step(dve.tensor_reduce(r_w[:], r_gt[:], AX.X, ALU.add))
                        chb.step(dve.scalar_tensor_tensor(out=r_w[:], in0=r_w[:], scalar=1.5, in1=r_p[:], op0=ALU.is_lt, op1=ALU.mult))
                        chb.step(dve.tensor_reduce(r_m[:], r_w[:], AX.X, ALU.add))
                        chb.step(dve.reciprocal(r_m[:], r_m[:]))
                        dve.tensor_tensor(r_w[:], r_w[:], r_m[:].unsqueeze(2).to_broadcast([P, J, E]), ALU.mult).then_inc(rw_ready, 1)

                    def route_turn():
                        dve.wait_ge(rwt_mm, 1)
                        dve.tensor_copy(r_wt[0:E, :], pb[0:E, 4, :]).then_inc(rwt_ready, 1)

                    def seed():
                        dve.wait_ge(seed_mm, 1)
                        dve.tensor_tensor(acc[:].rearrange("p j d -> p (j d)"), xh_in[:].rearrange("p j d -> p (j d)"),
                                          pb[:, 4:6, :].rearrange("p a t -> p (a t)"), ALU.add).then_inc(acc_ready, 1)

                    def mix(e, hf):
                        dve.wait_ge(down_mm, e * J + 2 * hf + 2)
                        if e == 0:
                            dve.wait_ge(acc_ready, 1)
                        else:
                            dve.wait_ge(mixed, 2 * (e - 1) + hf + 1)
                        ye = pb[:, 4 + hf].rearrange("p (j d) -> p j d", d=D)
                        for jj in range(2):
                            j = 2 * hf + jj
                            last = dve.scalar_tensor_tensor(out=acc[:, j], in0=ye[:, jj], scalar=r_w[:, j, e:e + 1],
                                                            in1=acc[:, j], op0=ALU.mult, op1=ALU.add)
                        last.then_inc(mixed, 1)

                    run(order, h_stats=h_stats, x_stats=x_stats, h_norm=h_norm, u_stats=u_stats, u_norm=u_norm,
                        ln_turn=ln_turn, conv=conv, x_proj=x_proj, sp_exp=sp_exp, sp_log=sp_log, sp_inv=sp_inv, u=u,
                        scan=scan, weigh=weigh, out=out, logits=logits, rank=rank, route_turn=route_turn, seed=seed, mix=mix)

                @block.scalar
                def _(act):
                    cha, chb = Chain(act, a_act), Chain(act, b_act)

                    def rstd():
                        if moe:
                            act.wait_ge(b_var, 1)
                            chb.inc(act.activation(b_rstd[:], b_mv[:, :, 1], ACT.Ln, bias=eps[:, 0:1]))
                        if mamba:
                            act.wait_ge(a_var, 1)
                            cha.inc(act.activation(a_rstd[:], a_mv[:, :, 1], ACT.Ln, bias=eps[:, 0:1]))
                            cha.sync()
                            act.activation(a_rstd[:], a_rstd[:], ACT.Exp, scale=-0.5).then_inc(a_rs, 1)
                        if moe:
                            chb.sync()
                            act.activation(b_rstd[:], b_rstd[:], ACT.Exp, scale=-0.5).then_inc(b_rs, 1)

                    def u_stats():
                        act.wait_ge(a_var, 2)
                        layer_rstd(cha, act, a_mv, a_rstd[:], eps[:, 0:1], a_rs)

                    def h_norm():
                        act.wait_ge(vb_turned, 1)
                        for k in range(KD):
                            act.activation(mt[:, k], pb[:, 4 + k], ACT.Identity, scale=v("ln_moe_g", k),
                                           bias=v("ln_moe_b", k)).then_inc(mt_ready, 1)

                    def logits():
                        act.wait_ge(r_neg, 1)
                        act.activation(r_p[:], r_p[:], ACT.Exp).then_inc(r_exp, 1)

                    def in_x(m):
                        act.wait_ge(in_ready, m + 1)
                        act.activation(xpad[:, m, KC - 1:], pa[:, m % 2], ACT.Identity, bias=v("in_proj_b", m)).then_inc(in_taken, 1)

                    def gate_silu(c):
                        act.wait_ge(gate_ready, c + 1)
                        act.activation(gate[:, c], gate_bank(c), ACT.Silu, bias=v("in_proj_b", C + c)).then_inc(gate_taken, 1)

                    def conv_silu(c):
                        act.wait_ge(conv_ready, c + 1)
                        act.activation(xc[:, c], y[:, c], ACT.Silu).then_inc(xc_ready, 1)

                    def x_proj():
                        act.wait_ge(bc_mm, 1)
                        act.activation(dtr[0:DTR, :], pa[3 * N:3 * N + DTR, 0], ACT.Copy).then_inc(dtr_ready, 1)

                    def dt_proj():
                        for c in range(C):
                            act.wait_ge(dt_mm, c + 1)
                            act.activation(delta[:, c], pb[:, c], ACT.Identity, bias=v("dt_proj_b", c))
                            act.activation(soft[:, c], pb[:, c], ACT.Abs, bias=v("dt_proj_b", c)).then_inc(dt_taken, 1)

                    def sp_exp(hf):
                        act.wait_ge(dt_taken, 2 * hf + 2)
                        act.activation(soft[:, half(hf)], soft[:, half(hf)], ACT.Exp, scale=-1.0).then_inc(sp_e, 1)

                    def sp_log(hf):
                        act.wait_ge(sp_one, hf + 1)
                        act.activation(dx[:, half(hf)], soft1[:, half(hf)], ACT.Ln).then_inc(sp_ln, 1)

                    def sp_inv(hf):
                        act.wait_ge(sp_ln, hf + 1)
                        act.wait_ge(sp_fix, hf + 1)
                        act.activation(soft1[:, half(hf)], dx[:, half(hf)], ACT.Exp, scale=-1.0).then_inc(sp_rec, 1)

                    def decay_(n):
                        if n == 1:
                            act.wait_ge(decay_zero, 1)
                        if n >= 2:
                            act.wait_ge(scan_done, n - 1)
                        for c in range(C):
                            if n == 0:
                                act.wait_ge(delta_ready, c // 2 + 1)
                            last = act.activation(decay[:, n % 2, c, 1:], delta[:, c, 1:], ACT.Exp, scale=neg_a[:, c, n:n + 1])
                        last.then_inc(decay_ready, 1)

                    def silu(e):
                        if e >= 2:
                            act.wait_ge(down_mm, (e - 1) * J)
                        for f in range(FE):
                            act.wait_ge(up_mm, e * FE + f + 1)
                            act.activation(h1[:, e % 2, f], pb[:, f], ACT.Silu, bias=v("b1", e * FE + f)).then_inc(h1_ready, 1)

                    run(order, rstd=rstd, u_stats=u_stats, h_norm=h_norm, logits=logits, in_x=in_x,
                        gate_silu=gate_silu, conv_silu=conv_silu, x_proj=x_proj, dt_proj=dt_proj, sp_exp=sp_exp, sp_log=sp_log,
                        sp_inv=sp_inv, decay=decay_, silu=silu)

                @block.gpsimd
                def _(pool):
                    def skip():
                        pool.wait_ge(xc_ready, C)
                        for c in range(C):
                            last = pool.tensor_scalar(y[:, c], xc[:, c], v("D_skip", c), None, ALU.mult)
                        last.then_inc(skip_ready, 1)

                    def weigh(n):
                        if n < NS - 1:
                            if n == 0:
                                pool.wait_ge(skip_ready, 1)
                            else:
                                pool.wait_ge(y_added, n)
                            pool.wait_ge(weighed, n + 1)
                            pool.tensor_tensor(y[:, half(0)], y[:, half(0)], state[:, n % 2, half(0)], ALU.add)
                            pool.wait_ge(scan_done, n + 2)
                            pool.tensor_tensor(y[:, half(1)], y[:, half(1)], state[:, n % 2, half(1)], ALU.add).then_inc(y_added, 1)

                    run(order, skip=skip, weigh=weigh)

                @block.tensor
                def _(pe):
                    def u_norm():
                        pe.wait_ge(va_ready, 1)
                        transpose_tokens(pe, pa, va, ident[:]).then_inc(va_turned, 1)

                    def in_proj(m):
                        if m == 0:
                            pe.wait_ge(ha_ready, 1)
                        if m >= 2:
                            pe.wait_ge(in_taken, m - 1)
                        for k in range(KD):
                            last = pe.matmul(pa[:, m % 2], w_in[:, k, m * P:(m + 1) * P], ha[:, k],
                                             start=k == 0, stop=k == KD - 1)
                        last.then_inc(in_ready, 1)

                    def gate_mm(c):
                        if c == 2:
                            pe.wait_ge(in_taken, C)
                        if c == 3:
                            pe.wait_ge(bc_ready, 1)
                        for k in range(KD):
                            last = pe.matmul(gate_bank(c), w_in[:, k, (C + c) * P:(C + c + 1) * P], ha[:, k],
                                             start=k == 0, stop=k == KD - 1)
                        last.then_inc(gate_ready, 1)

                    def x_proj():
                        pe.wait_ge(in_taken, C)
                        for c in range(C):
                            pe.wait_ge(xc_ready, c + 1)
                            last = pe.matmul(pa[0:3 * N + DTR, 0], w_x[:, c, :], xc[:, c], start=c == 0, stop=c == C - 1)
                        last.then_inc(bc_mm, 1)

                    def dt_proj():
                        pe.wait_ge(dtr_ready, 1)
                        for c in range(C):
                            if c < 2:
                                pe.wait_ge(gate_taken, c + 1)
                            pe.matmul(pb[:, c], w_dt[0:DTR, c * P:(c + 1) * P], dtr[0:DTR, :],
                                      start=True, stop=True).then_inc(dt_mm, 1)

                    def b_row(n):
                        if n == 0:
                            pe.wait_ge(bc_ready, 1)
                            pe.wait_ge(gate_taken, C)
                        else:
                            pe.wait_ge(u_done, n)
                        pe.matmul(pa[:, 0], pick[0:3 * N, n:n + 1].to_broadcast([3 * N, P]), bc3[0:3 * N, :],
                                  start=True, stop=True).then_inc(b_row_ready, 1)

                    def c_row(n):
                        if n >= 1:
                            pe.wait_ge(weighed, n)
                        pe.matmul(pa[:, 1], pick[0:3 * N, NS + n:NS + n + 1].to_broadcast([3 * N, P]), bc3[0:3 * N, :],
                                  start=True, stop=True).then_inc(c_row_ready, 1)

                    def out():
                        pe.wait_ge(weighed, NS)
                        po = pa[:].rearrange("p a (j d) -> p (a j) d", d=D)
                        for j in range(J):
                            pe.wait_ge(y_gated, j // 2 + 1)
                            for c in range(C):
                                last = pe.matmul(po[:, j], y[:, c, j * P:(j + 1) * P], w_op[:, c, :],
                                                 start=c == 0, stop=c == C - 1)
                            if j % 2:
                                last.then_inc(op_mm, 1)

                    def h_norm():
                        pe.wait_ge(vb_ready, 1)
                        transpose_tokens(pe, pb[:, 4:6], vb, ident[:]).then_inc(vb_turned, 1)

                    def logit_mm_():
                        pe.wait_ge(mt_ready, KD)
                        for j in range(J):
                            for k in range(KD):
                                last = pe.matmul(pb[:, 5, j * E:(j + 1) * E], mt[:, k, j * P:(j + 1) * P], w_rt[:, k, :],
                                                 start=k == 0, stop=k == KD - 1)
                        last.then_inc(logit_mm, 1)

                    def route_turn():
                        pe.wait_ge(rw_ready, 1)
                        for j in range(J):
                            last = pe.transpose(pb[0:E, 4, j * P:(j + 1) * P], r_w[:, j, :], ident[:])
                        last.then_inc(rwt_mm, 1)

                    def seed():
                        pe.wait_ge(rwt_ready, 1)
                        po = pb[:, 4:6].rearrange("p a (j d) -> p (a j) d", d=D)
                        for j in range(J):
                            last = pe.matmul(po[:, j], r_wt[0:E, j * P:(j + 1) * P], b_2[0:E, :], start=True, stop=True)
                        last.then_inc(seed_mm, 1)

                    def up(e, f):
                        if e >= 1:
                            pe.wait_ge(h1_ready, (e - 1) * FE + f + 1)
                        elif mamba:
                            pe.wait_ge(dt_taken, f + 1)
                        for k in range(KD):
                            last = pe.matmul(pb[:, f], w_1[:, e, k, f * P:(f + 1) * P], mt[:, k], start=k == 0, stop=k == KD - 1)
                        last.then_inc(up_mm, 1)

                    def down(e, j):
                        pe.wait_ge(h1_ready, (e + 1) * FE)
                        if e == 0:
                            pe.wait_ge(acc_ready, 1)
                        else:
                            pe.wait_ge(mixed, 2 * (e - 1) + j // 2 + 1)
                        for f in range(FE):
                            last = pe.matmul(pb[:, 4 + j // 2, (j % 2) * D:(j % 2 + 1) * D], h1[:, e % 2, f, j * P:(j + 1) * P],
                                             w_2[:, e, f, :], start=f == 0, stop=f == FE - 1)
                        last.then_inc(down_mm, 1)

                    run(order, u_norm=u_norm, in_x=in_proj, gate_mm=gate_mm, x_proj=x_proj, dt_proj=dt_proj, b_row=b_row,
                        c_row=c_row, out=out, h_norm=h_norm, logit_mm=logit_mm_, route_turn=route_turn, seed=seed, up=up, down=down)
            clear_all()

        body(0, True, False)
        if NB > 1:
            with nc.Fori(1, NB) as i:
                body(i, True, True)
        body(NB, False, True)


def attention_ffn_pass(nc, io, x1_dram):
    NB = io["x"].shape[0]
    out_dram = io["out"].rearrange("b (j p) d -> b p j d", p=P)
    with ExitStack() as ctx:
        sem_nums = []

        def sb(name, shape, dt=F32):
            return ctx.enter_context(nc.sbuf_tensor(name, [P] + shape, dt))

        def sem(name):
            s = ctx.enter_context(nc.semaphore(name))
            sem_nums.append(s.num)
            return s

        ident = sb("t_ident", [P])
        head_mask = sb("head_mask", [P // DH])
        w_gate = sb("w_gate", [KD, HID])
        w_up = sb("w_up", [KD, HID])
        w_down = sb("w_down", [FH, D])
        w_qkv = sb("w_qkv", [KD, 3 * D])
        w_out = sb("w_out", [KD, D])
        b_qkv = sb("b_qkv", [3 * D])
        b_out = sb("b_out", [D])
        eps = sb("t_eps", [1])
        norm_bias = sb("norm_bias", [1])
        acos_bias = sb("acos_bias", [1])
        xf = sb("xf", [J, D])
        f_stats = sb("f_stats", [2, J, 6]); f_mv = sb("f_mv", [2, J, 2]); f_rstd = sb("f_rstd", [2, J])
        nf = sb("nf", [KD, T])
        g_sb = sb("g_sb", [FH, T])
        vf = g_sb[:, 0:2].rearrange("p k (j d) -> p (k j) d", d=D)
        yf = sb("yf", [J, D])
        x2_next = sb("x2_next", [J, D])
        x3 = sb("x3", [J, D])
        x2 = sb("x2", [J, D])
        t_stats = sb("t_stats", [J, 6]); t_mv = sb("t_mv", [J, 2]); t_rstd = sb("t_rstd", [J])
        vt = sb("vt", [J, D])
        nt = sb("nt", [KD, T])
        qk = sb("qk", [J, 2 * D])
        val_next = sb("val_next", [J, D])
        val = sb("val", [J, D])
        ss = sb("ss", [J, 2 * H])
        qkt_next = sb("qkt_next", [2 * KD, T])
        qkt = sb("qkt", [2 * KD, T])
        k_one = sb("k_one", [2, T])
        score = sb("score", [2, HG, J, T])
        log_m = sb("log_m", [2, J, T])
        n_c2 = sb("n_c", [2, 2, J])
        v_n = sb("v_n", [HG, J, VW])
        o_t = sb("o_t", [T])
        d_n = sb("d_n", [J, HG]); d_m = sb("d_m", [J, HG])
        o_tok = sb("o_tok", [J, D])
        ot = nt
        pc = ctx.enter_context(nc.psum_tensor("pc", [P, 6, T], F32))
        pf = ctx.enter_context(nc.psum_tensor("pf", [P, 2, T], F32))

        loaded = sem("t_loaded")
        x1_loaded = sem("x1_loaded"); y_stored = sem("y_stored")
        f_dve = sem("f_dve"); f_act = sem("f_act"); f_var = sem("f_var"); f_rs = sem("f_rs")
        vf_ready = sem("vf_ready"); vf_turned = sem("vf_turned"); nf_ready = sem("nf_ready")
        gate_mm = sem("gate_mm"); gate_taken = sem("gate_taken"); up_mm = sem("upf_mm"); hid_ready = sem("hid_ready")
        silu_done = sem("silu_done"); dn_mm = sem("dn_mm"); ffn_done = sem("ffn_done")
        t_var = sem("t_var"); t_rs = sem("t_rs")
        vt_ready = sem("vt_ready"); vt_turned = sem("vt_turned"); nt_ready = sem("nt_ready")
        qkv_mm = sem("qkv_mm"); qkv_taken = sem("qkv_taken"); ss_ready = sem("ss_ready"); squared = sem("squared"); rn_ready = sem("rn_ready")
        qk_ready = sem("qk_ready"); qk_turned = sem("qk_turned"); qkt_taken = sem("qkt_taken")
        o_turned = sem("o_turned"); o_ready = sem("o_ready"); wo_mm = sem("wo_mm"); x3_ready = sem("x3_ready")
        t_dve = sem("t_dve")
        qkt_ready = sem("qkt_ready"); k_ready = sem("k_ready"); s_mm = sem("s_mm"); cos_ready = sem("cos_ready")
        logm_done = sem("logm_done"); logp_done = sem("logp_done")
        diff_pool = sem("diff_pool"); diff_dve = sem("diff_dve")
        tanh_done = sem("tanh_done"); atan_done = sem("atan_done"); log1_done = sem("log1_done"); s_ready = sem("s_ready")
        v_ready = sem("v_ready"); val_ready = sem("val_ready")
        pv_mm = sem("pv_mm"); ot_ready = sem("ot_ready"); ot_turned = sem("ot_turned"); o_norm = sem("o_norm")
        sems = range(min(sem_nums), max(sem_nums) + 1)
        assert len(sems) == len(sem_nums)

        def clear_all():
            nc.sync.sem_clear(sems)
            nc.all_engine_barrier()

        with nc.Block() as block:
            plain = [(ident, "ident"), (head_mask, "head_mask"), (w_qkv, "w_qkv"), (w_out, "w_out"),
                     (b_qkv, "b_qkv"), (b_out, "b_out")]
            coded = [(w_gate, "w_gate", score[:, 0, 0:1]), (w_up, "w_up", score[:, 0, 1:2]), (w_down, "w_down", score[:, 0, 2:3])]

            @block.sync
            def _(sp):
                for dst, name in plain:
                    src = io[name]
                    if name in ("b_qkv", "b_out"):
                        src = src.partition_broadcast(P)
                    sp.dma_start(dst[:], src).then_inc(loaded, 16)
                for dst, name, room in coded:
                    flat = room.rearrange("p a j t -> p (a j t)")[:, 0:FH * D].bitcast(I32)
                    sp.dma_start(flat, io[name].rearrange("p a b -> p (a b)")).then_inc(loaded, 16)

            @block.vector
            def _(dve):
                ch = Chain(dve, t_dve)
                ch.inc(dve.memset(eps[:], LN_EPS))
                ch.inc(dve.memset(norm_bias[:], 0.5 * math.log(Q_SHIFT)))
                ch.inc(dve.memset(acos_bias[:], 1.0 + math.pi / 2))
                ch.step(dve.memset(v_n[:], 0.0))
                ch.inc(dve.memset(v_n[:, :, :, DH + 1:DH + 2], 1.0))
                dve.wait_ge(loaded, 16 * (len(plain) + len(coded)))
                for dst, name, room in coded:
                    flat = room.rearrange("p a j t -> p (a j t)")[:, 0:FH * D].bitcast(I32)
                    ch.step(dve.tensor_scalar(dst[:].rearrange("p a b -> p (a b)"), flat, 1.0 / 127.0, None, ALU.mult))
        clear_all()

        def body(i, attend, before_, after):
            ffns = (["first"] if after else []) + (["last"] if before_ else [])
            n_first, n_last = 0, len(ffns) - 1
            extra = 1 if before_ else 0
            steps = []
            heads = [(g, hh) for g in range(NG) for hh in range(HG)] if attend else []
            made = [0]

            def make(n):
                out = [("t_make", g * HG + hh) for g, hh in heads[made[0]:made[0] + n]]
                made[0] += n
                return out

            def logs(g, mix):
                out = []
                for hh in range(HG):
                    out += mix.get(hh, [])
                    if attend:
                        out += [("t_log", g * HG + hh)]
                    if hh == 1:
                        out += column_sums(g - 1, 1) if attend or g == 0 else []
                return out

            def column_sums(g, half):
                return [("t_sum", g, half)] if (attend if g >= 0 else before_) else []

            def angle(g):
                return [("t_angle", g)] if attend else []

            def weigh(g):
                return [("t_weigh", g)] + column_sums(g, 0) if (attend if g >= 0 else before_) else []

            def log1(g):
                return [("t_log1", g)] if (attend if g >= 0 else before_) else []

            def values(g):
                return [("t_values", g)] if (attend if g >= 0 else before_) else []

            last, first = before_, after
            gates = lambda n: [("ffn_gate", n, m) for m in range(FH)]
            ups = lambda n: [("ffn_up", n, m) for m in range(FH)]
            downs = lambda n, which: [("ffn_down", n, which, j) for j in range(J)]
            only = lambda asked, *names: list(names) if asked else []
            steps += only(attend, ("t_take",)) + make(1) + only(first, ("ffn_stats", n_first, "first")) + make(HG - 1)
            steps += log1(-1) + only(first, ("ffn_rstd_log", n_first)) + weigh(-1)
            steps += only(first, ("ffn_rstd_exp", n_first), ("ffn_norm", n_first, "first"))
            steps += logs(0, {1: only(first, ("ffn_take", n_first)), 2: only(first, *gates(n_first)[:2]),
                              3: only(first, *gates(n_first)[2:4])})
            steps += only(attend, ("t_take_val",)) + values(-1) + only(first, *gates(n_first)[4:])
            steps += angle(0) + make(HG) + only(first, ("ffn_silu", n_first), *ups(n_first))
            steps += log1(0) + only(first, *downs(n_first, "first")[:2]) + weigh(0)
            steps += logs(1, {1: only(first, *downs(n_first, "first")[2:]), 2: only(first, ("t_stats",)), 3: only(last, ("t_out",))})
            steps += only(last, ("t_out_add",)) + only(first, ("t_ln",)) + only(last, ("ffn_stats", n_last, "last")) + values(0)
            steps += angle(1) + beside(only(first, *[("t_qkv", j) for j in range(J)]), make(HG)) + only(first, ("t_square",))
            steps += log1(1) + only(last, ("ffn_rstd_log", n_last)) + weigh(1)
            steps += only(last, ("ffn_rstd_exp", n_last), ("ffn_norm", n_last, "last"))
            steps += logs(2, {1: only(last, ("ffn_take", n_last)), 2: only(last, *gates(n_last)[:2]), 3: only(last, *gates(n_last)[2:3])})
            steps += only(first, ("t_norm",)) + only(last, *gates(n_last)[3:]) + values(1)
            steps += angle(2) + only(first, ("t_turn", 0), ("t_turn", 1)) + only(last, ("ffn_silu", n_last))
            steps += beside(make(HG), only(last, *ups(n_last)[:3]))
            steps += log1(2) + only(last, *ups(n_last)[3:]) + weigh(2)
            steps += logs(3, {2: only(last, *downs(n_last, "last")[:2]), 3: only(last, *downs(n_last, "last")[2:])}) + values(2)
            steps += angle(3) + [("t_shift",)]
            order = steps

            def buf(g):
                return g % 2

            with nc.Block() as block:
                @block.sync
                def _(sp):
                    if after:
                        sp.dma_start(xf[:], x1_dram[bass.ds(i + 1, 1)].rearrange("o p j d -> (o p) j d")).then_inc(x1_loaded, 16)
                    if before_:
                        sp.wait_ge(ffn_done, len(ffns))
                        sp.dma_start(out_dram[bass.ds(i - 1, 1)].rearrange("o p j d -> (o p) j d"), yf[:]).then_inc(y_stored, 16)
                        sp.wait_ge(y_stored, 16)

                @block.vector
                def _(dve):
                    chf, cht = Chain(dve, f_dve), Chain(dve, t_dve)

                    def ffn_stats(n, which):
                        if which == "first":
                            dve.wait_ge(x1_loaded, 16)
                        else:
                            dve.wait_ge(x3_ready, 1)
                        layer_stats(chf, dve, xf if which == "first" else x3, f_stats[:, n], f_mv[:, n], f_var)

                    def ffn_norm(n, which):
                        x = xf if which == "first" else x3
                        dve.wait_ge(f_rs, n + 1)
                        if n:
                            dve.wait_ge(dn_mm, n * J)
                        layer_apply(dve, vf, x, f_mv[:, n], f_rstd[:, n]).then_inc(vf_ready, 1)

                    def ffn_take(n):
                        dve.wait_ge(vf_turned, n + 1)
                        dve.tensor_copy(nf[:], pf[:]).then_inc(nf_ready, 1)

                    def ffn_gate(n, m):
                        dve.wait_ge(gate_mm, n * FH + m + 1)
                        dve.tensor_copy(g_sb[:, m], pf[:, m % 2]).then_inc(gate_taken, 1)

                    def ffn_up(n, m):
                        dve.wait_ge(up_mm, n * FH + m + 1)
                        dve.wait_ge(silu_done, n + 1)
                        dve.tensor_tensor(g_sb[:, m], g_sb[:, m], pf[:, m % 2], ALU.mult).then_inc(hid_ready, 1)

                    def ffn_down(n, which, j):
                        if j % 2 == 0:
                            return
                        dve.wait_ge(dn_mm, n * J + j + 1)
                        x, dst = (xf, xf) if which == "first" else (x3, yf)
                        last = dve.tensor_tensor(dst[:, j - 1:j + 1].rearrange("p j d -> p (j d)"),
                                                 x[:, j - 1:j + 1].rearrange("p j d -> p (j d)"), pf[:, j // 2], ALU.add)
                        if j == J - 1:
                            last.then_inc(ffn_done, 1)

                    def t_take():
                        dve.tensor_copy(qkt[:], qkt_next[:]).then_inc(qkt_ready, 1)

                    def t_take_val():
                        if before_:
                            dve.wait_ge(v_ready, 2)
                        dve.tensor_copy(val[:], val_next[:]).then_inc(val_ready, 1)

                    def t_stats_():
                        dve.wait_ge(ffn_done, 1)
                        layer_stats(chf, dve, xf, t_stats, t_mv, t_var)

                    def t_ln():
                        dve.wait_ge(t_rs, 1)
                        layer_apply(dve, vt, xf, t_mv, t_rstd).then_inc(vt_ready, 1)
                        dve.wait_ge(vt_turned, 1)
                        dve.tensor_copy(nt[:], pf[:]).then_inc(nt_ready, 1)

                    def t_qkv(j):
                        dve.wait_ge(qkv_mm, j + 1)
                        dve.tensor_tensor(qk[:, j], pf[:, 0], b_qkv[:, 0:2 * D], ALU.add).then_inc(qkv_taken, 1)
                        if j == 0 and attend:
                            dve.wait_ge(val_ready, 1)
                        dve.tensor_tensor(val_next[:, j], pf[:, 1, 0:D], b_qkv[:, 2 * D:], ALU.add).then_inc(qkv_taken, 1)

                    def t_square():
                        dve.wait_ge(squared, J)
                        sq = qkt_next[:].rearrange("p k t -> p (k t)")
                        chf.step(dve.tensor_reduce(ss[:], sq.rearrange("p (j h d) -> p j h d", j=J, d=DH), AX.X, ALU.add))
                        dve.tensor_scalar(ss[:], ss[:], 1e-24, None, ALU.max).then_inc(ss_ready, 1)

                    def t_norm():
                        dve.wait_ge(rn_ready, 1)
                        q4 = qk[:].rearrange("p j (h d) -> p (j h) d", d=DH)
                        dve.tensor_tensor(q4, q4, ss[:].rearrange("p j h -> p (j h)").unsqueeze(2).to_broadcast([P, J * 2 * H, DH]),
                                          ALU.mult).then_inc(qk_ready, 1)

                    def t_turn(k):
                        dve.wait_ge(qk_turned, k + 1)
                        dve.tensor_copy(qkt_next[:, 2 * k:2 * k + 2], pf[:]).then_inc(qkt_taken, 1)

                    def mask_keys(h):
                        if h >= 2:
                            dve.wait_ge(s_mm, 2 * (h - 1))
                        m = h % (P // DH)
                        dve.tensor_scalar(k_one[:, h % 2], qkt[:, KD + h // (P // DH)], head_mask[:, m:m + 1], None,
                                          ALU.mult).then_inc(k_ready, 1)

                    def t_make(h):
                        g = h // HG
                        if h == 0:
                            dve.wait_ge(qkt_ready, 1)
                            mask_keys(0)
                        if h + 1 < H:
                            mask_keys(h + 1)
                        if h % HG == 0 and g + extra >= 2:
                            dve.wait_ge(pv_mm, g + extra - 1)
                        for s in range(2):
                            dve.wait_ge(s_mm, 2 * h + s + 1)
                            dve.tensor_scalar(score[:, buf(g), h % HG, 2 * s:2 * s + 2], pc[:, 2 * s:2 * s + 2], -1.0 + 1e-7,
                                              1.0 - 1e-7, ALU.max, ALU.min).then_inc(cos_ready, 1)

                    def t_log(h):
                        if h % 2:
                            s = score[:, buf(h // HG), h % HG]
                            dve.wait_ge(logp_done, h + 1)
                            dve.tensor_tensor(s, s, log_m[:, h % 2], ALU.subtract).then_inc(diff_dve, 1)

                    def t_sum(g, half):
                        k = g + extra
                        h = (g % NG) * HG + 2 * half
                        n_c = n_c2[:, half]
                        if k >= 1:
                            dve.wait_ge(v_ready, 2 * k)
                        dve.wait_ge(s_ready, 2 * k + half + 1)
                        s = score[:, buf(g), 2 * half:2 * half + 2]
                        cht.step(dve.tensor_reduce(n_c, s, AX.X, ALU.add))
                        cht.step(dve.reciprocal(n_c, n_c))
                        if half == 0 and k >= 1:
                            dve.wait_ge(pv_mm, k)
                        if g == 0:
                            dve.wait_ge(val_ready, 1)
                        cht.inc(dve.tensor_tensor(v_n[:, 2 * half:2 * half + 2, :, 0:DH],
                                                  val[:, :, h * DH:(h + 2) * DH].rearrange("p j (h d) -> p h j d", d=DH),
                                                  n_c.unsqueeze(3).to_broadcast([P, 2, J, DH]), ALU.mult))
                        dve.tensor_copy(v_n[:, 2 * half:2 * half + 2, :, DH:DH + 1], n_c.unsqueeze(3)).then_inc(v_ready, 1)

                    def t_values(g):
                        k = g + extra
                        dve.wait_ge(pv_mm, k + 1)
                        if k >= 1:
                            dve.wait_ge(ot_turned, k)
                        dve.tensor_copy(o_t[:], pc[:, 4]).then_inc(ot_ready, 1)
                        dve.wait_ge(ot_turned, k + 1)
                        o = pc[:, 5].rearrange("p (j h w) -> p j h w", h=HG, w=P // HG)
                        cht.step(dve.reciprocal(d_n[:], o[:, :, :, DH + 1]))
                        cht.step(dve.tensor_tensor(d_m[:], d_n[:], o[:, :, :, DH], ALU.mult))
                        cht.step(dve.tensor_scalar(d_m[:], d_m[:], 1e-12, None, ALU.max))
                        cht.step(dve.reciprocal(d_m[:], d_m[:]))
                        cht.step(dve.tensor_tensor(d_m[:], d_m[:], d_n[:], ALU.mult))
                        if g == 0 and before_:
                            dve.wait_ge(o_turned, 1)
                        a = (g % NG) * HG * DH
                        dst = o_tok[:, :, a:a + HG * DH].rearrange("p j (h d) -> p j h d", d=DH)
                        dve.tensor_tensor(dst, o[:, :, :, 0:DH], d_m[:].unsqueeze(3).to_broadcast([P, J, HG, DH]),
                                          ALU.mult).then_inc(o_norm, 1)

                    def t_out():
                        dve.wait_ge(o_turned, 1)
                        chf.inc(dve.tensor_tensor(x2[:], x2[:], b_out[:].unsqueeze(1).to_broadcast([P, J, D]), ALU.add))
                        dve.tensor_copy(nt[:], pf[:]).then_inc(o_ready, 1)

                    def t_out_add():
                        dve.wait_ge(wo_mm, 1)
                        chf.sync()
                        dve.tensor_tensor(x3[:].rearrange("p j d -> p (j d)"), x2[:].rearrange("p j d -> p (j d)"),
                                          pf[:].rearrange("p a t -> p (a t)"), ALU.add).then_inc(x3_ready, 1)

                    def t_shift():
                        if before_:
                            dve.wait_ge(x3_ready, 1)
                        if attend:
                            chf.step(dve.tensor_copy(x2[:], x2_next[:]))
                        if after:
                            dve.tensor_copy(x2_next[:], xf[:])

                    run(order, ffn_stats=ffn_stats, t_stats=t_stats_, t_square=t_square, ffn_norm=ffn_norm, ffn_take=ffn_take, ffn_gate=ffn_gate, ffn_up=ffn_up,
                        ffn_down=ffn_down, t_take=t_take,
                        t_take_val=t_take_val, t_ln=t_ln,
                        t_qkv=t_qkv, t_norm=t_norm, t_turn=t_turn, t_make=t_make, t_log=t_log, t_sum=t_sum,
                        t_values=t_values, t_out=t_out, t_out_add=t_out_add, t_shift=t_shift)

                @block.scalar
                def _(act):
                    chf = Chain(act, f_act)

                    def ffn_rstd_log(n):
                        act.wait_ge(f_var, n + 1)
                        chf.inc(act.activation(f_rstd[:, n], f_mv[:, n, :, 1], ACT.Ln, bias=eps[:, 0:1]))

                    def ffn_rstd_exp(n):
                        chf.sync()
                        act.activation(f_rstd[:, n], f_rstd[:, n], ACT.Exp, scale=-0.5).then_inc(f_rs, 1)

                    def ffn_silu(n):
                        act.wait_ge(gate_taken, (n + 1) * FH)
                        act.activation(g_sb[:], g_sb[:], ACT.Silu).then_inc(silu_done, 1)

                    def t_ln():
                        act.wait_ge(t_var, 1)
                        layer_rstd(chf, act, t_mv, t_rstd[:], eps[:, 0:1], t_rs)

                    def t_norm():
                        act.wait_ge(ss_ready, 1)
                        chf.step(act.activation(ss[:], ss[:], ACT.Ln, scale=Q_SHIFT))
                        act.activation(ss[:], ss[:], ACT.Exp, scale=-0.5, bias=norm_bias[:, 0:1]).then_inc(rn_ready, 1)

                    def t_log(h):
                        s = score[:, buf(h // HG), h % HG]
                        act.wait_ge(cos_ready, 2 * (h + 1))
                        if h >= 2:
                            act.wait_ge(diff_dve if h % 2 else diff_pool, h // 2)
                        act.activation(log_m[:, h % 2], s, ACT.Ln, scale=-1.0, bias=1.0).then_inc(logm_done, 1)
                        act.wait_ge(logm_done, h + 1)
                        act.activation(s, s, ACT.Ln, bias=1.0).then_inc(logp_done, 1)

                    def t_angle(g):
                        pairs = [score[:, buf(g), 0:2], score[:, buf(g), 2:4]]
                        for half, s in enumerate(pairs):
                            act.wait_ge(diff_pool, 2 * g + half + 1)
                            act.wait_ge(diff_dve, 2 * g + half + 1)
                            act.activation(s, s, ACT.Tanh, scale=0.25).then_inc(tanh_done, 1)
                        for half, s in enumerate(pairs):
                            act.wait_ge(tanh_done, 2 * g + half + 1)
                            act.activation(s, s, ACT.Arctan).then_inc(atan_done, 1)

                    def t_log1(g):
                        pairs = [score[:, buf(g), 0:2], score[:, buf(g), 2:4]]
                        for half, s in enumerate(pairs):
                            if g >= 0:
                                act.wait_ge(atan_done, 2 * g + half + 1)
                            act.activation(s, s, ACT.Ln, scale=-2.0, bias=acos_bias[:, 0:1]).then_inc(log1_done, 1)

                    def t_weigh(g):
                        k = g + extra
                        pairs = [score[:, buf(g), 0:2], score[:, buf(g), 2:4]]
                        for half, s in enumerate(pairs):
                            act.wait_ge(log1_done, 2 * k + half + 1)
                            act.activation(s, s, ACT.Exp, scale=-3.2).then_inc(s_ready, 1)

                    run(order, ffn_rstd_log=ffn_rstd_log, ffn_rstd_exp=ffn_rstd_exp, ffn_silu=ffn_silu, t_ln=t_ln, t_norm=t_norm, t_log=t_log, t_angle=t_angle,
                        t_log1=t_log1, t_weigh=t_weigh)

                @block.gpsimd
                def _(pool):
                    def t_log(h):
                        if h % 2 == 0:
                            s = score[:, buf(h // HG), h % HG]
                            pool.wait_ge(logp_done, h + 1)
                            pool.tensor_tensor(s, s, log_m[:, h % 2], ALU.subtract).then_inc(diff_pool, 1)

                    def t_qkv(j):
                        if j == 0 and attend:
                            pool.wait_ge(qkt_ready, 1)
                        pool.wait_ge(qkv_taken, 2 * j + 1)
                        pool.tensor_tensor(qkt_next[:, j], qk[:, j], qk[:, j], ALU.mult).then_inc(squared, 1)

                    run(order, t_log=t_log, t_qkv=t_qkv)

                @block.tensor
                def _(pe):
                    def ffn_take(n):
                        pe.wait_ge(vf_ready, n + 1)
                        if n:
                            pe.wait_ge(qkv_taken, 2 * J)
                        transpose_tokens(pe, pf, vf, ident[:]).then_inc(vf_turned, 1)

                    def ffn_gate(n, m):
                        if m == 0:
                            pe.wait_ge(nf_ready, n + 1)
                        if m >= 2:
                            pe.wait_ge(gate_taken, n * FH + m - 1)
                        for k in range(KD):
                            last = pe.matmul(pf[:, m % 2], w_gate[:, k, m * P:(m + 1) * P], nf[:, k], start=k == 0, stop=k == KD - 1)
                        last.then_inc(gate_mm, 1)

                    def ffn_up(n, m):
                        if m < 2 and n:
                            pe.wait_ge(qkt_taken, 2)
                        elif m < 2:
                            pe.wait_ge(gate_taken, n * FH + FH - 1 + m)
                        else:
                            pe.wait_ge(hid_ready, n * FH + m - 1)
                        for k in range(KD):
                            last = pe.matmul(pf[:, m % 2], w_up[:, k, m * P:(m + 1) * P], nf[:, k], start=k == 0, stop=k == KD - 1)
                        last.then_inc(up_mm, 1)

                    def ffn_down(n, which, j):
                        pe.wait_ge(hid_ready, (n + 1) * FH)
                        for m in range(FH):
                            last = pe.matmul(pf[:, j // 2, (j % 2) * D:(j % 2 + 1) * D], g_sb[:, m, j * P:(j + 1) * P],
                                             w_down[:, m, :], start=m == 0, stop=m == FH - 1)
                        last.then_inc(dn_mm, 1)

                    def t_ln():
                        pe.wait_ge(vt_ready, 1)
                        pe.wait_ge(ffn_done, 1)
                        if before_:
                            pe.wait_ge(x3_ready, 1)
                        transpose_tokens(pe, pf, vt, ident[:]).then_inc(vt_turned, 1)

                    def t_qkv(j):
                        if j == 0:
                            pe.wait_ge(nt_ready, 1)
                        else:
                            pe.wait_ge(qkv_taken, 2 * j)
                        for k in range(KD):
                            pe.matmul(pf[:, 0], nt[:, k, j * P:(j + 1) * P], w_qkv[:, k, 0:2 * D], start=k == 0, stop=k == KD - 1)
                        for k in range(KD):
                            last = pe.matmul(pf[:, 1, 0:D], nt[:, k, j * P:(j + 1) * P], w_qkv[:, k, 2 * D:],
                                             start=k == 0, stop=k == KD - 1)
                        last.then_inc(qkv_mm, 1)

                    def t_turn(k):
                        pe.wait_ge(qk_ready, 1)
                        if k:
                            pe.wait_ge(qkt_taken, k)
                        elif before_:
                            pe.wait_ge(gate_taken, 2 * FH)
                        for c in range(2):
                            a = (2 * k + c) * P
                            for j in range(J):
                                last = pe.transpose(pf[:, c, j * P:(j + 1) * P], qk[:, j, a:a + P], ident[:])
                        last.then_inc(qk_turned, 1)

                    def t_make(h):
                        pe.wait_ge(k_ready, h + 1)
                        for s in range(2):
                            if h:
                                pe.wait_ge(cos_ready, 2 * (h - 1) + s + 1)
                            for c in range(2):
                                t = 2 * s + c
                                last = pe.matmul(pc[:, t], k_one[:, h % 2, t * P:(t + 1) * P], qkt[:, h // (P // DH)],
                                                 start=True, stop=True)
                            last.then_inc(s_mm, 1)

                    def t_values(g):
                        k = g + extra
                        pe.wait_ge(v_ready, 2 * (k + 1))
                        if k >= 1:
                            pe.wait_ge(ot_ready, k)
                        for t in range(J):
                            for hh in range(HG):
                                a = hh * VW
                                last = pe.matmul(pc[a:a + VW, 4], v_n[:, hh, t, :], score[:, buf(g), hh, t], start=t == 0,
                                                 stop=t == J - 1)
                        last.then_inc(pv_mm, 1)
                        pe.wait_ge(ot_ready, k + 1)
                        if k >= 1:
                            pe.wait_ge(o_norm, k)
                        for j in range(J):
                            last = pe.transpose(pc[:, 5, j * P:(j + 1) * P], o_t[:, j * P:(j + 1) * P], ident[:])
                        last.then_inc(ot_turned, 1)

                    def t_out():
                        pe.wait_ge(o_norm, 1)
                        if after:
                            pe.wait_ge(ffn_done, 1)
                        transpose_tokens(pe, pf, o_tok, ident[:]).then_inc(o_turned, 1)
                        pe.wait_ge(o_ready, 1)
                        for j in range(J):
                            for k in range(KD):
                                last = pe.matmul(pf[:, j // 2, (j % 2) * D:(j % 2 + 1) * D], nt[:, k, j * P:(j + 1) * P],
                                                 w_out[:, k, :], start=k == 0, stop=k == KD - 1)
                        last.then_inc(wo_mm, 1)

                    run(order, ffn_take=ffn_take, ffn_gate=ffn_gate, ffn_up=ffn_up, ffn_down=ffn_down, t_ln=t_ln, t_qkv=t_qkv,
                        t_turn=t_turn, t_make=t_make, t_values=t_values, t_out=t_out)
            clear_all()

        body(-1, False, False, True)
        body(0, True, False, NB > 1)
        if NB > 2:
            with nc.Fori(1, NB - 1) as i:
                body(i, True, True, True)
        if NB > 1:
            body(NB - 1, True, True, False)
        body(NB, False, True, False)


def program(nc, io):
    x1_dram = nc.dram_tensor("x1_rows", (io["x"].shape[0], P, J, D), F32, kind="Internal").ap()
    mamba_moe_pass(nc, io, x1_dram)
    attention_ffn_pass(nc, io, x1_dram)


def kernel(**inputs):
    import numpy as np
    import concourse.bacc as bacc
    from concourse import mybir as my
    from concourse.bass_utils import run_bass_kernel_spmd

    a = {k.replace("L0_attn_a_", "").replace("L0_ffn_", "").replace("L0_attn_b_", "t_"): np.asarray(x)
         for k, x in inputs.items()}
    rows = lambda w: np.ascontiguousarray(w.reshape(-1, P, w.shape[-1]).transpose(1, 0, 2))
    cols = lambda w: w.reshape(-1, P).T
    x_proj = a["x_proj_w"].T
    before = np.tril(np.ones((E, E), np.float32), -1).reshape(1, -1).repeat(P, 0)
    head_mask = np.kron(np.eye(P // DH, dtype=np.float32), np.ones((DH, 1), np.float32))
    vectors = {
        "ln_mamba_g": cols(a["ln_mamba_g"]), "ln_mamba_b": cols(a["ln_mamba_b"]), "ln_moe_g": cols(a["ln_moe_g"]),
        "ln_moe_b": cols(a["ln_moe_b"]), "in_proj_b": cols(a["in_proj_b"]),
        "conv_w": rows(a["conv_w"]).reshape(P, -1), "conv_b": cols(a["conv_b"]), "dt_proj_b": cols(a["dt_proj_b"]),
        "A_log": rows(a["A_log"]).reshape(P, -1), "D_skip": cols(a["D_skip"]),
        "b1": cols(a["b1"]), "head_mask": head_mask, "before": before,
    }
    arrays = {
        "x": a["x"],
        "vectors": np.concatenate([vectors[n] for n in VEC], axis=1),
        "ident": np.eye(P, dtype=np.float32),
        "pick": np.tile(np.eye(2 * NS, dtype=np.float32), (3, 1)).astype(my.dt.np(BF16)),
        "head_mask": head_mask,
        "w_in": rows(a["in_proj_w"].T),
        "w_x": rows(np.concatenate([np.tile(x_proj[:, DTR:], (1, 3)), x_proj[:, :DTR]], axis=1)),
        "w_dt": a["dt_proj_w"].T,
        "w_op": rows(a["out_proj_w"].T),
        "w_rt": rows(a["router_w"].T),
        "w_1": a["w1"].transpose(2, 0, 1).reshape(KD, P, E, DFF).transpose(1, 2, 0, 3),
        "w_2": a["w2"].transpose(2, 0, 1).reshape(FE, P, E, D).transpose(1, 2, 0, 3),
        "b2": a["b2"],
        "w_gate": rows(a["w_gate"].T), "w_up": rows(a["w_up"].T), "w_down": rows(a["w_down"].T),
        "w_qkv": rows(a["t_w_qkv"].T), "w_out": rows(a["t_w_out"].T), "b_qkv": a["t_b_qkv"], "b_out": a["t_b_out"],
    }
    arrays = {n: np.ascontiguousarray(x) for n, x in arrays.items()}
    nc = bacc.Bacc("TRN2", target_bir_lowering=False, num_devices=1)
    io = {n: nc.dram_tensor(f"in_{n}", x.shape, my.dt.from_np(x.dtype), kind="ExternalInput").ap() for n, x in arrays.items()}
    io["out"] = nc.dram_tensor("out_0", arrays["x"].shape, F32, kind="ExternalOutput").ap()
    program(nc, io)
    r = run_bass_kernel_spmd(nc, [{f"in_{n}": x for n, x in arrays.items()}], core_ids=[0])
    return r.results[0]["out_0"]
```
